# Optimizing a Trainium2 kernel written in Bass

```python
import numpy as np
import jax
import jax.numpy as jnp

def _softmax(x, axis=-1):
    return jax.nn.softmax(x, axis=axis)

def _gelu(x):
    return jax.nn.gelu(x, approximate=True)

def _silu(x):
    return jax.nn.silu(x)

def _sigmoid(x):
    return jax.nn.sigmoid(x)

def _layernorm(x, axis=-1, eps=1e-05):
    m = jnp.mean(x, axis=axis, keepdims=True)
    v = jnp.var(x, axis=axis, keepdims=True)
    return (x - m) / jnp.sqrt(v + eps)

def _scatter_add(tgt, idx, src, axis=0):
    return tgt.at[idx].add(src)

def _segment_sum(src, seg, n):
    return jax.ops.segment_sum(src, seg, n)
kernel_name = 'mk_gnn_resnorm_d2_gnn_r32_d7d7f8'

def setup_inputs(seed: int=0):
    np.random.seed(seed)
    _w = jnp.asarray

    def _rec_inputs():
        import jax
        import jax.numpy as jnp
        _gk = jax.random.key(seed)
        x = -0.0002117 + 1 * jax.random.normal(jax.random.fold_in(_gk, 1), (3125, 256), jnp.float32)
        src = jax.random.randint(jax.random.fold_in(_gk, 2), (50000,), 0, 3125, jnp.int32)
        dst = jax.random.randint(jax.random.fold_in(_gk, 3), (50000,), 0, 3125, jnp.int32)
        _o = jnp.argsort(dst, stable=True)
        src = src[_o]
        dst = dst[_o]
        return (x, src, dst)
    x, src, dst = _rec_inputs()

    def _L0_gnn_setup():
        import jax, jax.numpy as jnp
        import numpy as np
        N = 3125
        E = 100000
        IN_DIM = 256

        def _edge_vals(rows):
            deg = jnp.zeros((N,), dtype=jnp.float32).at[rows].add(1.0)
            deg = jnp.where(deg == 0, 1.0, deg)
            return 1.0 / deg[rows]

        def _layer(x, rows, cols, vals, W, b):
            neigh = jax.ops.segment_sum(vals[:, None] * x[cols], rows, num_segments=N)
            cat = jnp.concatenate([x, neigh], axis=1)
            return jax.nn.relu(cat @ W.T + b)
        key = jax.random.key(seed)
        k1, k2, k3, k4, k5 = jax.random.split(key, 5)
        features = jax.random.normal(k1, (N, IN_DIM), dtype=jnp.float32)
        rows = jax.random.randint(k2, (E,), 0, N, dtype=jnp.int64)
        cols = jax.random.randint(k3, (E,), 0, N, dtype=jnp.int64)
        s0 = 1.0 / np.sqrt(2 * IN_DIM)
        W0 = jax.random.normal(k4, (256, 2 * IN_DIM), dtype=jnp.float32) * s0
        b0 = jnp.zeros((256,), dtype=jnp.float32)
        s1 = 1.0 / np.sqrt(2 * 256)
        W1 = jax.random.normal(k5, (256, 2 * 256), dtype=jnp.float32) * s1
        b1 = jnp.zeros((256,), dtype=jnp.float32)
        return {'features': features, 'rows': rows, 'cols': cols, 'W0': W0, 'b0': b0, 'W1': W1, 'b1': b1}
    _L0_gnn_all = _L0_gnn_setup()
    _L0_gnn_in = {k: v for k, v in _L0_gnn_all.items() if k in ('W0', 'b0', 'W1', 'b1')}
    del _L0_gnn_all

    def _L1_gnn_setup():
        import jax, jax.numpy as jnp
        import numpy as np
        N = 3125
        E = 50000
        IN_FEATS = 256
        OUT_FEATS = 256
        MAXK = 32

        def _maxk(x, k):
            _, idx = jax.lax.top_k(x, k)
            rows = jnp.arange(x.shape[0])[:, None]
            mask = jnp.zeros_like(x).at[rows, idx].set(1.0)
            return x * mask
        key = jax.random.key(seed)
        k1, k2, k3, k4, k5 = jax.random.split(key, 5)
        feat = jax.random.normal(k1, (N, IN_FEATS), dtype=jnp.float32)
        W_self = jax.random.normal(k2, (IN_FEATS, OUT_FEATS), dtype=jnp.float32) * (1.0 / np.sqrt(IN_FEATS))
        W_neigh = jax.random.normal(k3, (IN_FEATS, OUT_FEATS), dtype=jnp.float32) * (1.0 / np.sqrt(IN_FEATS))
        src = jax.random.randint(k4, (E,), 0, N, dtype=jnp.int64)
        dst = jax.random.randint(k5, (E,), 0, N, dtype=jnp.int64)
        return {'feat': feat, 'W_self': W_self, 'W_neigh': W_neigh, 'src': src, 'dst': dst}
    _L1_gnn_all = _L1_gnn_setup()
    _L1_gnn_in = {k: v for k, v in _L1_gnn_all.items() if k in ('W_self', 'W_neigh')}
    del _L1_gnn_all
    return {'x': x, 'src': src, 'dst': dst, 'L0_gnn_W0': _L0_gnn_in['W0'], 'L0_gnn_b0': _L0_gnn_in['b0'], 'L0_gnn_W1': _L0_gnn_in['W1'], 'L0_gnn_b1': _L0_gnn_in['b1'], 'L1_gnn_W_self': _L1_gnn_in['W_self'], 'L1_gnn_W_neigh': _L1_gnn_in['W_neigh']}

def reference(x, src, dst, L0_gnn_W0, L0_gnn_b0, L0_gnn_W1, L0_gnn_b1, L1_gnn_W_self, L1_gnn_W_neigh):
    import jax
    import jax.numpy as jnp

    def _L0_gnn_ref(features, rows, cols, W0, b0, W1, b1):
        import jax, jax.numpy as jnp
        import numpy as np
        N = 3125
        E = 100000
        IN_DIM = 256

        def _edge_vals(rows):
            deg = jnp.zeros((N,), dtype=jnp.float32).at[rows].add(1.0)
            deg = jnp.where(deg == 0, 1.0, deg)
            return 1.0 / deg[rows]

        def _layer(x, rows, cols, vals, W, b):
            neigh = jax.ops.segment_sum(vals[:, None] * x[cols], rows, num_segments=N)
            cat = jnp.concatenate([x, neigh], axis=1)
            return jax.nn.relu(cat @ W.T + b)
        vals = _edge_vals(rows)
        x = _layer(features, rows, cols, vals, W0, b0)
        x = _layer(x, rows, cols, vals, W1, b1)
        return x

    def _L1_gnn_ref(feat, W_self, W_neigh, src, dst):
        import jax, jax.numpy as jnp
        import numpy as np
        N = 3125
        E = 50000
        IN_FEATS = 256
        OUT_FEATS = 256
        MAXK = 32

        def _maxk(x, k):
            _, idx = jax.lax.top_k(x, k)
            rows = jnp.arange(x.shape[0])[:, None]
            mask = jnp.zeros_like(x).at[rows, idx].set(1.0)
            return x * mask
        n = feat.shape[0]
        h_self = feat @ W_self
        h_neigh = feat @ W_neigh
        h_sparse = _maxk(h_neigh, MAXK)
        msg = h_sparse[src]
        summed = jax.ops.segment_sum(msg, dst, num_segments=n)
        deg = jax.ops.segment_sum(jnp.ones((src.shape[0],), dtype=feat.dtype), dst, num_segments=n)
        neigh = summed / jnp.maximum(deg, 1.0)[:, None]
        return h_self + neigh
    x = _layernorm(x + _L0_gnn_ref(x, src, dst, L0_gnn_W0, L0_gnn_b0, L0_gnn_W1, L0_gnn_b1), axis=-1)
    x = _layernorm(x + _L1_gnn_ref(x, L1_gnn_W_self, L1_gnn_W_neigh, src, dst), axis=-1)
    return x

_drawn_inputs = setup_inputs


def setup_inputs(seed=0):
    import zlib

    import numpy as np

    out = dict(_drawn_inputs(seed))
    spreads = {'L0_gnn_b0': (0.0, 0.1), 'L0_gnn_b1': (0.0, 0.1)}
    factors = {}
    for name, (base, spread) in spreads.items():
        noise = np.random.default_rng([zlib.crc32(name.encode()), seed]).standard_normal(out[name].shape)
        drawn = base * np.exp(spread * noise) if base else spread * noise
        out[name] = jnp.asarray(drawn.astype(out[name].dtype))
    for name, factor in factors.items():
        out[name] = (out[name] * factor).astype(out[name].dtype)
    return out
```

```python
from contextlib import ExitStack

import concourse.bass as bass
from concourse import mybir

N, E, F = 3125, 50000, 256
P = 125
NT = N // P
CH = E // P
G = 4
W = 25
WT = P // W
NW = N // W
KEY = NT * W
B0W = 13
EQ, EG = 4, CH // 4
BT = 5
NB = NT // BT
H0, H1 = 313, 312
MAXK = 32
EPS = 1e-5
NEG = -3.0e38
ROUND = 12582912.0
TG = [7, 6, 6, 6]
TG0 = [0, 7, 13, 19]

F32, F16, I32 = mybir.dt.float32, mybir.dt.float16, mybir.dt.int32
ALU = mybir.AluOpType
ACT = mybir.ActivationFunctionType
X = mybir.AxisListType.X
ds = bass.ds


def gnn(nc, x, src, dst, w0, b0, w1, b1, wself, wneigh, out):
    ctx = ExitStack()
    with ctx:
        sem_names = set()

        def sem(name):
            assert name not in sem_names
            sem_names.add(name)
            return ctx.enter_context(nc.semaphore(name))

        class Arena:

            def __init__(self, at, end):
                self.at, self.end = at, end

            def __call__(self, name, shape, dt):
                size = 2 if dt == F16 else 4
                for n in shape[1:]:
                    size *= n
                t = nc.alloc_sbuf_tensor_at(name, shape, dt, offset=self.at)
                self.at += (size + 31) // 32 * 32
                assert self.at <= self.end, (name, self.at, self.end)
                return t

        keep = Arena((nc.sbuf_base + 31) // 32 * 32, nc.sbuf_usable_end)
        ct_at = keep.at
        ct = keep("ct", [P, NT, N], F16)
        xs = keep("xs", [P, NT, 2 * F], F16)
        identf = keep("identf", [128, 128], F32)
        ident16 = keep("ident16", [P, P], F16)
        ones16 = keep("ones16", [P, 1], F16)
        onesf = keep("onesf", [1, 128], F32)
        scales = keep("scales", [128, 6], F32)
        rdeg_src = keep("rdeg_src", [P, NT], F32)
        rdeg_dst = keep("rdeg_dst", [P, NT], F32)
        deg_part = keep("deg_part", [P, NT, 4], F32)
        epsb = keep("epsb", [P, 1], F32)
        xs32 = xs[:, :, :].bitcast(F32)
        shared_at = keep.at

        bld = Arena(shared_at, nc.sbuf_usable_end)
        slab = [bld(f"slab{i}", [P, NT, P], F16) for i in range(2)]
        key_hot = [bld(f"key_hot{k}", [P, KEY], F16) for k in range(G)]
        src_hot = [bld(f"src_hot{k}", [P, P], F16) for k in range(G)]
        iota16 = bld("iota16", [P, KEY], F16)
        key_t = bld("key_t", [P, CH + G], F32)
        srcp_t = bld("srcp_t", [P, CH + G], F32)
        woff = bld("woff", [P, NW], F32)
        table = bld("table", [1, 2, 128], I32)
        xscaled = bld("xscaled", [P, F], F32)
        xparts = bld("xparts", [P, 2 * F], F16)

        pre = Arena(ct_at, ct_at + NT * N * 2)
        edges_i = pre("edges_i", [EG, 2, EQ, P], I32)
        edges_f = pre("edges_f", [EG, 2, EQ, P], F32)
        hi_f = pre("hi_f", [EG, 2, EQ, P], F32)
        srcp = pre("srcp", [EG, EQ, P], F32)
        key = pre("key", [EG, EQ, P], F32)
        wlim = pre("wlim", [EG, 2, EQ], F32)
        onesq = pre("onesq", [EG, P], F32)
        wdiag = pre("wdiag", [EG, 2, EQ, EG], F32)
        inc_f = pre("inc_f", [P, CH], F32)
        rev_f = pre("rev_f", [P, CH], F32)
        wcol = pre("wcol", [P, 1], F32)
        cover = pre("cover", [P, CH], F32)
        cover2 = pre("cover2", [P, CH], F32)
        cover3 = pre("cover3", [P, CH], F32)
        cover4 = pre("cover4", [P, CH], F32)
        lim = pre("lim", [P, 8], F32)
        rows = pre("rows", [1, 4, 128], F32)
        w_nat = pre("w_nat", [128, 2, 2, 2 * F], F32)
        w_t = pre("w_t", [128, 2, 4, F], F32)
        wn_nat = pre("wn_nat", [128, 2, F], F32)
        bcol = pre("bcol", [128, 2], F32)
        junk = pre("junk", [128, 2 * F], F32)
        stat = pre("stat", [128, 8], F32)
        stat_r = pre("stat_r", [8, 2], F32)
        sv = pre("sv", [1, 2, 8], F32)
        sw = pre("sw", [1, 16], F32)
        svi = pre("svi", [1, 8], I32)
        sbits = pre("sbits", [1, 8], I32)
        srow = pre("srow", [1, 6], F32)

        lay = Arena(shared_at, nc.sbuf_usable_end)
        wt_sb = lay("wt_sb", [128, 4, F], F32)
        wsn_sb = lay("wsn_sb", [128, 2, 2 * F], F32)
        bias_sb = lay("bias_sb", [P, F], F32)
        nt_sb = [lay(f"nt_sb{i}", [128, 2, BT * P], F32) for i in range(2)]
        selfb = lay("selfb", [P, BT, F], F32)
        xy = [lay(f"xy{i}", [P, BT, F], F32) for i in range(2)]
        tr_sb = [lay(f"tr_sb{i}", [128, 2, P], F32) for i in range(2)]
        t2 = [lay(f"t2_{i}", [P, F], F32) for i in range(2)]
        hb = [lay(f"hb{i}", [P, F], F32) for i in range(2)]
        part = [lay(f"part{i}", [P, 2 * F], F16) for i in range(2)]
        work = lay("work", [P, F], F32)
        m8 = lay("m8", [P, 8], F32)
        st6 = [lay(f"st6_{i}", [P, 6], F32) for i in range(2)]
        mv = [lay(f"mv{i}", [P, 2], F32) for i in range(2)]
        sd = [lay(f"sd{i}", [P, 2], F32) for i in range(2)]
        t1 = work
        sparse = t2

        c_dram = nc.dram_tensor("c_dram", (NT, P, N), F16).ap()
        wt_dram = nc.dram_tensor("wt_dram", (2, 128, 4 * F), F32).ap()
        h1_dram = nc.dram_tensor("h1_dram", (NT, P, F), F32).ap()
        parts_dram = [nc.dram_tensor(f"parts_dram{i}", (NT, P, 2 * F), F16).ap() for i in range(2)]
        z_dram = nc.dram_tensor("z_dram", (NT, P, F), F32).ap()
        x_t = x.rearrange("(t p) f -> t p f", p=P)
        out_t = out.rearrange("(t p) f -> t p f", p=P)

        bank = [ctx.enter_context(nc.psum_tensor(f"bank{i}", [128, 512], F32)) for i in range(8)]
        tr16 = [bank[4 + i][:, :].bitcast(F16).rearrange("p (k c) -> p k c", c=128) for i in range(2)]
        agg = [[bank[0], bank[1]], [bank[2], bank[3]]]
        tp = bank[4][:, 0:2 * P].rearrange("p (c n) -> p c n", c=2)
        dense = [bank[5], bank[6]]
        degb = bank[7]

        const_ready = sem("const_ready")
        src_loaded, dst_loaded = sem("src_loaded"), sem("dst_loaded")
        x_loaded, w_loaded, wn_loaded, b_loaded = sem("x_loaded"), sem("w_loaded"), sem("wn_loaded"), sem("b_loaded")
        edge_keys, win_lims, lims_rows = sem("edge_keys"), sem("win_lims"), sem("lims_rows")
        keys_t, lims_b, rows_t = sem("keys_t"), sem("lims_b"), sem("rows_t")
        diag_ready = sem("diag_ready")
        wt_psum, wt_copied, wt_stored = sem("wt_psum"), sem("wt_copied"), sem("wt_stored")
        stat_ready, stat_psum, stat_red, stat_row = sem("stat_ready"), sem("stat_psum"), sem("stat_red"), sem("stat_row")
        scale_row, scale_psum, scale_ready = sem("scale_row"), sem("scale_psum"), sem("scale_ready")
        table_ready, act_sums = sem("table_ready"), sem("act_sums")
        hot_ready, jobs_done = sem("hot_ready"), sem("jobs_done")
        win_free, tr_done, tr_free = sem("win_free"), sem("tr_done"), sem("tr_free")
        slab_stored = [sem("slab_stored0"), sem("slab_stored1")]
        x_split, x_parts, stats3 = sem("x_split"), sem("x_parts"), sem("stats3")
        deg_done, rdeg_ready = sem("deg_done"), sem("rdeg_ready")
        agg_done, agg_copied = sem("agg_done"), sem("agg_copied")
        tp_done, tp_copied = sem("tp_done"), sem("tp_copied")
        mm_done, bank_read = sem("mm_done"), sem("bank_read")
        relu_ready, lo_ready = sem("relu_ready"), sem("lo_ready")
        part_stored = [sem("part_stored0"), sem("part_stored1")]
        self_loaded, xy_loaded = sem("self_loaded"), [sem("xy_loaded0"), sem("xy_loaded1")]
        wts_loaded, wsn_loaded = [sem("wts_loaded0"), sem("wts_loaded1")], sem("wsn_loaded")
        var_ready, sd_ready, y_ready = sem("var_ready"), sem("sd_ready"), sem("y_ready")
        hn_copied, sparse_ready, sphi_ready, sp_lo = sem("hn_copied"), sem("sparse_ready"), sem("sphi_ready"), sem("sp_lo")
        sp_stored, z_stored = [sem("sp_stored0"), sem("sp_stored1")], sem("z_stored")
        z_ready = sem("z_ready")
        xs_loaded = [[sem(f"xs_loaded{l}_{c}") for c in range(NB)] for l in (2, 3)]
        c_loaded = [sem("c_loaded0"), sem("c_loaded1")]
        n3_done, n3_read = sem("n3_done"), sem("n3_read")
        z_loaded, o_stored = [sem(f"z_loaded{i}") for i in range(BT)], [sem(f"o_stored{i}") for i in range(BT)]
        o_ready, var3, sd3 = sem("o_ready"), sem("var3"), sem("sd3")
        dve_step, act_step, pool_step = sem("dve_step"), sem("act_step"), sem("pool_step")

        phases2, q = [("B", 0)], 0
        for k in range(2, NB):
            phases2 += [("C", k - 2), ("B", k - 1)]
        phases2 += [("C", NB - 2), ("B", NB - 1), ("C", NB - 1)]
        phase_of = {p: NB + i for i, p in enumerate(phases2)}

        def c0(i):
            return i // 2

        def uses(i):
            return 3 if i % 2 == 0 else 2

        def free_at(Q, i):
            return Q if i == 0 else Q - 1

        block = ctx.enter_context(nc.Block())

        @block.sync
        def _(sp):
            sp.dma_start(edges_i[:, 0], src.rearrange("(g q p) -> q g p", g=EQ, p=P)).then_inc(src_loaded, 16)
            sp.dma_start(edges_i[:, 1], dst.rearrange("(g q p) -> q g p", g=EQ, p=P)).then_inc(dst_loaded, 16)
            sp.dma_start(w_nat[:, 0], w0.rearrange("(h p) k -> p h k", p=128)).then_inc(w_loaded, 16)
            sp.dma_start(w_nat[:, 1], w1.rearrange("(h p) k -> p h k", p=128)).then_inc(w_loaded, 16)
            sp.dma_start(wn_nat[:, :, :], wneigh.rearrange("(h p) k -> p h k", p=128)).then_inc(wn_loaded, 16)
            sp.dma_start(bcol[:, :], b0.rearrange("(h p) -> p h", p=128),
                         allow_slow_non_contiguous=True).then_inc(b_loaded, 16)
            sp.dma_start(xs32[:, :, :], x.rearrange("(t p) f -> p t f", p=P)).then_inc(x_loaded, 16)
            sp.wait_ge(wt_copied, 4)
            sp.dma_start(wt_dram.rearrange("l p f -> p l f"), w_t[:, :, :, :].rearrange("p l c f -> p l (c f)")
                         ).then_inc(wt_stored, 16)

            def store_slab(t, par):
                sp.wait_ge(win_free, WT * t + WT + 2)
                sp.dma_start(c_dram[ds(t, 1), :, :].rearrange("o p n -> (o p) n"),
                             slab[par][:, :, :].rearrange("p b d -> p (b d)")).then_inc(slab_stored[par], 16)

            with sp.Fori(0, NT // 2) as m:
                t = m * 2
                store_slab(t, 0)
                store_slab(t + 1, 1)
            store_slab(NT - 1, 0)

            sp.wait_ge(tr_done, 4 * NT)
            sp.wait_ge(x_split, NT)
            sp.wait_ge(slab_stored[0], 16 * 13)
            sp.wait_ge(slab_stored[1], 16 * 12)
            sp.dma_start(wt_sb[:, :, :].rearrange("p c f -> p (c f)"), wt_dram[0]).then_inc(wts_loaded[0], 16)
            sp.dma_start(bias_sb[:, :], b0.rearrange("(o f) -> o f", o=1).broadcast_to([P, F])).then_inc(wts_loaded[0], 16)
            sp.dma_start(wsn_sb[:, :, 0:F], wself.rearrange("(c p) f -> p c f", p=128)).then_inc(wsn_loaded, 16)
            sp.dma_start(wsn_sb[:, :, F:2 * F], wneigh.rearrange("(c p) f -> p c f", p=128)).then_inc(wsn_loaded, 16)

            def load_self(dram, n):
                sp.dma_start(selfb[:, :, :], dram[ds(n * BT, BT), :, :].rearrange("t p f -> p t f")
                             ).then_inc(self_loaded, 16)

            load_self(x_t, 0)

            def store_h(n, phase):
                for i in range(BT):
                    b = i % 2
                    sp.wait_ge(lo_ready, 5 * phase + i + 1)
                    T = n * BT + i
                    sp.dma_start(parts_dram[0][ds(T, 1), :, :].rearrange("o p n -> (o p) n"), part[b][:, :]
                                 ).then_inc(part_stored[b], 16)
                    sp.dma_start(h1_dram[ds(T, 1), :, :].rearrange("o p n -> (o p) n"), hb[b][:, :]
                                 ).then_inc(part_stored[b], 16)

            with sp.Fori(0, NB - 1) as n:
                store_h(n, n)
                sp.wait_ge(tp_done, BT * n + BT)
                load_self(x_t, n + 1)
            sp.wait_ge(agg_done, NB)
            sp.wait_ge(part_stored[0], 32 * 3 * (NB - 1))
            sp.wait_ge(part_stored[1], 32 * 2 * (NB - 1))

            def load_parts(l, c):
                sp.dma_start(xs[:, c * BT:(c + 1) * BT, :],
                             parts_dram[l][c * BT:(c + 1) * BT, :, :].rearrange("t p f -> p t f")
                             ).then_inc(xs_loaded[l][c], 16)

            for c in range(NB - 1):
                load_parts(0, c)
            sp.dma_start(xy[0][:, :, :], x_t[0:BT, :, :].rearrange("t p f -> p t f")).then_inc(xy_loaded[0], 16)
            sp.dma_start(xy[1][:, :, :], x_t[BT:2 * BT, :, :].rearrange("t p f -> p t f")).then_inc(xy_loaded[1], 16)
            sp.wait_ge(tp_done, BT * NB)
            load_self(h1_dram, 0)
            store_h(NB - 1, NB - 1)
            sp.wait_ge(part_stored[0], 32 * 3 * NB)
            sp.wait_ge(part_stored[1], 32 * 2 * NB)
            load_parts(0, NB - 1)
            sp.wait_ge(mm_done, BT * NB)
            sp.wait_ge(bank_read, BT * NB)
            sp.dma_start(wt_sb[:, :, :].rearrange("p c f -> p (c f)"), wt_dram[1]).then_inc(wts_loaded[1], 16)
            sp.dma_start(bias_sb[:, :], b1.rearrange("(o f) -> o f", o=1).broadcast_to([P, F])).then_inc(wts_loaded[1], 16)

            for kind, n in phases2:
                Q0 = BT * phase_of[kind, n]
                if kind == "B":
                    sp.wait_ge(tp_done, Q0 + BT)
                    if n + 1 < NB:
                        load_self(h1_dram, n + 1)
                    continue
                for i in range(BT):
                    b, T = i % 2, n * BT + i
                    sp.wait_ge(z_ready, T + 1)
                    sp.dma_start(z_dram[T], xy[n % 2][:, i, :]).then_inc(z_stored, 16)
                    sp.wait_ge(sp_lo, T + 1)
                    sp.dma_start(parts_dram[1][T], part[b][:, :]).then_inc(sp_stored[b], 16)
                if n + 2 < NB:
                    sp.wait_ge(z_stored, 16 * BT * (n + 1))
                    sp.wait_ge(tp_done, Q0 + BT)
                    sp.dma_start(xy[n % 2][:, :, :], x_t[(n + 2) * BT:(n + 3) * BT, :, :].rearrange("t p f -> p t f")
                                 ).then_inc(xy_loaded[n % 2], 16)
                if n >= NB - 2:
                    sp.wait_ge(agg_done, 2 * NB)
                    sp.wait_ge(sp_stored[0], 16 * 3 * (n + 1))
                    sp.wait_ge(sp_stored[1], 16 * 2 * (n + 1))
                    for c in (range(NB - 1) if n == NB - 2 else [NB - 1]):
                        load_parts(1, c)

            sp.wait_ge(z_stored, 16 * NT)

            def load_z(g, i):
                sp.dma_start(xy[0][:, i, :], z_dram[ds(g * BT + i, 1), :, :].rearrange("o p n -> (o p) n")
                             ).then_inc(z_loaded[i], 16)

            def store_out(g, i):
                sp.wait_ge(o_ready, g * BT + i + 1)
                sp.dma_start(out_t[ds(g * BT + i, 1), :, :].rearrange("o p n -> (o p) n"), xy[1][:, i, :]
                             ).then_inc(o_stored[i], 16)

            for i in range(BT):
                load_z(0, i)
            with sp.Fori(0, NB - 1) as g:
                for i in range(BT):
                    store_out(g, i)
                    load_z(g + 1, i)
            for i in range(BT):
                store_out(NB - 1, i)
            for i in range(BT):
                sp.wait_ge(o_stored[i], 16 * NB)
            sp.wait_ge(wt_stored, 16)

        @block.gpsimd
        def _(pool):
            nc.gpsimd.iota(iota16[:, :], [[1, KEY]], base=0, channel_multiplier=0,
                           allow_small_or_imprecise_dtypes=True).then_inc(const_ready, 1)
            nc.gpsimd.iota(woff[:, :], [[KEY, NW]], base=0, channel_multiplier=0,
                           allow_small_or_imprecise_dtypes=True).then_inc(const_ready, 1)
            nc.gpsimd.iota(inc_f[:, :], [[1, CH]], base=1, channel_multiplier=0,
                           allow_small_or_imprecise_dtypes=True).then_inc(const_ready, 1)
            nc.gpsimd.iota(rev_f[:, :], [[-1, CH]], base=CH, channel_multiplier=0,
                           allow_small_or_imprecise_dtypes=True).then_inc(const_ready, 1)
            nc.gpsimd.iota(wcol[:, :], [[0, 1]], base=0, channel_multiplier=1,
                           allow_small_or_imprecise_dtypes=True).then_inc(const_ready, 1)
            nc.gpsimd.memset(identf[:, :], 0.0).then_inc(pool_step, 1)
            nc.gpsimd.memset(ident16[:, :], 0.0).then_inc(pool_step, 1)
            nc.gpsimd.memset(ones16[:, :], 1.0).then_inc(const_ready, 1)
            nc.gpsimd.memset(onesf[:, :], 1.0).then_inc(const_ready, 1)
            nc.gpsimd.memset(onesq[:, :], 1.0).then_inc(const_ready, 1)
            nc.gpsimd.memset(epsb[:, :], EPS).then_inc(const_ready, 1)
            nc.gpsimd.memset(key_t[:, CH:CH + G], -1.0).then_inc(const_ready, 1)
            nc.gpsimd.memset(srcp_t[:, CH:CH + G], 0.0).then_inc(const_ready, 1)
            nc.gpsimd.memset(stat[:, :], 0.0).then_inc(const_ready, 1)
            pool.wait_ge(pool_step, 2)
            for m, n in ((identf, 128), (ident16, P)):
                nc.gpsimd.affine_select(out=m[:, :], in_=m[:, :], compare_op=ALU.not_equal, fill=1.0, base=0,
                                        pattern=[[-1, n]], channel_multiplier=1).then_inc(const_ready, 1)
            pool.wait_ge(scale_ready, 1)
            with pool.Fori(0, NT) as t:
                step = 2 + 3 * t
                nc.gpsimd.tensor_tensor(xscaled[:, :], xs32[:, ds(t, 1), :].rearrange("p o f -> p (o f)"),
                                        scales[0:P, 0:1].broadcast_to([P, F]), ALU.mult).then_inc(pool_step, 1)
                nc.gpsimd.tensor_tensor(xparts[:, 0:F], xs32[:, ds(t, 1), :].rearrange("p o f -> p (o f)"),
                                        scales[0:P, 0:1].broadcast_to([P, F]), ALU.mult).then_inc(pool_step, 1)
                pool.wait_ge(pool_step, step + 2)
                nc.gpsimd.tensor_tensor(xparts[:, F:2 * F], xscaled[:, :], xparts[:, 0:F], ALU.subtract
                                        ).then_inc(pool_step, 1)
                pool.wait_ge(pool_step, step + 3)
                pool.sem_inc(x_parts, 1)
                nc.gpsimd.tensor_copy(xs[:, ds(t, 1), :].rearrange("p o f -> p (o f)"), xparts[:, :]
                                      ).then_inc(x_split, 1)
                pool.wait_ge(x_split, t + 1)
                pool.sem_inc(x_parts, 1)

        NCONST = 14

        @block.vector
        def _(dve):
            done = [0]

            def step(ins):
                done[0] += 1
                ins.then_inc(dve_step, 1)
                dve.wait_ge(dve_step, done[0])

            v = nc.vector
            for j, (s, size) in enumerate(((src_loaded, P), (dst_loaded, W))):
                dve.wait_ge(s, 16)
                step(v.tensor_copy(edges_f[:, j], edges_i[:, j]))
                step(v.tensor_scalar(hi_f[:, j], edges_f[:, j], 1.0 / size, 0.5 / size - 0.5, ALU.mult, ALU.add))
                step(v.tensor_scalar(hi_f[:, j], hi_f[:, j], ROUND, -ROUND, ALU.add, ALU.add))
            v.scalar_tensor_tensor(srcp[:, :, :], hi_f[:, 0], -float(P), edges_f[:, 0], ALU.mult, ALU.add
                                   ).then_inc(edge_keys, 1)
            step(v.scalar_tensor_tensor(key[:, :, :], hi_f[:, 1], float(KEY - W), edges_f[:, 1], ALU.mult, ALU.add))
            v.scalar_tensor_tensor(key[:, :, :], hi_f[:, 0], float(W), key[:, :, :], ALU.mult, ALU.add
                                   ).then_inc(edge_keys, 1)
            step(v.tensor_reduce(wlim[:, 0, :], hi_f[:, 1], X, ALU.min))
            step(v.tensor_reduce(wlim[:, 1, :], hi_f[:, 1], X, ALU.max))
            dve.wait_ge(const_ready, NCONST)
            for j in range(2):
                for g in range(EQ):
                    last = v.tensor_scalar(wdiag[:, j, g, :], identf[0:EG, 0:EG], wlim[:, j, g:g + 1], None, ALU.mult)
            last.then_inc(diag_ready, 1)
            dve.wait_ge(keys_t, 1)
            v.tensor_copy(srcp_t[:, 0:CH], bank[0][0:P, 0:CH]).then_inc(dve_step, 1)
            done[0] += 1
            step(v.tensor_copy(key_t[:, 0:CH], bank[1][0:P, 0:CH]))
            dve.wait_ge(lims_b, 1)
            step(v.tensor_scalar(cover[:, :], bank[2][0:P, 0:CH], wcol[:, :], None, ALU.is_le))
            step(v.scalar_tensor_tensor(cover2[:, :], bank[3][0:P, 0:CH], wcol[:, :], cover[:, :], ALU.is_ge, ALU.mult))
            step(v.tensor_tensor(cover3[:, :], cover2[:, :], rev_f[:, :], ALU.mult))
            step(v.tensor_tensor(cover4[:, :], cover2[:, :], inc_f[:, :], ALU.mult))
            step(v.tensor_reduce(lim[:, 0:1], cover3[:, :], X, ALU.max))
            step(v.tensor_reduce(lim[:, 1:2], cover4[:, :], X, ALU.max))
            step(v.tensor_scalar(lim[:, 2:3], lim[:, 0:1], -1.0, float(CH), ALU.mult, ALU.add))
            step(v.tensor_tensor(lim[:, 3:4], lim[:, 1:2], lim[:, 2:3], ALU.subtract))
            step(v.tensor_scalar(lim[:, 4:5], lim[:, 3:4], 1.0 / G, (G - 1.0) / G + 0.5 / G - 0.5, ALU.mult, ALU.add))
            step(v.tensor_scalar(lim[:, 5:6], lim[:, 4:5], ROUND, -ROUND, ALU.add, ALU.add))
            v.tensor_scalar(lim[:, 6:7], lim[:, 5:6], 1.0, None, ALU.max).then_inc(win_lims, 1)
            dve.wait_ge(rows_t, 1)
            step(v.memset(rows[:, :, :], 0.0))
            step(v.memset(rows[:, 3, :], 1.0))
            step(v.tensor_copy(rows[:, 0, 0:NW], bank[4][0:1, 0:NW]))
            step(v.tensor_copy(rows[:, 2, 0:NW], bank[4][0:1, 128:128 + NW]))
            step(v.tensor_tensor_scan(rows[:, 1, 1:NW + 1], rows[:, 3, 0:NW], rows[:, 2, 0:NW], 0.0, ALU.mult, ALU.add))
            v.tensor_copy(table[:, :, :], rows[:, 0:2, :]).then_inc(table_ready, 1)

            dve.wait_ge(x_loaded, 16)
            v.tensor_reduce(stat[0:P, 0:1], xs32[:, :, :].rearrange("p t f -> p (t f)"), X, ALU.max,
                            apply_absolute_value=True).then_inc(stat_ready, 1)
            dve.wait_ge(b_loaded, 16)
            v.tensor_reduce(stat[:, 3:5], bcol[:, :].rearrange("p (h o) -> p h o", o=1), X, ALU.max,
                            apply_absolute_value=True).then_inc(stat_ready, 1)
            dve.wait_ge(wn_loaded, 16)
            v.tensor_reduce(stat[:, 5:7], wn_nat[:, :, :], X, ALU.max, apply_absolute_value=True
                            ).then_inc(stat_ready, 1)
            dve.wait_ge(stat_psum, 1)
            step(v.tensor_reduce(stat_r[:, 0:1], bank[5][0:8, 0:128], X, ALU.max))
            v.tensor_reduce(stat_r[:, 1:2], bank[5][0:8, 0:128], X, ALU.add).then_inc(stat_red, 1)
            dve.wait_ge(stat_row, 1)
            step(v.tensor_copy(sv[:, :, :], bank[6][0:1, 0:16].rearrange("p (a b) -> p a b", a=2)))
            step(v.tensor_tensor(sw[:, 0:1], sv[:, 0, 1:2], sv[:, 0, 2:3], ALU.max))
            step(v.tensor_tensor(sw[:, 1:2], sv[:, 0, 3:4], sv[:, 0, 4:5], ALU.max))
            step(v.tensor_copy(sw[:, 4:5], sv[:, 0, 0:1]))
            step(v.tensor_tensor(sw[:, 2:3], sw[:, 4:5], sw[:, 0:1], ALU.mult))
            step(v.tensor_tensor(sw[:, 5:6], sw[:, 2:3], sw[:, 1:2], ALU.add))
            step(v.tensor_tensor(sw[:, 3:4], sv[:, 1, 5:6], sv[:, 1, 6:7], ALU.add))
            step(v.tensor_scalar(sw[:, 6:7], sw[:, 3:4], 1.01 * F ** 0.5, None, ALU.mult))
            step(v.tensor_scalar(sw[:, 8:11], sw[:, 4:7], 1e-20, None, ALU.max))
            step(v.tensor_scalar(svi[:, 0:3], sw[:, 8:11].bitcast(I32), 0x7F800000, None, ALU.bitwise_and))
            step(v.tensor_scalar(sbits[:, 0:3], svi[:, 0:3], -1.0, float(268 << 23), ALU.mult, ALU.add))
            step(v.tensor_copy(srow[:, 0:3], sbits[:, 0:3].bitcast(F32)))
            v.tensor_scalar(srow[:, 3:6], svi[:, 0:3].bitcast(F32), 2.0 ** -14, None, ALU.mult).then_inc(scale_row, 1)
            dve.wait_ge(scale_psum, 1)
            v.tensor_copy(scales[:, :], bank[7][:, 0:6]).then_inc(scale_ready, 1)

            dve.wait_ge(table_ready, 1)
            with dve.Fori(0, NW) as w:
                first = dve.value_load(table[0:1, 0, ds(w, 1)], min_val=0, max_val=CH)
                g0 = dve.value_load(table[0:1, 1, ds(w, 1)], min_val=0, max_val=NW * CH)
                g1 = dve.value_load(table[0:1, 1, ds(w + 1, 1)], min_val=0, max_val=NW * CH)
                off = woff[:, ds(w, 1)]
                with dve.Fori(g0, g1) as j:
                    chunk = nc.s_assert_within((j - g0) * G + first, 0, CH,
                                               skip_runtime_bounds_check_because="groups cover whole chunks up to the padding")
                    for k in range(G):
                        dve.wait_ge(jobs_done, j * G + k + 1)
                        v.tensor_scalar(src_hot[k][:, :], iota16[:, 0:P], srcp_t[:, ds(chunk + k, 1)], None,
                                        ALU.is_equal)
                        v.tensor_scalar(key_hot[k][:, :], iota16[:, :], off, key_t[:, ds(chunk + k, 1)], ALU.add,
                                        ALU.is_equal).then_inc(hot_ready, 1)

            dve.wait_ge(tr_free, 4 * NT + 2)
            step(v.tensor_reduce(rdeg_dst[:, :], deg_part[:, :, :], X, ALU.add))
            step(v.tensor_scalar(rdeg_dst[:, :], rdeg_dst[:, :], 1.0, None, ALU.max))
            step(v.reciprocal(rdeg_dst[:, :], rdeg_dst[:, :]))
            step(v.tensor_scalar(rdeg_dst[:, :], rdeg_dst[:, :], scales[0:P, 5:6], None, ALU.mult))
            dve.wait_ge(deg_done, NT)
            step(v.tensor_scalar(rdeg_src[:, :], degb[0:P, 0:NT], 1.0, None, ALU.max))
            step(v.reciprocal(rdeg_src[:, :], rdeg_src[:, :]))

            def affine(T, Q, i, base):
                ps = dense[i % 2]
                dve.wait_ge(mm_done, Q + 1)
                v.scalar_tensor_tensor(t1[:, :], ps[0:P, 0:F], 1.0, bias_sb[:, :], ALU.mult, ALU.add
                                       ).then_inc(dve_step, 1)
                dve.wait_ge(dve_step, base + 1)
                v.scalar_tensor_tensor(t2[i % 2][:, :], ps[0:P, F:2 * F], rdeg_src[:, ds(T, 1)], t1[:, :],
                                       ALU.mult, ALU.add).then_inc(bank_read, 1)
                dve.wait_ge(bank_read, Q + 1)

            def low_part1(Q, i):
                dve.wait_ge(relu_ready, Q + 1)
                v.scalar_tensor_tensor(part[i % 2][:, F:2 * F], hb[i % 2][:, :], scales[0:P, 1:2],
                                       part[i % 2][:, 0:F], ALU.mult, ALU.subtract).then_inc(lo_ready, 1)

            dve.wait_ge(wts_loaded[0], 32)
            base0 = done[0]
            with dve.Fori(0, NB) as n:
                for i in range(BT):
                    Q = n * BT + i
                    affine(Q, Q, i, base0 + Q)
                    if i:
                        low_part1(Q - 1, i - 1)
                low_part1(n * BT + BT - 1, BT - 1)
            done[0] = base0 + NT

            dve.wait_ge(wts_loaded[1], 32)
            dve.wait_ge(part_stored[0], 32 * 3 * NB)
            dve.wait_ge(part_stored[1], 32 * 2 * NB)

            def norm_tail(n, i):
                T, b = n * BT + i, i % 2
                dve.wait_ge(sd_ready, T + 1)
                step(v.reciprocal(sd[b][:, 1:2], sd[b][:, 0:1]))
                v.tensor_scalar(xy[n % 2][:, i, :], hb[b][:, :], mv[b][:, 0:1], sd[b][:, 1:2], ALU.subtract, ALU.mult
                                ).then_inc(y_ready, 1)

            def phase_b(n):
                Q0 = BT * phase_of["B", n]
                dve.wait_ge(xy_loaded[n % 2], 16 * (n // 2 + 1))
                for i in range(BT):
                    T, b = n * BT + i, i % 2
                    affine(T, Q0 + i, i, done[0])
                    done[0] += 1
                    step(v.scalar_tensor_tensor(hb[b][:, :], t2[b][:, :], 0.0, xy[n % 2][:, i, :], ALU.max, ALU.add))
                    step(v.bn_stats(st6[b][:, :], hb[b][:, :]))
                    v.bn_aggr(mv[b][:, :], st6[b][:, :]).then_inc(var_ready, 1)
                    if i:
                        norm_tail(n, i - 1)
                norm_tail(n, BT - 1)

            def low_part2(n, i):
                T, b = n * BT + i, i % 2
                dve.wait_ge(sphi_ready, T + 1)
                v.scalar_tensor_tensor(part[b][:, F:2 * F], sparse[b][:, :], scales[0:P, 2:3], part[b][:, 0:F],
                                       ALU.mult, ALU.subtract).then_inc(sp_lo, 1)

            def phase_c(n):
                Q0 = BT * phase_of["C", n]
                for i in range(BT):
                    T, b = n * BT + i, i % 2
                    dve.wait_ge(hn_copied, T + 1)
                    v.scalar_tensor_tensor(xy[n % 2][:, i, :], dense[b][0:P, 0:F], 1.0, xy[n % 2][:, i, :], ALU.mult, ALU.add
                                           ).then_inc(z_ready, 1)
                    dve.wait_ge(z_ready, T + 1)
                    dve.sem_inc(bank_read, 1)
                    cur = hb[b]
                    for r in range(MAXK // 8):
                        step(v.max(m8[:, :], cur[:, :]))
                        step(v.match_replace(work[:, :], m8[:, :], cur[:, :], NEG))
                        cur = work
                    v.scalar_tensor_tensor(sparse[b][:, :], work[:, :], NEG, hb[b][:, :], ALU.is_equal, ALU.mult
                                           ).then_inc(sparse_ready, 1)
                    if i:
                        low_part2(n, i - 1)
                low_part2(n, BT - 1)

            for kind, n in phases2:
                (phase_b if kind == "B" else phase_c)(n)

            base3 = done[0]
            dve.sem_inc(n3_read, BT)
            with dve.Fori(0, NB) as g:
                for i in range(BT):
                    T = g * BT + i
                    base = base3 + T * 4
                    dve.wait_ge(n3_done, T + 1)
                    dve.wait_ge(z_loaded[i], g * 16 + 16)
                    ps, zt = bank[i], xy[0][:, i, :]
                    v.scalar_tensor_tensor(zt, ps[0:P, 0:F], rdeg_dst[:, ds(T, 1)], zt, ALU.mult, ALU.add
                                           ).then_inc(dve_step, 1)
                    dve.wait_ge(dve_step, base + 1)
                    v.scalar_tensor_tensor(zt, ps[0:P, F:2 * F], rdeg_dst[:, ds(T, 1)], zt, ALU.mult, ALU.add
                                           ).then_inc(dve_step, 1)
                    dve.wait_ge(dve_step, base + 2)
                    v.bn_stats(st6[i % 2][:, :], zt).then_inc(dve_step, 1)
                    dve.wait_ge(dve_step, base + 3)
                    dve.sem_inc(stats3, 1)
                    v.bn_aggr(mv[i % 2][:, :], st6[i % 2][:, :]).then_inc(var3, 1)
                    dve.wait_ge(sd3, T + 1)
                    v.reciprocal(sd[i % 2][:, 1:2], sd[i % 2][:, 0:1]).then_inc(dve_step, 1)
                    dve.wait_ge(dve_step, base + 4)
                    dve.wait_ge(o_stored[i], g * 16)
                    v.tensor_scalar(xy[1][:, i, :], zt, mv[i % 2][:, 0:1], sd[i % 2][:, 1:2],
                                    ALU.subtract, ALU.mult).then_inc(o_ready, 1)
                    dve.wait_ge(o_ready, T + 1)
                    dve.sem_inc(n3_read, 1)

        @block.scalar
        def _(act):
            a = nc.scalar
            act.wait_ge(w_loaded, 32)
            act.wait_ge(const_ready, NCONST)
            for h in range(2):
                a.activation(junk[:, :], w_nat[:, 0, h, :], ACT.Abs, accum_out=stat[:, 1 + h:2 + h]
                             ).then_inc(act_step, 1)
                act.wait_ge(act_step, h + 1)
            act.sem_inc(act_sums, 1)
            for l in range(2):
                for h in range(2):
                    act.wait_ge(wt_psum, 2 * l + h + 1)
                    b = bank[6 + h]
                    a.activation(w_t[:, l, :, h * 128:(h + 1) * 128],
                                 b[:, :].rearrange("p (c o) -> p c o", c=4), ACT.Copy).then_inc(wt_copied, 1)
            act.sem_inc(win_free, 2)
            act.sem_inc(tr_free, 2)
            act.wait_ge(table_ready, 1)
            act.wait_ge(wt_stored, 16)
            act.wait_ge(scale_ready, 1)

            def win_copy(t, par, u):
                w = t * WT + u
                g1 = act.value_load(table[0:1, 1, ds(w + 1, 1)], min_val=0, max_val=NW * CH)
                act.wait_ge(jobs_done, g1 * G + G)
                if u == 0:
                    act.wait_ge(slab_stored[par], t * 8 if par == 0 else (t - 1) * 8)
                q = (par + u) % 2
                out0 = slab[par][:, 0:B0W, u * W:(u + 1) * W]
                out1 = slab[par][:, B0W:NT, u * W:(u + 1) * W]
                a.activation(out0, bank[2 * q][0:P, 0:B0W * W].rearrange("p (b d) -> p b d", d=W), ACT.Copy)
                a.activation(out1, bank[2 * q + 1][0:P, 0:(NT - B0W) * W].rearrange("p (b d) -> p b d", d=W),
                             ACT.Copy).then_inc(win_free, 1)

            def tr_copy(t):
                for g in range(4):
                    act.wait_ge(tr_done, 4 * t + g + 1)
                    a.activation(ct[:, ds(t, 1), TG0[g] * P:(TG0[g] + TG[g]) * P].rearrange("p o (b s) -> p (o b) s", s=P),
                                 tr16[g % 2][0:P, 0:TG[g], 0:P], ACT.Copy,
                                 accum_out=deg_part[:, ds(t, 1), g:g + 1].rearrange("p o g -> p (o g)")
                                 ).then_inc(tr_free, 1)

            for u in range(WT):
                win_copy(0, 0, u)
            with act.Fori(0, NT // 2) as m:
                t = m * 2 + 1
                for par, tt in ((1, t), (0, t + 1)):
                    win_copy(tt, par, 0)
                    tr_copy(tt - 1)
                    for u in range(1, WT):
                        win_copy(tt, par, u)
            tr_copy(NT - 1)

            act.wait_ge(tr_done, 4 * NT)
            act.wait_ge(slab_stored[0], 16 * 13)
            act.wait_ge(slab_stored[1], 16 * 12)
            act.wait_ge(x_split, NT)

            def agg_copy(k, n, par, l):
                act.wait_ge(agg_done, k + 1)
                for f in range(2):
                    for h, (lo, wd) in enumerate(((0, H0), (H0, H1))):
                        last = a.activation(nt_sb[par][:, f, lo:lo + wd], agg[f][h][:, 0:wd], ACT.Copy,
                                            scale=scales[:, 3 + l:4 + l])
                last.then_inc(agg_copied, 1)

            def tr_out(Q, i):
                act.wait_ge(tp_done, Q + 1)
                act.wait_ge(mm_done, free_at(Q, i))
                a.activation(tr_sb[i % 2][:, :, :], tp, ACT.Copy).then_inc(tp_copied, 1)

            def b1(n, Q0):
                tr_out(Q0, 0)
                for i in range(BT):
                    if i + 1 < BT:
                        tr_out(Q0 + i + 1, i + 1)
                    b = i % 2
                    act.wait_ge(bank_read, Q0 + i + 1)
                    act.wait_ge(part_stored[b], (n * uses(i) + c0(i)) * 32)
                    a.activation(hb[b][:, :], t2[b][:, :], ACT.Relu)
                    a.activation(part[b][:, 0:F], t2[b][:, :], ACT.Relu, scale=scales[0:P, 1:2]
                                 ).then_inc(relu_ready, 1)

            agg_copy(0, 0, 0, 0)
            with act.Fori(0, NB // 2) as m:
                n = m * 2 + 1
                agg_copy(n, n, 1, 0)
                b1(n - 1, (n - 1) * BT)
                agg_copy(n + 1, n + 1, 0, 0)
                b1(n, n * BT)
            b1(NB - 1, (NB - 1) * BT)

            def phase_b(n):
                Q0 = BT * phase_of["B", n]
                tr_out(Q0, 0)
                for i in range(BT):
                    if i + 1 < BT:
                        tr_out(Q0 + i + 1, i + 1)
                    b, T = i % 2, n * BT + i
                    act.wait_ge(var_ready, T + 1)
                    a.activation(sd[b][:, 0:1], mv[b][:, 1:2], ACT.Sqrt, bias=epsb[:, :]).then_inc(sd_ready, 1)

            def phase_c(n):
                Q0 = BT * phase_of["C", n]
                tr_out(Q0, 0)

                def high(i):
                    b, T = i % 2, n * BT + i
                    act.wait_ge(sparse_ready, T + 1)
                    act.wait_ge(sp_stored[b], 16 * (uses(i) * n + c0(i)))
                    a.activation(part[b][:, 0:F], sparse[b][:, :], ACT.Copy, scale=scales[0:P, 2:3]
                                 ).then_inc(sphi_ready, 1)

                for i in range(BT):
                    if i + 1 < BT:
                        tr_out(Q0 + i + 1, i + 1)
                    b, T = i % 2, n * BT + i
                    act.wait_ge(mm_done, Q0 + i + 1)
                    if i == 0:
                        act.wait_ge(y_ready, (n + 1) * BT)
                    if i >= 2:
                        act.wait_ge(sparse_ready, T - 1)
                    a.activation(hb[b][:, :], dense[b][0:P, F:2 * F], ACT.Copy).then_inc(hn_copied, 1)
                    if i:
                        high(i - 1)
                high(BT - 1)

            act.wait_ge(part_stored[0], 32 * 3 * NB)
            act.wait_ge(part_stored[1], 32 * 2 * NB)
            agg_copy(NB, 0, 1, 1)
            agg_copy(NB + 1, 1, 0, 1)
            phase_b(0)
            for k in range(2, NB):
                agg_copy(NB + k, k, (k + 1) % 2, 1)
                if k == NB - 1:
                    for c in range(NB):
                        act.dma_start(ct[:, c * BT:(c + 1) * BT, :],
                                      c_dram[c * BT:(c + 1) * BT, :, :].rearrange("t p n -> p t n")
                                      ).then_inc(c_loaded[c // 3], 16)
                phase_c(k - 2)
                phase_b(k - 1)
            phase_c(NB - 2)
            phase_b(NB - 1)
            phase_c(NB - 1)

            with act.Fori(0, NB) as g:
                for i in range(BT):
                    act.wait_ge(var3, g * BT + i + 1)
                    a.activation(sd[i % 2][:, 0:1], mv[i % 2][:, 1:2], ACT.Sqrt, bias=epsb[:, :]).then_inc(sd3, 1)

        @block.tensor
        def _(pe):
            mm = nc.tensor.matmul
            pe.wait_ge(const_ready, NCONST)
            for j, (m, b) in enumerate(((srcp, bank[0]), (key, bank[1]))):
                pe.wait_ge(edge_keys, j + 1)
                for g in range(EQ):
                    last = nc.tensor.transpose(b[0:P, g * EG:(g + 1) * EG], m[:, g, :], identf[0:EG, 0:EG])
            last.then_inc(keys_t, 1)
            pe.wait_ge(diag_ready, 1)
            for j in range(2):
                for g in range(EQ):
                    last = mm(bank[2 + j][0:P, g * EG:(g + 1) * EG], onesq[:, :], wdiag[:, j, g, :],
                              start=True, stop=True)
            last.then_inc(lims_b, 1)
            pe.wait_ge(w_loaded, 32)
            for l in range(2):
                for h in range(2):
                    if l:
                        pe.wait_ge(wt_copied, h + 1)
                    for c in range(4):
                        last = nc.tensor.transpose(bank[6 + h][:, c * 128:(c + 1) * 128],
                                                   w_nat[:, l, h, c * 128:(c + 1) * 128], identf[:, :])
                    last.then_inc(wt_psum, 1)
            pe.wait_ge(win_lims, 1)
            mm(bank[4][0:1, 0:P], lim[:, 2:3], identf[0:P, 0:P], start=True, stop=True)
            mm(bank[4][0:1, 128:128 + P], lim[:, 6:7], identf[0:P, 0:P], start=True, stop=True).then_inc(rows_t, 1)
            pe.wait_ge(stat_ready, 3)
            pe.wait_ge(act_sums, 1)
            nc.tensor.transpose(bank[5][0:8, 0:128], stat[:, :], identf[:, :]).then_inc(stat_psum, 1)
            pe.wait_ge(stat_red, 1)
            pe.wait_ge(wt_copied, 4)
            mm(bank[6][0:1, 0:8], stat_r[:, 0:1], identf[0:8, 0:8], start=True, stop=True)
            mm(bank[6][0:1, 8:16], stat_r[:, 1:2], identf[0:8, 0:8], start=True, stop=True).then_inc(stat_row, 1)
            pe.wait_ge(scale_row, 1)
            mm(bank[7][:, 0:6], onesf[:, :], srow[:, :], start=True, stop=True).then_inc(scale_psum, 1)
            pe.wait_ge(table_ready, 1)
            pe.sem_inc(jobs_done, G)

            def job(q, k, start, stop):
                pe_kw = dict(start=start, stop=stop, skip_group_check=True)
                mm(bank[2 * q][0:P, 0:B0W * W], src_hot[k][:, :], key_hot[k][:, 0:B0W * W], **pe_kw)
                mm(bank[2 * q + 1][0:P, 0:(NT - B0W) * W], src_hot[k][:, :], key_hot[k][:, B0W * W:KEY], **pe_kw
                   ).then_inc(jobs_done, 1)

            def window(t, par, u):
                w = t * WT + u
                q = (par + u) % 2
                g0 = pe.value_load(table[0:1, 1, ds(w, 1)], min_val=0, max_val=NW * CH)
                g1 = pe.value_load(table[0:1, 1, ds(w + 1, 1)], min_val=0, max_val=NW * CH)
                pe.wait_ge(win_free, w + 1)
                for k in range(G):
                    pe.wait_ge(hot_ready, g0 * G + k + 1)
                    job(q, k, k == 0, False)
                with pe.If(g0 + 1 < g1):
                    with pe.Fori(g0 + 1, g1) as j:
                        for k in range(G):
                            pe.wait_ge(hot_ready, j * G + k + 1)
                            job(q, k, False, False)

            def transposes(t, par):
                pe.wait_ge(win_free, WT * t + WT + 2)
                for g in range(4):
                    pe.wait_ge(tr_free, 4 * t + g + 1)
                    for i in range(TG[g]):
                        last = nc.tensor.transpose(tr16[g % 2][0:P, i, 0:P], slab[par][:, TG0[g] + i, :], ident16[:, :])
                    last.then_inc(tr_done, 1)

            for u in range(WT):
                window(0, 0, u)
            with pe.Fori(0, NT // 2) as m:
                t = m * 2 + 1
                for par, tt in ((1, t), (0, t + 1)):
                    window(tt, par, 0)
                    transposes(tt - 1, 1 - par)
                    for u in range(1, WT):
                        window(tt, par, u)
            transposes(NT - 1, 0)

            pe.wait_ge(tr_free, 4 * NT + 2)
            pe.wait_ge(scale_ready, 1)
            with pe.Fori(0, NT) as b:
                for t in range(NT):
                    last = mm(degb[0:P, ds(b, 1)], ct[:, t, ds(b * P, P)], ones16[:, :], start=t == 0, stop=t == NT - 1)
                last.then_inc(deg_done, 1)

            pe.wait_ge(x_split, NT)

            def aggregate(k, n, parts=None):
                pe.wait_ge(agg_copied, k)

                def one(t, start, stop):
                    for h, (lo, wd) in enumerate(((0, H0), (H0, H1))):
                        for f in range(2):
                            for p in range(2):
                                if isinstance(t, int):
                                    lhs = xs[:, t, p * F + f * 128:p * F + f * 128 + 128]
                                    rhs = ct[:, t, ds(n * BT * P + lo, wd)]
                                else:
                                    lhs = xs[:, ds(t, 1), p * F + f * 128:p * F + f * 128 + 128].rearrange("p o f -> p (o f)")
                                    rhs = ct[:, ds(t, 1), ds(n * BT * P + lo, wd)].rearrange("p o f -> p (o f)")
                                last = mm(agg[f][h][:, 0:wd], lhs, rhs, start=start and p == 0, stop=stop and p == 1,
                                          skip_group_check=True)
                    return last

                if parts is None:
                    one(0, True, False)
                    with pe.Fori(1, NT - 1) as t:
                        one(t, False, False)
                else:
                    for c in range(NB):
                        pe.wait_ge(parts[c], 16)
                        if c == 0:
                            one(0, True, False)
                        with pe.Fori(max(1, c * BT), min(NT - 1, (c + 1) * BT)) as t:
                            one(t, False, False)
                one(NT - 1, False, True).then_inc(agg_done, 1)

            def transpose_tile(Q, tile):
                pe.wait_ge(tp_copied, Q)
                for c in range(2):
                    last = nc.tensor.transpose(tp[:, c, :], tile[:, c * 128:(c + 1) * 128], identf[0:P, 0:P])
                last.then_inc(tp_done, 1)

            def products(n, Q0, nt, selfs):
                pe.wait_ge(self_loaded, selfs * 16)
                transpose_tile(Q0, selfb[:, 0, :])
                for i in range(BT):
                    if i + 1 < BT:
                        transpose_tile(Q0 + i + 1, selfb[:, i + 1, :])
                    pe.wait_ge(tp_copied, Q0 + i + 1)
                    pe.wait_ge(bank_read, free_at(Q0 + i, i))
                    ps = dense[i % 2]
                    for c in range(2):
                        mm(ps[0:P, 0:F], tr_sb[i % 2][:, c, :], wt_sb[:, c, :], start=c == 0, stop=c == 1,
                           skip_group_check=True)
                    for c in range(2):
                        last = mm(ps[0:P, F:2 * F], nt[:, c, i * P:(i + 1) * P], wt_sb[:, 2 + c, :],
                                  start=c == 0, stop=c == 1, skip_group_check=True)
                    last.then_inc(mm_done, 1)

            aggregate(0, 0)
            pe.wait_ge(wts_loaded[0], 32)
            with pe.Fori(0, NB // 2) as m:
                n = m * 2 + 1
                aggregate(n, n)
                products(n - 1, (n - 1) * BT, nt_sb[0], n)
                aggregate(n + 1, n + 1)
                products(n, n * BT, nt_sb[1], n + 1)
            pe.wait_ge(agg_copied, NB)
            products(NB - 1, (NB - 1) * BT, nt_sb[0], NB)

            def products2(n):
                products(n, BT * phase_of["B", n], nt_sb[(n + 1) % 2], NB + n + 1)

            def sparse_products(n):
                Q0 = BT * phase_of["C", n]
                pe.wait_ge(y_ready, n * BT + 1)
                transpose_tile(Q0, xy[n % 2][:, 0, :])
                for i in range(BT):
                    if i + 1 < BT:
                        pe.wait_ge(y_ready, n * BT + i + 2)
                        transpose_tile(Q0 + i + 1, xy[n % 2][:, i + 1, :])
                    pe.wait_ge(tp_copied, Q0 + i + 1)
                    pe.wait_ge(bank_read, free_at(Q0 + i, i))
                    for c in range(2):
                        last = mm(dense[i % 2][0:P, :], tr_sb[i % 2][:, c, :], wsn_sb[:, c, :], start=c == 0, stop=c == 1)
                    last.then_inc(mm_done, 1)

            aggregate(NB, 0, xs_loaded[0])
            aggregate(NB + 1, 1)
            pe.wait_ge(wts_loaded[1], 32)
            products2(0)
            pe.wait_ge(wsn_loaded, 32)
            for k in range(2, NB):
                aggregate(NB + k, k)
                sparse_products(k - 2)
                products2(k - 1)
            sparse_products(NB - 2)
            pe.wait_ge(agg_copied, 2 * NB)
            products2(NB - 1)
            sparse_products(NB - 1)

            pe.wait_ge(bank_read, BT * (NB + len(phases2)))
            for c in range(NB):
                pe.wait_ge(xs_loaded[1][c], 16)
            for g0, g1, s, cnt in ((0, 3, c_loaded[0], 48), (3, NB, c_loaded[1], 32)):
                pe.wait_ge(s, cnt)
                with pe.Fori(g0, g1) as g:
                    for i in range(BT):
                        T = g * BT + i
                        pe.wait_ge(n3_read, T + 1)
                        for b in range(NT):
                            last = mm(bank[i][0:P, :], ct[:, ds(T, 1), b * P:(b + 1) * P].rearrange("p o d -> p (o d)"),
                                      xs[:, b, :], start=b == 0, stop=b == NT - 1)
                        last.then_inc(n3_done, 1)


_INS = ["x", "src", "dst", "L0_gnn_W0", "L0_gnn_b0", "L0_gnn_W1", "L0_gnn_b1", "L1_gnn_W_self", "L1_gnn_W_neigh"]


def kernel(**inputs):
    import numpy as _np
    import concourse.bacc as _bacc
    from concourse import mybir as _mybir
    from concourse.bass_utils import run_bass_kernel_spmd as _run

    nc = _bacc.Bacc("TRN2", target_bir_lowering=False, num_devices=1, dynamic_dma_scratch_size=1024)
    arrays, args = {}, []
    for name in _INS:
        a = _np.ascontiguousarray(inputs[name])
        arrays[f"in_{name}_dram"] = a
        args.append(nc.dram_tensor(f"in_{name}_dram", a.shape, _mybir.dt.from_np(a.dtype), kind="ExternalInput").ap())
    out = nc.dram_tensor("out_dram", (N, F), _mybir.dt.float32, kind="ExternalOutput").ap()
    gnn(nc, *args, out)
    r = _run(nc, [arrays], core_ids=[0])
    return r.results[0]["out_dram"]
```

```python
from contextlib import ExitStack

import concourse.bass as bass
from concourse import mybir

N, E, F = 3125, 50000, 256
P = 125
NT = N // P
CH = E // P
SLAB = N + 3
G = 4
W = 25
WT = P // W
NW = N // W
S = 5
SH = 63
KEY = NT * W
B0W = 13
EQ, EG = 4, CH // 4
DQ = 4
DR = (NT + DQ - 1) // DQ
BT = 5
NB = NT // BT
H0, H1 = 313, 312
MAXK = 32
EPS = 1e-5
NEG = -3.0e38
ROUND = 12582912.0
TG = [7, 6, 6, 6]
TG0 = [0, 7, 13, 19]

F32, F16, I32 = mybir.dt.float32, mybir.dt.float16, mybir.dt.int32
ALU = mybir.AluOpType
ACT = mybir.ActivationFunctionType
X = mybir.AxisListType.X
ds = bass.ds


def gnn(nc, x, src, dst, w0, b0, w1, b1, wself, wneigh, out):
    ctx = ExitStack()
    with ctx:
        sem_names = set()

        def sem(name):
            assert name not in sem_names
            sem_names.add(name)
            return ctx.enter_context(nc.semaphore(name))

        class Arena:

            def __init__(self, at, end):
                self.at, self.end = at, end

            def __call__(self, name, shape, dt):
                size = 2 if dt == F16 else 4
                for n in shape[1:]:
                    size *= n
                t = nc.alloc_sbuf_tensor_at(name, shape, dt, offset=self.at)
                self.at += (size + 31) // 32 * 32
                assert self.at <= self.end, (name, self.at, self.end)
                return t

        keep = Arena((nc.sbuf_base + 31) // 32 * 32, nc.sbuf_usable_end)
        ct_at = keep.at
        ct = keep("ct", [P, NT, N], F16)
        xs = keep("xs", [P, NT, 2 * F], F16)
        identf = keep("identf", [128, 128], F32)
        ident16 = keep("ident16", [P, P], F16)
        sel8 = keep("sel8", [P, DR, 8], F16)
        onesf = keep("onesf", [1, 128], F32)
        scales = keep("scales", [128, 6], F32)
        rdeg_src = keep("rdeg_src", [P, DR * DQ], F32)
        rdeg_dst = keep("rdeg_dst", [P, NT], F32)
        deg_part = keep("deg_part", [P, NT, 4], F32)
        epsb = keep("epsb", [P, 1], F32)
        xs32 = xs[:, :, :].bitcast(F32)
        shared_at = keep.at

        bld = Arena(shared_at, nc.sbuf_usable_end)
        slab = [bld(f"slab{i}", [P, SLAB], F16) for i in range(2)]
        slab3 = [t[:, 0:N].rearrange("p (b d) -> p b d", d=P) for t in slab]
        src_hot2 = [bld(f"src_hot{i}", [P, S, 128], F16) for i in range(2)]
        key_hot2 = [bld(f"key_hot{i}", [P, S, KEY], F16) for i in range(2)]
        src_hot = [src_hot2[0][:, k, :] for k in range(G)]
        key_hot = [key_hot2[0][:, k, :] for k in range(G)]
        job_key = bld("job_key", [P, NW, S], F32)
        job_src = bld("job_src", [P, NW, S], F32)
        iota16 = bld("iota16", [P, KEY], F16)
        key_t = bld("key_t", [P, CH + G], F32)
        srcp_t = bld("srcp_t", [P, CH + G], F32)
        woff = bld("woff", [P, NW], F32)
        table = bld("table", [1, 3, 128], I32)
        xscaled = bld("xscaled", [P, F], F32)
        xparts = bld("xparts", [P, 2 * F], F16)

        pre = Arena(ct_at, ct_at + NT * N * 2)
        edges_i = pre("edges_i", [EG, 2, EQ, P], I32)
        edges_f = pre("edges_f", [EG, 2, EQ, P], F32)
        hi_f = pre("hi_f", [EG, 2, EQ, P], F32)
        srcp = pre("srcp", [EG, EQ, P], F32)
        key = pre("key", [EG, EQ, P], F32)
        jcol = pre("jcol", [EG, EQ, P], F32)
        wlim = pre("wlim", [EG, 2, EQ], F32)
        onesq = pre("onesq", [P, P], F32)
        gather_k = [pre(f"gather_k{i}", [EG, EQ, P], F16) for i in range(3)]
        chunk_no = pre("chunk_no", [EG, EQ], F32)
        slot_no = pre("slot_no", [EG, NW, S], F32)
        fdiag = pre("fdiag", [P, NW], F32)
        firsts = pre("firsts", [EG, NW], F32)
        want = pre("want", [EG, NW, S], F32)
        pick = pre("pick", [EG, EQ, NW, S], F16)
        jwin = pre("jwin", [P, NW, S], F32)
        wdiag = pre("wdiag", [EG, 2, EQ, EG], F32)
        inc_f = pre("inc_f", [P, CH], F32)
        rev_f = pre("rev_f", [P, CH], F32)
        wcol = pre("wcol", [P, 1], F32)
        cover = pre("cover", [P, CH], F32)
        cover2 = pre("cover2", [P, CH], F32)
        cover3 = pre("cover3", [P, CH], F32)
        cover4 = pre("cover4", [P, CH], F32)
        lim = pre("lim", [P, 8], F32)
        rows = pre("rows", [1, 5, 128], F32)
        w_nat = pre("w_nat", [128, 2, 2, 2 * F], F32)
        w_t = pre("w_t", [128, 2, 4, F], F32)
        wn_nat = pre("wn_nat", [128, 2, F], F32)
        bcol = pre("bcol", [128, 2], F32)
        junk = pre("junk", [128, 2 * F], F32)
        stat = pre("stat", [128, 8], F32)
        stat_r = pre("stat_r", [8, 2], F32)
        sv = pre("sv", [1, 2, 8], F32)
        sw = pre("sw", [1, 16], F32)
        svi = pre("svi", [1, 8], I32)
        sbits = pre("sbits", [1, 8], I32)
        srow = pre("srow", [1, 6], F32)

        lay = Arena(shared_at, nc.sbuf_usable_end)
        wt_sb = lay("wt_sb", [128, 4, F], F32)
        wsn_sb = lay("wsn_sb", [128, 2, 2 * F], F32)
        bias_sb = lay("bias_sb", [P, F], F32)
        nt_sb = [lay(f"nt_sb{i}", [128, 2, BT * P], F32) for i in range(2)]
        selfb = lay("selfb", [P, BT, F], F32)
        xy = [lay(f"xy{i}", [P, BT, F], F32) for i in range(2)]
        tr_sb = [lay(f"tr_sb{i}", [128, 2, P], F32) for i in range(2)]
        t2 = [lay(f"t2_{i}", [P, F], F32) for i in range(2)]
        hb = [lay(f"hb{i}", [P, F], F32) for i in range(2)]
        part = [lay(f"part{i}", [P, 2 * F], F16) for i in range(2)]
        work = lay("work", [P, F], F32)
        m8 = lay("m8", [P, 8], F32)
        st6 = [lay(f"st6_{i}", [P, 6], F32) for i in range(2)]
        mv = [lay(f"mv{i}", [P, 2], F32) for i in range(2)]
        sd = [lay(f"sd{i}", [P, 2], F32) for i in range(2)]
        deg_rows = xy[1][0:8, 0:2, :].rearrange("p i f -> p (i f)")[:, 0:DQ * P]
        t1 = work
        sparse = t2

        c_dram = nc.dram_tensor("c_dram", (NT, P, N), F16).ap()
        wt_dram = nc.dram_tensor("wt_dram", (2, 128, 4 * F), F32).ap()
        h1_dram = nc.dram_tensor("h1_dram", (NT, P, F), F32).ap()
        parts_dram = [nc.dram_tensor(f"parts_dram{i}", (NT, P, 2 * F), F16).ap() for i in range(2)]
        z_dram = nc.dram_tensor("z_dram", (NT, P, F), F32).ap()
        x_t = x.rearrange("(t p) f -> t p f", p=P)
        out_t = out.rearrange("(t p) f -> t p f", p=P)

        bank = [ctx.enter_context(nc.psum_tensor(f"bank{i}", [128, 512], F32)) for i in range(8)]
        pick_bank = [[bank[0], bank[1]], [bank[2], bank[3]], [bank[4], bank[5]]]
        tr16 = [bank[4 + i][:, :].bitcast(F16).rearrange("p (k c) -> p k c", c=128) for i in range(2)]
        agg = [[bank[0], bank[1]], [bank[2], bank[3]]]
        tp = bank[4][:, 0:2 * P].rearrange("p (c n) -> p c n", c=2)
        dense = [bank[5], bank[6]]

        const_ready = sem("const_ready")
        src_loaded, dst_loaded = sem("src_loaded"), sem("dst_loaded")
        x_loaded, w_loaded, wn_loaded, b_loaded = sem("x_loaded"), sem("w_loaded"), sem("wn_loaded"), sem("b_loaded")
        edge_keys, win_lims, lims_rows = sem("edge_keys"), sem("win_lims"), sem("lims_rows")
        keys_t, lims_b, rows_t = sem("keys_t"), sem("lims_b"), sem("rows_t")
        diag_ready = sem("diag_ready")
        wt_psum, wt_copied, wt_stored = sem("wt_psum"), sem("wt_copied"), sem("wt_stored")
        stat_ready, stat_psum, stat_red, stat_row = sem("stat_ready"), sem("stat_psum"), sem("stat_red"), sem("stat_row")
        scale_row, scale_psum, scale_ready = sem("scale_row"), sem("scale_psum"), sem("scale_ready")
        table_ready, act_sums = sem("table_ready"), sem("act_sums")
        first_rows, picked, job_table = sem("first_rows"), sem("picked"), sem("job_table")
        firsts_b, fdiag_ready = sem("firsts_b"), sem("fdiag_ready")
        win_hot, win_done, deg_summed, deg_copied = sem("win_hot"), sem("win_done"), sem("deg_summed"), sem("deg_copied")
        hot_ready, jobs_done = sem("hot_ready"), sem("jobs_done")
        win_free, tr_done, tr_free = sem("win_free"), sem("tr_done"), sem("tr_free")
        slab_stored = [sem("slab_stored0"), sem("slab_stored1")]
        x_split, x_parts, stats3 = sem("x_split"), sem("x_parts"), sem("stats3")
        deg_done, rdeg_ready = sem("deg_done"), sem("rdeg_ready")
        agg_done, agg_copied = sem("agg_done"), sem("agg_copied")
        tp_done, tp_copied = sem("tp_done"), sem("tp_copied")
        mm_done, bank_read = sem("mm_done"), sem("bank_read")
        relu_ready, lo_ready = sem("relu_ready"), sem("lo_ready")
        part_stored = [sem("part_stored0"), sem("part_stored1")]
        self_loaded, xy_loaded = sem("self_loaded"), [sem("xy_loaded0"), sem("xy_loaded1")]
        wts_loaded, wsn_loaded = [sem("wts_loaded0"), sem("wts_loaded1")], sem("wsn_loaded")
        var_ready, sd_ready, y_ready = sem("var_ready"), sem("sd_ready"), sem("y_ready")
        hn_copied, sparse_ready, sphi_ready, sp_lo = sem("hn_copied"), sem("sparse_ready"), sem("sphi_ready"), sem("sp_lo")
        sp_stored, z_stored = [sem("sp_stored0"), sem("sp_stored1")], sem("z_stored")
        z_ready = sem("z_ready")
        xs_loaded = [[sem(f"xs_loaded{l}_{c}") for c in range(NB)] for l in (2, 3)]
        c_loaded = [sem("c_loaded0"), sem("c_loaded1")]
        n3_done, n3_read = sem("n3_done"), sem("n3_read")
        z_loaded, o_stored = [sem(f"z_loaded{i}") for i in range(BT)], [sem(f"o_stored{i}") for i in range(BT)]
        o_ready, var3, sd3 = sem("o_ready"), sem("var3"), sem("sd3")
        dve_step, act_step, pool_step = sem("dve_step"), sem("act_step"), sem("pool_step")

        phases2, q = [("B", 0)], 0
        for k in range(2, NB):
            phases2 += [("C", k - 2), ("B", k - 1)]
        phases2 += [("C", NB - 2), ("B", NB - 1), ("C", NB - 1)]
        phase_of = {p: NB + i for i, p in enumerate(phases2)}

        def c0(i):
            return i // 2

        def uses(i):
            return 3 if i % 2 == 0 else 2

        def free_at(Q, i):
            return Q if i == 0 else Q - 1

        block = ctx.enter_context(nc.Block())

        @block.sync
        def _(sp):
            sp.dma_start(edges_i[:, 0], src.rearrange("(g q p) -> q g p", g=EQ, p=P)).then_inc(src_loaded, 16)
            sp.dma_start(edges_i[:, 1], dst.rearrange("(g q p) -> q g p", g=EQ, p=P)).then_inc(dst_loaded, 16)
            sp.dma_start(w_nat[:, 0], w0.rearrange("(h p) k -> p h k", p=128)).then_inc(w_loaded, 16)
            sp.dma_start(w_nat[:, 1], w1.rearrange("(h p) k -> p h k", p=128)).then_inc(w_loaded, 16)
            sp.dma_start(wn_nat[:, :, :], wneigh.rearrange("(h p) k -> p h k", p=128)).then_inc(wn_loaded, 16)
            sp.dma_start(bcol[:, :], b0.rearrange("(h p) -> p h", p=128),
                         allow_slow_non_contiguous=True).then_inc(b_loaded, 16)
            sp.dma_start(xs32[:, :, :], x.rearrange("(t p) f -> p t f", p=P)).then_inc(x_loaded, 16)
            sp.wait_ge(wt_copied, 4)
            sp.dma_start(wt_dram.rearrange("l p f -> p l f"), w_t[:, :, :, :].rearrange("p l c f -> p l (c f)")
                         ).then_inc(wt_stored, 16)

            def store_slab(t, par):
                sp.wait_ge(win_free, WT * t + WT + 2)
                sp.dma_start(c_dram[ds(t, 1), :, :].rearrange("o p n -> (o p) n"),
                             slab[par][:, 0:N]).then_inc(slab_stored[par], 16)

            with sp.Fori(0, NT // 2) as m:
                t = m * 2
                store_slab(t, 0)
                store_slab(t + 1, 1)
            store_slab(NT - 1, 0)

            sp.wait_ge(tr_done, 4 * NT)
            sp.wait_ge(x_split, NT)
            sp.wait_ge(slab_stored[0], 16 * 13)
            sp.wait_ge(slab_stored[1], 16 * 12)
            sp.dma_start(wt_sb[:, :, :].rearrange("p c f -> p (c f)"), wt_dram[0]).then_inc(wts_loaded[0], 16)
            sp.dma_start(bias_sb[:, :], b0.rearrange("(o f) -> o f", o=1).broadcast_to([P, F])).then_inc(wts_loaded[0], 16)
            sp.dma_start(wsn_sb[:, :, 0:F], wself.rearrange("(c p) f -> p c f", p=128)).then_inc(wsn_loaded, 16)
            sp.dma_start(wsn_sb[:, :, F:2 * F], wneigh.rearrange("(c p) f -> p c f", p=128)).then_inc(wsn_loaded, 16)

            def load_self(dram, n):
                sp.dma_start(selfb[:, :, :], dram[ds(n * BT, BT), :, :].rearrange("t p f -> p t f")
                             ).then_inc(self_loaded, 16)

            load_self(x_t, 0)

            def store_h(n, phase):
                for i in range(BT):
                    b = i % 2
                    sp.wait_ge(lo_ready, 5 * phase + i + 1)
                    T = n * BT + i
                    sp.dma_start(parts_dram[0][ds(T, 1), :, :].rearrange("o p n -> (o p) n"), part[b][:, :]
                                 ).then_inc(part_stored[b], 16)
                    sp.dma_start(h1_dram[ds(T, 1), :, :].rearrange("o p n -> (o p) n"), hb[b][:, :]
                                 ).then_inc(part_stored[b], 16)

            with sp.Fori(0, NB - 1) as n:
                store_h(n, n)
                sp.wait_ge(tp_done, BT * n + BT)
                load_self(x_t, n + 1)
            sp.wait_ge(agg_done, NB)
            sp.wait_ge(part_stored[0], 32 * 3 * (NB - 1))
            sp.wait_ge(part_stored[1], 32 * 2 * (NB - 1))

            def load_parts(l, c):
                sp.dma_start(xs[:, c * BT:(c + 1) * BT, :],
                             parts_dram[l][c * BT:(c + 1) * BT, :, :].rearrange("t p f -> p t f")
                             ).then_inc(xs_loaded[l][c], 16)

            for c in range(NB - 1):
                load_parts(0, c)
            sp.dma_start(xy[0][:, :, :], x_t[0:BT, :, :].rearrange("t p f -> p t f")).then_inc(xy_loaded[0], 16)
            sp.dma_start(xy[1][:, :, :], x_t[BT:2 * BT, :, :].rearrange("t p f -> p t f")).then_inc(xy_loaded[1], 16)
            sp.wait_ge(tp_done, BT * NB)
            load_self(h1_dram, 0)
            store_h(NB - 1, NB - 1)
            sp.wait_ge(part_stored[0], 32 * 3 * NB)
            sp.wait_ge(part_stored[1], 32 * 2 * NB)
            load_parts(0, NB - 1)
            sp.wait_ge(mm_done, BT * NB)
            sp.wait_ge(bank_read, BT * NB)
            sp.dma_start(wt_sb[:, :, :].rearrange("p c f -> p (c f)"), wt_dram[1]).then_inc(wts_loaded[1], 16)
            sp.dma_start(bias_sb[:, :], b1.rearrange("(o f) -> o f", o=1).broadcast_to([P, F])).then_inc(wts_loaded[1], 16)

            for kind, n in phases2:
                Q0 = BT * phase_of[kind, n]
                if kind == "B":
                    sp.wait_ge(tp_done, Q0 + BT)
                    if n + 1 < NB:
                        load_self(h1_dram, n + 1)
                    continue
                for i in range(BT):
                    b, T = i % 2, n * BT + i
                    sp.wait_ge(z_ready, T + 1)
                    sp.dma_start(z_dram[T], xy[n % 2][:, i, :]).then_inc(z_stored, 16)
                    sp.wait_ge(sp_lo, T + 1)
                    sp.dma_start(parts_dram[1][T], part[b][:, :]).then_inc(sp_stored[b], 16)
                if n + 2 < NB:
                    sp.wait_ge(z_stored, 16 * BT * (n + 1))
                    sp.wait_ge(tp_done, Q0 + BT)
                    sp.dma_start(xy[n % 2][:, :, :], x_t[(n + 2) * BT:(n + 3) * BT, :, :].rearrange("t p f -> p t f")
                                 ).then_inc(xy_loaded[n % 2], 16)
                if n >= NB - 2:
                    sp.wait_ge(agg_done, 2 * NB)
                    sp.wait_ge(sp_stored[0], 16 * 3 * (n + 1))
                    sp.wait_ge(sp_stored[1], 16 * 2 * (n + 1))
                    for c in (range(NB - 1) if n == NB - 2 else [NB - 1]):
                        load_parts(1, c)

            sp.wait_ge(z_stored, 16 * NT)

            def load_z(g, i):
                sp.dma_start(xy[0][:, i, :], z_dram[ds(g * BT + i, 1), :, :].rearrange("o p n -> (o p) n")
                             ).then_inc(z_loaded[i], 16)

            def store_out(g, i):
                sp.wait_ge(o_ready, g * BT + i + 1)
                sp.dma_start(out_t[ds(g * BT + i, 1), :, :].rearrange("o p n -> (o p) n"), xy[1][:, i, :]
                             ).then_inc(o_stored[i], 16)

            for i in range(BT):
                load_z(0, i)
            with sp.Fori(0, NB - 1) as g:
                for i in range(BT):
                    store_out(g, i)
                    load_z(g + 1, i)
            for i in range(BT):
                store_out(NB - 1, i)
            for i in range(BT):
                sp.wait_ge(o_stored[i], 16 * NB)
            sp.wait_ge(wt_stored, 16)

        @block.gpsimd
        def _(pool):
            nc.gpsimd.iota(iota16[:, :], [[1, KEY]], base=0, channel_multiplier=0,
                           allow_small_or_imprecise_dtypes=True).then_inc(const_ready, 1)
            nc.gpsimd.iota(woff[:, :], [[KEY, NW]], base=0, channel_multiplier=0,
                           allow_small_or_imprecise_dtypes=True).then_inc(const_ready, 1)
            nc.gpsimd.iota(inc_f[:, :], [[1, CH]], base=1, channel_multiplier=0,
                           allow_small_or_imprecise_dtypes=True).then_inc(const_ready, 1)
            nc.gpsimd.iota(rev_f[:, :], [[-1, CH]], base=CH, channel_multiplier=0,
                           allow_small_or_imprecise_dtypes=True).then_inc(const_ready, 1)
            nc.gpsimd.iota(wcol[:, :], [[0, 1]], base=0, channel_multiplier=1,
                           allow_small_or_imprecise_dtypes=True).then_inc(const_ready, 1)
            nc.gpsimd.memset(identf[:, :], 0.0).then_inc(pool_step, 1)
            nc.gpsimd.memset(ident16[:, :], 0.0).then_inc(pool_step, 1)
            nc.gpsimd.memset(sel8[:, :, :], 0.0).then_inc(pool_step, 1)
            for i in range(2):
                nc.gpsimd.memset(slab[i][:, N:SLAB], 0.0).then_inc(const_ready, 1)
            nc.gpsimd.iota(chunk_no[:, :], [[EG, EQ]], base=0, channel_multiplier=1,
                           allow_small_or_imprecise_dtypes=True).then_inc(const_ready, 1)
            nc.gpsimd.iota(slot_no[:, :, :], [[0, NW], [1, S]], base=0, channel_multiplier=0,
                           allow_small_or_imprecise_dtypes=True).then_inc(const_ready, 1)
            nc.gpsimd.memset(onesf[:, :], 1.0).then_inc(const_ready, 1)
            nc.gpsimd.memset(onesq[:, :], 1.0).then_inc(const_ready, 1)
            nc.gpsimd.memset(epsb[:, :], EPS).then_inc(const_ready, 1)
            nc.gpsimd.memset(key_t[:, CH:CH + G], -1.0).then_inc(const_ready, 1)
            nc.gpsimd.memset(srcp_t[:, CH:CH + G], 0.0).then_inc(const_ready, 1)
            nc.gpsimd.memset(stat[:, :], 0.0).then_inc(const_ready, 1)
            pool.wait_ge(pool_step, 3)
            nc.gpsimd.affine_select(out=sel8[:, :, :], in_=sel8[:, :, :], compare_op=ALU.not_equal, fill=1.0, base=0,
                                    pattern=[[1, DR], [-1, 8]], channel_multiplier=0).then_inc(const_ready, 1)
            for m, n in ((identf, 128), (ident16, P)):
                nc.gpsimd.affine_select(out=m[:, :], in_=m[:, :], compare_op=ALU.not_equal, fill=1.0, base=0,
                                        pattern=[[-1, n]], channel_multiplier=1).then_inc(const_ready, 1)
            pool.wait_ge(scale_ready, 1)
            with pool.Fori(0, NT) as t:
                step = 3 + 3 * t
                nc.gpsimd.tensor_tensor(xscaled[:, :], xs32[:, ds(t, 1), :].rearrange("p o f -> p (o f)"),
                                        scales[0:P, 0:1].broadcast_to([P, F]), ALU.mult).then_inc(pool_step, 1)
                nc.gpsimd.tensor_tensor(xparts[:, 0:F], xs32[:, ds(t, 1), :].rearrange("p o f -> p (o f)"),
                                        scales[0:P, 0:1].broadcast_to([P, F]), ALU.mult).then_inc(pool_step, 1)
                pool.wait_ge(pool_step, step + 2)
                nc.gpsimd.tensor_tensor(xparts[:, F:2 * F], xscaled[:, :], xparts[:, 0:F], ALU.subtract
                                        ).then_inc(pool_step, 1)
                pool.wait_ge(pool_step, step + 3)
                pool.sem_inc(x_parts, 1)
                nc.gpsimd.tensor_copy(xs[:, ds(t, 1), :].rearrange("p o f -> p (o f)"), xparts[:, :]
                                      ).then_inc(x_split, 1)
                pool.wait_ge(x_split, t + 1)
                pool.sem_inc(x_parts, 1)

        NCONST = 18

        @block.vector
        def _(dve):
            done = [0]

            def step(ins):
                done[0] += 1
                ins.then_inc(dve_step, 1)
                dve.wait_ge(dve_step, done[0])

            v = nc.vector
            for j, (s, size) in enumerate(((src_loaded, P), (dst_loaded, W))):
                dve.wait_ge(s, 16)
                step(v.tensor_copy(edges_f[:, j], edges_i[:, j]))
                step(v.tensor_scalar(hi_f[:, j], edges_f[:, j], 1.0 / size, 0.5 / size - 0.5, ALU.mult, ALU.add))
                step(v.tensor_scalar(hi_f[:, j], hi_f[:, j], ROUND, -ROUND, ALU.add, ALU.add))
            v.scalar_tensor_tensor(srcp[:, :, :], hi_f[:, 0], -float(P), edges_f[:, 0], ALU.mult, ALU.add
                                   ).then_inc(edge_keys, 1)
            step(v.scalar_tensor_tensor(key[:, :, :], hi_f[:, 1], float(KEY - W), edges_f[:, 1], ALU.mult, ALU.add))
            v.scalar_tensor_tensor(key[:, :, :], hi_f[:, 0], float(W), key[:, :, :], ALU.mult, ALU.add
                                   ).then_inc(edge_keys, 1)
            v.tensor_copy(gather_k[0][:, :, :], hi_f[:, 1]).then_inc(edge_keys, 1)
            step(v.scalar_tensor_tensor(jcol[:, :, :], hi_f[:, 1], -float(W), edges_f[:, 1], ALU.mult, ALU.add))
            step(v.scalar_tensor_tensor(jcol[:, :, :], hi_f[:, 0], float(W), jcol[:, :, :], ALU.mult, ALU.add))
            v.tensor_scalar(gather_k[1][:, :, :], jcol[:, :, :], 1.0, None, ALU.add).then_inc(edge_keys, 1)
            v.tensor_copy(gather_k[2][:, :, :], srcp[:, :, :]).then_inc(edge_keys, 1)
            step(v.tensor_reduce(wlim[:, 0, :], hi_f[:, 1], X, ALU.min))
            step(v.tensor_reduce(wlim[:, 1, :], hi_f[:, 1], X, ALU.max))
            dve.wait_ge(const_ready, NCONST)
            for j in range(2):
                for g in range(EQ):
                    last = v.tensor_scalar(wdiag[:, j, g, :], identf[0:EG, 0:EG], wlim[:, j, g:g + 1], None, ALU.mult)
            last.then_inc(diag_ready, 1)
            dve.wait_ge(keys_t, 1)
            v.tensor_copy(srcp_t[:, 0:CH], bank[0][0:P, 0:CH]).then_inc(dve_step, 1)
            done[0] += 1
            step(v.tensor_copy(key_t[:, 0:CH], bank[1][0:P, 0:CH]))
            dve.wait_ge(lims_b, 1)
            step(v.tensor_scalar(cover[:, :], bank[2][0:P, 0:CH], wcol[:, :], None, ALU.is_le))
            step(v.scalar_tensor_tensor(cover2[:, :], bank[3][0:P, 0:CH], wcol[:, :], cover[:, :], ALU.is_ge, ALU.mult))
            step(v.tensor_tensor(cover3[:, :], cover2[:, :], rev_f[:, :], ALU.mult))
            step(v.tensor_tensor(cover4[:, :], cover2[:, :], inc_f[:, :], ALU.mult))
            step(v.tensor_reduce(lim[:, 0:1], cover3[:, :], X, ALU.max))
            step(v.tensor_reduce(lim[:, 1:2], cover4[:, :], X, ALU.max))
            step(v.tensor_scalar(lim[:, 2:3], lim[:, 0:1], -1.0, float(CH), ALU.mult, ALU.add))
            v.tensor_scalar(fdiag[:, :], identf[0:P, 0:NW], lim[:, 2:3], None, ALU.mult).then_inc(fdiag_ready, 1)
            step(v.tensor_tensor(lim[:, 3:4], lim[:, 1:2], lim[:, 2:3], ALU.subtract))
            step(v.tensor_scalar(lim[:, 4:5], lim[:, 3:4], 1.0 / G, (G - 1.0) / G + 0.5 / G - 0.5, ALU.mult, ALU.add))
            step(v.tensor_scalar(lim[:, 5:6], lim[:, 4:5], ROUND, -ROUND, ALU.add, ALU.add))
            v.tensor_scalar(lim[:, 6:7], lim[:, 5:6], 1.0, None, ALU.max).then_inc(win_lims, 1)
            dve.wait_ge(rows_t, 1)
            step(v.memset(rows[:, :, :], 0.0))
            step(v.memset(rows[:, 3, :], 1.0))
            step(v.tensor_copy(rows[:, 0, 0:NW], bank[4][0:1, 0:NW]))
            step(v.tensor_copy(rows[:, 2, 0:NW], bank[4][0:1, 128:128 + NW]))
            step(v.tensor_reduce(rows[:, 4, 0:1], bank[4][0:1, 256:256 + NW], X, ALU.max))
            step(v.tensor_tensor_scan(rows[:, 1, 1:NW + 1], rows[:, 3, 0:NW], rows[:, 2, 0:NW], 0.0, ALU.mult, ALU.add))
            step(v.tensor_copy(table[:, 0:2, :], rows[:, 0:2, :]))
            v.tensor_copy(table[:, 2, 0:1], rows[:, 4, 0:1]).then_inc(table_ready, 1)

            dve.wait_ge(firsts_b, 1)
            step(v.tensor_copy(firsts[:, :], bank[5][0:EG, 0:NW]))
            step(v.tensor_tensor(want[:, :, :], slot_no[:, :, :],
                                 firsts[:, :].rearrange("p (w o) -> p w o", o=1).broadcast_to([EG, NW, S]), ALU.add))
            for g in range(EQ):
                last = v.tensor_scalar(pick[:, g, :, :], want[:, :, :], chunk_no[:, g:g + 1], None, ALU.is_equal)
            last.then_inc(first_rows, 1)
            dve.wait_ge(picked, 1)
            for h, (w0_, w1_) in enumerate(((0, SH), (SH, NW))):
                n = (w1_ - w0_) * S
                v.tensor_copy(jwin[:, w0_:w1_, :].rearrange("p w s -> p (w s)"), pick_bank[0][h][0:P, 0:n]
                              ).then_inc(dve_step, 1)
                v.tensor_copy(job_src[:, w0_:w1_, :].rearrange("p w s -> p (w s)"), pick_bank[2][h][0:P, 0:n]
                              ).then_inc(dve_step, 1)
                done[0] += 2
            dve.wait_ge(dve_step, done[0])
            for h, (w0_, w1_) in enumerate(((0, SH), (SH, NW))):
                n = (w1_ - w0_) * S
                step(v.scalar_tensor_tensor(job_key[:, w0_:w1_, :].rearrange("p w s -> p (w s)"),
                                            jwin[:, w0_:w1_, :].rearrange("p w s -> p (w s)"), float(KEY),
                                            pick_bank[1][h][0:P, 0:n], ALU.mult, ALU.add))
            v.scalar_tensor_tensor(job_key[:, :, :], job_key[:, :, :], -1.0,
                                   woff[:, :].rearrange("p (w o) -> p w o", o=1).broadcast_to([P, NW, S]),
                                   ALU.add, ALU.subtract).then_inc(job_table, 1)

            dve.wait_ge(x_loaded, 16)
            v.tensor_reduce(stat[0:P, 0:1], xs32[:, :, :].rearrange("p t f -> p (t f)"), X, ALU.max,
                            apply_absolute_value=True).then_inc(stat_ready, 1)
            dve.wait_ge(b_loaded, 16)
            v.tensor_reduce(stat[:, 3:5], bcol[:, :].rearrange("p (h o) -> p h o", o=1), X, ALU.max,
                            apply_absolute_value=True).then_inc(stat_ready, 1)
            dve.wait_ge(wn_loaded, 16)
            v.tensor_reduce(stat[:, 5:7], wn_nat[:, :, :], X, ALU.max, apply_absolute_value=True
                            ).then_inc(stat_ready, 1)
            dve.wait_ge(stat_psum, 1)
            step(v.tensor_reduce(stat_r[:, 0:1], bank[5][0:8, 0:128], X, ALU.max))
            v.tensor_reduce(stat_r[:, 1:2], bank[5][0:8, 0:128], X, ALU.add).then_inc(stat_red, 1)
            dve.wait_ge(stat_row, 1)
            step(v.tensor_copy(sv[:, :, :], bank[6][0:1, 0:16].rearrange("p (a b) -> p a b", a=2)))
            step(v.tensor_tensor(sw[:, 0:1], sv[:, 0, 1:2], sv[:, 0, 2:3], ALU.max))
            step(v.tensor_tensor(sw[:, 1:2], sv[:, 0, 3:4], sv[:, 0, 4:5], ALU.max))
            step(v.tensor_copy(sw[:, 4:5], sv[:, 0, 0:1]))
            step(v.tensor_tensor(sw[:, 2:3], sw[:, 4:5], sw[:, 0:1], ALU.mult))
            step(v.tensor_tensor(sw[:, 5:6], sw[:, 2:3], sw[:, 1:2], ALU.add))
            step(v.tensor_tensor(sw[:, 3:4], sv[:, 1, 5:6], sv[:, 1, 6:7], ALU.add))
            step(v.tensor_scalar(sw[:, 6:7], sw[:, 3:4], 1.01 * F ** 0.5, None, ALU.mult))
            step(v.tensor_scalar(sw[:, 8:11], sw[:, 4:7], 1e-20, None, ALU.max))
            step(v.tensor_scalar(svi[:, 0:3], sw[:, 8:11].bitcast(I32), 0x7F800000, None, ALU.bitwise_and))
            step(v.tensor_scalar(sbits[:, 0:3], svi[:, 0:3], -1.0, float(268 << 23), ALU.mult, ALU.add))
            step(v.tensor_copy(srow[:, 0:3], sbits[:, 0:3].bitcast(F32)))
            v.tensor_scalar(srow[:, 3:6], svi[:, 0:3].bitcast(F32), 2.0 ** -14, None, ALU.mult).then_inc(scale_row, 1)
            dve.wait_ge(scale_psum, 1)
            v.tensor_copy(scales[:, :], bank[7][:, 0:6]).then_inc(scale_ready, 1)

            dve.wait_ge(table_ready, 1)
            dve.wait_ge(job_table, 1)

            def quick_hots(w, b):
                dve.wait_ge(win_done, w + 1)
                v.tensor_tensor(src_hot2[b][:, :, :],
                                iota16[:, 0:128].rearrange("p (o a) -> p o a", o=1).broadcast_to([P, S, 128]),
                                job_src[:, ds(w, 1), :].rearrange("p w (s o) -> p (w s) o", o=1).broadcast_to([P, S, 128]),
                                ALU.is_equal)
                for s in range(S):
                    last = v.tensor_scalar(key_hot2[b][:, s, :], iota16[:, :],
                                           job_key[:, ds(w, 1), s:s + 1].rearrange("p w s -> p (w s)"), None, ALU.is_equal)
                last.then_inc(win_hot, 1)

            most = dve.value_load(table[0:1, 2, 0:1], min_val=0, max_val=CH)
            quick = dve.If(most < S + 1)
            with quick:
                with dve.Fori(0, NW // 4) as m:
                    for j in range(4):
                        quick_hots(m * 4 + j, j % 2)
                quick_hots(NW - 1, 0)
            slow = dve.If(most > S)
            with slow, dve.Fori(0, NW) as w:
                first = dve.value_load(table[0:1, 0, ds(w, 1)], min_val=0, max_val=CH)
                g0 = dve.value_load(table[0:1, 1, ds(w, 1)], min_val=0, max_val=NW * CH)
                g1 = dve.value_load(table[0:1, 1, ds(w + 1, 1)], min_val=0, max_val=NW * CH)
                off = woff[:, ds(w, 1)]
                with dve.Fori(g0, g1) as j:
                    chunk = nc.s_assert_within((j - g0) * G + first, 0, CH,
                                               skip_runtime_bounds_check_because="groups cover whole chunks up to the padding")
                    for k in range(G):
                        dve.wait_ge(jobs_done, j * G + k + 1)
                        v.tensor_scalar(src_hot[k][:, 0:P], iota16[:, 0:P], srcp_t[:, ds(chunk + k, 1)], None,
                                        ALU.is_equal)
                        v.tensor_scalar(key_hot[k][:, :], iota16[:, :], off, key_t[:, ds(chunk + k, 1)], ALU.add,
                                        ALU.is_equal).then_inc(hot_ready, 1)

            dve.wait_ge(tr_free, 4 * NT + 2)
            step(v.tensor_reduce(rdeg_dst[:, :], deg_part[:, :, :], X, ALU.add))
            step(v.tensor_scalar(rdeg_dst[:, :], rdeg_dst[:, :], 1.0, None, ALU.max))
            step(v.reciprocal(rdeg_dst[:, :], rdeg_dst[:, :]))
            step(v.tensor_scalar(rdeg_dst[:, :], rdeg_dst[:, :], scales[0:P, 5:6], None, ALU.mult))
            dve.wait_ge(deg_summed, 1)
            dve.wait_ge(slab_stored[0], 16 * 13)
            dve.wait_ge(slab_stored[1], 16 * 12)
            dve.wait_ge(x_split, NT)
            v.tensor_copy(deg_rows, bank[7][0:8, 0:DQ * P]).then_inc(deg_copied, 1)
            dve.wait_ge(deg_done, 1)
            step(v.tensor_scalar(rdeg_src[:, :].rearrange("p (j q) -> p j q", q=DQ),
                                 bank[7][0:P, 0:DQ * 8].rearrange("p (q j) -> p j q", j=8)[:, 0:DR, :], 1.0, None, ALU.max))
            step(v.reciprocal(rdeg_src[:, :], rdeg_src[:, :]))

            def affine(T, Q, i, base):
                ps = dense[i % 2]
                dve.wait_ge(mm_done, Q + 1)
                v.scalar_tensor_tensor(t1[:, :], ps[0:P, 0:F], 1.0, bias_sb[:, :], ALU.mult, ALU.add
                                       ).then_inc(dve_step, 1)
                dve.wait_ge(dve_step, base + 1)
                v.scalar_tensor_tensor(t2[i % 2][:, :], ps[0:P, F:2 * F], rdeg_src[:, ds(T, 1)], t1[:, :],
                                       ALU.mult, ALU.add).then_inc(bank_read, 1)
                dve.wait_ge(bank_read, Q + 1)

            def low_part1(Q, i):
                dve.wait_ge(relu_ready, Q + 1)
                v.scalar_tensor_tensor(part[i % 2][:, F:2 * F], hb[i % 2][:, :], scales[0:P, 1:2],
                                       part[i % 2][:, 0:F], ALU.mult, ALU.subtract).then_inc(lo_ready, 1)

            dve.wait_ge(wts_loaded[0], 32)
            base0 = done[0]
            with dve.Fori(0, NB) as n:
                for i in range(BT):
                    Q = n * BT + i
                    affine(Q, Q, i, base0 + Q)
                    if i:
                        low_part1(Q - 1, i - 1)
                low_part1(n * BT + BT - 1, BT - 1)
            done[0] = base0 + NT

            dve.wait_ge(wts_loaded[1], 32)
            dve.wait_ge(part_stored[0], 32 * 3 * NB)
            dve.wait_ge(part_stored[1], 32 * 2 * NB)

            def norm_tail(n, i):
                T, b = n * BT + i, i % 2
                dve.wait_ge(sd_ready, T + 1)
                step(v.reciprocal(sd[b][:, 1:2], sd[b][:, 0:1]))
                v.tensor_scalar(xy[n % 2][:, i, :], hb[b][:, :], mv[b][:, 0:1], sd[b][:, 1:2], ALU.subtract, ALU.mult
                                ).then_inc(y_ready, 1)

            def phase_b(n):
                Q0 = BT * phase_of["B", n]
                dve.wait_ge(xy_loaded[n % 2], 16 * (n // 2 + 1))
                for i in range(BT):
                    T, b = n * BT + i, i % 2
                    affine(T, Q0 + i, i, done[0])
                    done[0] += 1
                    step(v.scalar_tensor_tensor(hb[b][:, :], t2[b][:, :], 0.0, xy[n % 2][:, i, :], ALU.max, ALU.add))
                    step(v.bn_stats(st6[b][:, :], hb[b][:, :]))
                    v.bn_aggr(mv[b][:, :], st6[b][:, :]).then_inc(var_ready, 1)
                    if i:
                        norm_tail(n, i - 1)
                norm_tail(n, BT - 1)

            def low_part2(n, i):
                T, b = n * BT + i, i % 2
                dve.wait_ge(sphi_ready, T + 1)
                v.scalar_tensor_tensor(part[b][:, F:2 * F], sparse[b][:, :], scales[0:P, 2:3], part[b][:, 0:F],
                                       ALU.mult, ALU.subtract).then_inc(sp_lo, 1)

            def phase_c(n):
                Q0 = BT * phase_of["C", n]
                for i in range(BT):
                    T, b = n * BT + i, i % 2
                    dve.wait_ge(hn_copied, T + 1)
                    v.scalar_tensor_tensor(xy[n % 2][:, i, :], dense[b][0:P, 0:F], 1.0, xy[n % 2][:, i, :], ALU.mult, ALU.add
                                           ).then_inc(z_ready, 1)
                    dve.wait_ge(z_ready, T + 1)
                    dve.sem_inc(bank_read, 1)
                    cur = hb[b]
                    for r in range(MAXK // 8):
                        step(v.max(m8[:, :], cur[:, :]))
                        step(v.match_replace(work[:, :], m8[:, :], cur[:, :], NEG))
                        cur = work
                    v.scalar_tensor_tensor(sparse[b][:, :], work[:, :], NEG, hb[b][:, :], ALU.is_equal, ALU.mult
                                           ).then_inc(sparse_ready, 1)
                    if i:
                        low_part2(n, i - 1)
                low_part2(n, BT - 1)

            for kind, n in phases2:
                (phase_b if kind == "B" else phase_c)(n)

            base3 = done[0]
            dve.sem_inc(n3_read, BT)
            with dve.Fori(0, NB) as g:
                for i in range(BT):
                    T = g * BT + i
                    base = base3 + T * 4
                    dve.wait_ge(n3_done, T + 1)
                    dve.wait_ge(z_loaded[i], g * 16 + 16)
                    ps, zt = bank[i], xy[0][:, i, :]
                    v.scalar_tensor_tensor(zt, ps[0:P, 0:F], rdeg_dst[:, ds(T, 1)], zt, ALU.mult, ALU.add
                                           ).then_inc(dve_step, 1)
                    dve.wait_ge(dve_step, base + 1)
                    v.scalar_tensor_tensor(zt, ps[0:P, F:2 * F], rdeg_dst[:, ds(T, 1)], zt, ALU.mult, ALU.add
                                           ).then_inc(dve_step, 1)
                    dve.wait_ge(dve_step, base + 2)
                    v.bn_stats(st6[i % 2][:, :], zt).then_inc(dve_step, 1)
                    dve.wait_ge(dve_step, base + 3)
                    dve.sem_inc(stats3, 1)
                    v.bn_aggr(mv[i % 2][:, :], st6[i % 2][:, :]).then_inc(var3, 1)
                    dve.wait_ge(sd3, T + 1)
                    v.reciprocal(sd[i % 2][:, 1:2], sd[i % 2][:, 0:1]).then_inc(dve_step, 1)
                    dve.wait_ge(dve_step, base + 4)
                    dve.wait_ge(o_stored[i], g * 16)
                    v.tensor_scalar(xy[1][:, i, :], zt, mv[i % 2][:, 0:1], sd[i % 2][:, 1:2],
                                    ALU.subtract, ALU.mult).then_inc(o_ready, 1)
                    dve.wait_ge(o_ready, T + 1)
                    dve.sem_inc(n3_read, 1)

        @block.scalar
        def _(act):
            a = nc.scalar
            act.wait_ge(w_loaded, 32)
            act.wait_ge(const_ready, NCONST)
            for h in range(2):
                a.activation(junk[:, :], w_nat[:, 0, h, :], ACT.Abs, accum_out=stat[:, 1 + h:2 + h]
                             ).then_inc(act_step, 1)
                act.wait_ge(act_step, h + 1)
            act.sem_inc(act_sums, 1)
            for l in range(2):
                for h in range(2):
                    act.wait_ge(wt_psum, 2 * l + h + 1)
                    b = bank[6 + h]
                    a.activation(w_t[:, l, :, h * 128:(h + 1) * 128],
                                 b[:, :].rearrange("p (c o) -> p c o", c=4), ACT.Copy).then_inc(wt_copied, 1)
            act.sem_inc(win_free, 2)
            act.sem_inc(tr_free, 2)
            act.wait_ge(table_ready, 1)
            act.wait_ge(wt_stored, 16)
            act.wait_ge(scale_ready, 1)

            def win_copy(t, par, u, quick):
                w = t * WT + u
                if quick:
                    act.wait_ge(win_done, w + 3)
                else:
                    g1 = act.value_load(table[0:1, 1, ds(w + 1, 1)], min_val=0, max_val=NW * CH)
                    act.wait_ge(jobs_done, g1 * G + G)
                if u == 0:
                    act.wait_ge(slab_stored[par], t * 8 if par == 0 else (t - 1) * 8)
                q = (par + u) % 2
                out0 = slab3[par][:, 0:B0W, u * W:(u + 1) * W]
                out1 = slab3[par][:, B0W:NT, u * W:(u + 1) * W]
                a.activation(out0, bank[2 * q][0:P, 0:B0W * W].rearrange("p (b d) -> p b d", d=W), ACT.Copy)
                a.activation(out1, bank[2 * q + 1][0:P, 0:(NT - B0W) * W].rearrange("p (b d) -> p b d", d=W),
                             ACT.Copy).then_inc(win_free, 1)

            def tr_copy(t):
                for g in range(4):
                    act.wait_ge(tr_done, 4 * t + g + 1)
                    a.activation(ct[:, ds(t, 1), TG0[g] * P:(TG0[g] + TG[g]) * P].rearrange("p o (b s) -> p (o b) s", s=P),
                                 tr16[g % 2][0:P, 0:TG[g], 0:P], ACT.Copy,
                                 accum_out=deg_part[:, ds(t, 1), g:g + 1].rearrange("p o g -> p (o g)")
                                 ).then_inc(tr_free, 1)

            def copies(quick):
                for u in range(WT):
                    win_copy(0, 0, u, quick)
                with act.Fori(0, NT // 2) as m:
                    t = m * 2 + 1
                    for par, tt in ((1, t), (0, t + 1)):
                        win_copy(tt, par, 0, quick)
                        tr_copy(tt - 1)
                        for u in range(1, WT):
                            win_copy(tt, par, u, quick)

            most = act.value_load(table[0:1, 2, 0:1], min_val=0, max_val=CH)
            with act.If(most < S + 1):
                copies(True)
            with act.If(most > S):
                copies(False)
            tr_copy(NT - 1)

            act.wait_ge(tr_done, 4 * NT)
            act.wait_ge(slab_stored[0], 16 * 13)
            act.wait_ge(slab_stored[1], 16 * 12)
            act.wait_ge(x_split, NT)

            def agg_copy(k, n, par, l):
                act.wait_ge(agg_done, k + 1)
                for f in range(2):
                    for h, (lo, wd) in enumerate(((0, H0), (H0, H1))):
                        last = a.activation(nt_sb[par][:, f, lo:lo + wd], agg[f][h][:, 0:wd], ACT.Copy,
                                            scale=scales[:, 3 + l:4 + l])
                last.then_inc(agg_copied, 1)

            def tr_out(Q, i):
                act.wait_ge(tp_done, Q + 1)
                act.wait_ge(mm_done, free_at(Q, i))
                a.activation(tr_sb[i % 2][:, :, :], tp, ACT.Copy).then_inc(tp_copied, 1)

            def b1(n, Q0):
                tr_out(Q0, 0)
                for i in range(BT):
                    if i + 1 < BT:
                        tr_out(Q0 + i + 1, i + 1)
                    b = i % 2
                    act.wait_ge(bank_read, Q0 + i + 1)
                    act.wait_ge(part_stored[b], (n * uses(i) + c0(i)) * 32)
                    a.activation(hb[b][:, :], t2[b][:, :], ACT.Relu)
                    a.activation(part[b][:, 0:F], t2[b][:, :], ACT.Relu, scale=scales[0:P, 1:2]
                                 ).then_inc(relu_ready, 1)

            agg_copy(0, 0, 0, 0)
            with act.Fori(0, NB // 2) as m:
                n = m * 2 + 1
                agg_copy(n, n, 1, 0)
                b1(n - 1, (n - 1) * BT)
                agg_copy(n + 1, n + 1, 0, 0)
                b1(n, n * BT)
            b1(NB - 1, (NB - 1) * BT)

            def phase_b(n):
                Q0 = BT * phase_of["B", n]
                tr_out(Q0, 0)
                for i in range(BT):
                    if i + 1 < BT:
                        tr_out(Q0 + i + 1, i + 1)
                    b, T = i % 2, n * BT + i
                    act.wait_ge(var_ready, T + 1)
                    a.activation(sd[b][:, 0:1], mv[b][:, 1:2], ACT.Sqrt, bias=epsb[:, :]).then_inc(sd_ready, 1)

            def phase_c(n):
                Q0 = BT * phase_of["C", n]
                tr_out(Q0, 0)

                def high(i):
                    b, T = i % 2, n * BT + i
                    act.wait_ge(sparse_ready, T + 1)
                    act.wait_ge(sp_stored[b], 16 * (uses(i) * n + c0(i)))
                    a.activation(part[b][:, 0:F], sparse[b][:, :], ACT.Copy, scale=scales[0:P, 2:3]
                                 ).then_inc(sphi_ready, 1)

                for i in range(BT):
                    if i + 1 < BT:
                        tr_out(Q0 + i + 1, i + 1)
                    b, T = i % 2, n * BT + i
                    act.wait_ge(mm_done, Q0 + i + 1)
                    if i == 0:
                        act.wait_ge(y_ready, (n + 1) * BT)
                    if i >= 2:
                        act.wait_ge(sparse_ready, T - 1)
                    a.activation(hb[b][:, :], dense[b][0:P, F:2 * F], ACT.Copy).then_inc(hn_copied, 1)
                    if i:
                        high(i - 1)
                high(BT - 1)

            act.wait_ge(part_stored[0], 32 * 3 * NB)
            act.wait_ge(part_stored[1], 32 * 2 * NB)
            agg_copy(NB, 0, 1, 1)
            agg_copy(NB + 1, 1, 0, 1)
            phase_b(0)
            for k in range(2, NB):
                agg_copy(NB + k, k, (k + 1) % 2, 1)
                if k == NB - 1:
                    for c in range(NB):
                        act.dma_start(ct[:, c * BT:(c + 1) * BT, :],
                                      c_dram[c * BT:(c + 1) * BT, :, :].rearrange("t p n -> p t n")
                                      ).then_inc(c_loaded[c // 3], 16)
                phase_c(k - 2)
                phase_b(k - 1)
            phase_c(NB - 2)
            phase_b(NB - 1)
            phase_c(NB - 1)

            with act.Fori(0, NB) as g:
                for i in range(BT):
                    act.wait_ge(var3, g * BT + i + 1)
                    a.activation(sd[i % 2][:, 0:1], mv[i % 2][:, 1:2], ACT.Sqrt, bias=epsb[:, :]).then_inc(sd3, 1)

        @block.tensor
        def _(pe):
            mm = nc.tensor.matmul
            pe.wait_ge(const_ready, NCONST)
            for j, (m, b) in enumerate(((srcp, bank[0]), (key, bank[1]))):
                pe.wait_ge(edge_keys, j + 1)
                for g in range(EQ):
                    last = nc.tensor.transpose(b[0:P, g * EG:(g + 1) * EG], m[:, g, :], identf[0:EG, 0:EG])
            last.then_inc(keys_t, 1)
            pe.wait_ge(diag_ready, 1)
            for j in range(2):
                for g in range(EQ):
                    last = mm(bank[2 + j][0:P, g * EG:(g + 1) * EG], onesq[0:EG, :], wdiag[:, j, g, :],
                              start=True, stop=True)
            last.then_inc(lims_b, 1)
            pe.wait_ge(w_loaded, 32)
            for l in range(2):
                for h in range(2):
                    if l:
                        pe.wait_ge(wt_copied, h + 1)
                    for c in range(4):
                        last = nc.tensor.transpose(bank[6 + h][:, c * 128:(c + 1) * 128],
                                                   w_nat[:, l, h, c * 128:(c + 1) * 128], identf[:, :])
                    last.then_inc(wt_psum, 1)
            pe.wait_ge(fdiag_ready, 1)
            mm(bank[5][0:EG, 0:NW], onesq[:, 0:EG], fdiag[:, :], start=True, stop=True).then_inc(firsts_b, 1)
            pe.wait_ge(win_lims, 1)
            mm(bank[4][0:1, 0:P], lim[:, 2:3], identf[0:P, 0:P], start=True, stop=True)
            mm(bank[4][0:1, 128:128 + P], lim[:, 6:7], identf[0:P, 0:P], start=True, stop=True)
            mm(bank[4][0:1, 256:256 + P], lim[:, 3:4], identf[0:P, 0:P], start=True, stop=True).then_inc(rows_t, 1)
            pe.wait_ge(first_rows, 1)
            pe.wait_ge(edge_keys, 5)
            for i in range(3):
                for h, (w0_, w1_) in enumerate(((0, SH), (SH, NW))):
                    for g in range(EQ):
                        last = mm(pick_bank[i][h][0:P, 0:(w1_ - w0_) * S], gather_k[i][:, g, :],
                                  pick[:, g, w0_:w1_, :].rearrange("p w s -> p (w s)"), start=g == 0, stop=g == EQ - 1)
            last.then_inc(picked, 1)
            pe.wait_ge(job_table, 1)
            pe.wait_ge(stat_ready, 3)
            pe.wait_ge(act_sums, 1)
            nc.tensor.transpose(bank[5][0:8, 0:128], stat[:, :], identf[:, :]).then_inc(stat_psum, 1)
            pe.wait_ge(stat_red, 1)
            pe.wait_ge(wt_copied, 4)
            mm(bank[6][0:1, 0:8], stat_r[:, 0:1], identf[0:8, 0:8], start=True, stop=True)
            mm(bank[6][0:1, 8:16], stat_r[:, 1:2], identf[0:8, 0:8], start=True, stop=True).then_inc(stat_row, 1)
            pe.wait_ge(scale_row, 1)
            mm(bank[7][:, 0:6], onesf[:, :], srow[:, :], start=True, stop=True).then_inc(scale_psum, 1)
            pe.wait_ge(table_ready, 1)
            pe.sem_inc(jobs_done, G)
            pe.sem_inc(win_done, 2)

            def job(q, k, start, stop):
                pe_kw = dict(start=start, stop=stop, skip_group_check=True)
                mm(bank[2 * q][0:P, 0:B0W * W], src_hot[k][:, 0:P], key_hot[k][:, 0:B0W * W], **pe_kw)
                mm(bank[2 * q + 1][0:P, 0:(NT - B0W) * W], src_hot[k][:, 0:P], key_hot[k][:, B0W * W:KEY], **pe_kw
                   ).then_inc(jobs_done, 1)

            def quick_window(t, par, u):
                w = t * WT + u
                q = b = (par + u) % 2
                pe.wait_ge(win_hot, w + 1)
                pe.wait_ge(win_free, w + 1)
                for s in range(S):
                    kw = dict(start=s == 0, stop=s == S - 1, skip_group_check=True)
                    mm(bank[2 * q][:, 0:B0W * W], src_hot2[b][:, s, :], key_hot2[b][:, s, 0:B0W * W], **kw)
                    last = mm(bank[2 * q + 1][:, 0:(NT - B0W) * W], src_hot2[b][:, s, :],
                              key_hot2[b][:, s, B0W * W:KEY], **kw)
                last.then_inc(win_done, 1)

            def window(t, par, u):
                w = t * WT + u
                q = (par + u) % 2
                g0 = pe.value_load(table[0:1, 1, ds(w, 1)], min_val=0, max_val=NW * CH)
                g1 = pe.value_load(table[0:1, 1, ds(w + 1, 1)], min_val=0, max_val=NW * CH)
                pe.wait_ge(win_free, w + 1)
                for k in range(G):
                    pe.wait_ge(hot_ready, g0 * G + k + 1)
                    job(q, k, k == 0, False)
                with pe.If(g0 + 1 < g1):
                    with pe.Fori(g0 + 1, g1) as j:
                        for k in range(G):
                            pe.wait_ge(hot_ready, j * G + k + 1)
                            job(q, k, False, False)

            def transposes(t, par):
                pe.wait_ge(win_free, WT * t + WT + 2)
                for g in range(4):
                    pe.wait_ge(tr_free, 4 * t + g + 1)
                    for i in range(TG[g]):
                        last = nc.tensor.transpose(tr16[g % 2][:, i, 0:P],
                                                   slab[par][:, (TG0[g] + i) * P:(TG0[g] + i) * P + 128], ident16[:, :])
                    last.then_inc(tr_done, 1)

            def windows(one_window):
                for u in range(WT):
                    one_window(0, 0, u)
                with pe.Fori(0, NT // 2) as m:
                    t = m * 2 + 1
                    for par, tt in ((1, t), (0, t + 1)):
                        one_window(tt, par, 0)
                        transposes(tt - 1, 1 - par)
                        for u in range(1, WT):
                            one_window(tt, par, u)

            most = pe.value_load(table[0:1, 2, 0:1], min_val=0, max_val=CH)
            with pe.If(most < S + 1):
                windows(quick_window)
            with pe.If(most > S):
                windows(window)
            transposes(NT - 1, 0)

            pe.wait_ge(tr_free, 4 * NT + 2)
            pe.wait_ge(scale_ready, 1)

            def degree_sums(t, first, end):
                for j in range(DR):
                    wd = min(DQ, NT - DQ * j) * P
                    rhs = ct[:, ds(t, 1), j * DQ * P:j * DQ * P + wd].rearrange("p o f -> p (o f)")
                    last = mm(bank[7][0:8, 0:wd], sel8[:, j, :], rhs, start=first and j == 0, stop=end and j == DR - 1,
                              skip_group_check=True)
                return last

            degree_sums(0, True, False)
            with pe.Fori(1, NT - 1) as t:
                degree_sums(t, False, False)
            degree_sums(NT - 1, False, True).then_inc(deg_summed, 1)

            pe.wait_ge(x_split, NT)

            def aggregate(k, n, parts=None):
                pe.wait_ge(agg_copied, k)

                def one(t, start, stop):
                    for h, (lo, wd) in enumerate(((0, H0), (H0, H1))):
                        for f in range(2):
                            for p in range(2):
                                if isinstance(t, int):
                                    lhs = xs[:, t, p * F + f * 128:p * F + f * 128 + 128]
                                    rhs = ct[:, t, ds(n * BT * P + lo, wd)]
                                else:
                                    lhs = xs[:, ds(t, 1), p * F + f * 128:p * F + f * 128 + 128].rearrange("p o f -> p (o f)")
                                    rhs = ct[:, ds(t, 1), ds(n * BT * P + lo, wd)].rearrange("p o f -> p (o f)")
                                last = mm(agg[f][h][:, 0:wd], lhs, rhs, start=start and p == 0, stop=stop and p == 1,
                                          skip_group_check=True)
                    return last

                if parts is None:
                    one(0, True, False)
                    with pe.Fori(1, NT - 1) as t:
                        one(t, False, False)
                else:
                    for c in range(NB):
                        pe.wait_ge(parts[c], 16)
                        if c == 0:
                            one(0, True, False)
                        with pe.Fori(max(1, c * BT), min(NT - 1, (c + 1) * BT)) as t:
                            one(t, False, False)
                one(NT - 1, False, True).then_inc(agg_done, 1)

            def transpose_tile(Q, tile):
                pe.wait_ge(tp_copied, Q)
                for c in range(2):
                    last = nc.tensor.transpose(tp[:, c, :], tile[:, c * 128:(c + 1) * 128], identf[0:P, 0:P])
                last.then_inc(tp_done, 1)

            def products(n, Q0, nt, selfs):
                pe.wait_ge(self_loaded, selfs * 16)
                transpose_tile(Q0, selfb[:, 0, :])
                for i in range(BT):
                    if i + 1 < BT:
                        transpose_tile(Q0 + i + 1, selfb[:, i + 1, :])
                    pe.wait_ge(tp_copied, Q0 + i + 1)
                    pe.wait_ge(bank_read, free_at(Q0 + i, i))
                    ps = dense[i % 2]
                    for c in range(2):
                        mm(ps[0:P, 0:F], tr_sb[i % 2][:, c, :], wt_sb[:, c, :], start=c == 0, stop=c == 1,
                           skip_group_check=True)
                    for c in range(2):
                        last = mm(ps[0:P, F:2 * F], nt[:, c, i * P:(i + 1) * P], wt_sb[:, 2 + c, :],
                                  start=c == 0, stop=c == 1, skip_group_check=True)
                    last.then_inc(mm_done, 1)

            aggregate(0, 0)
            pe.wait_ge(deg_copied, 1)
            for g in range(DQ):
                last = nc.tensor.transpose(bank[7][0:P, g * 8:(g + 1) * 8], deg_rows[:, g * P:(g + 1) * P],
                                           identf[0:8, 0:8])
            last.then_inc(deg_done, 1)
            pe.wait_ge(wts_loaded[0], 32)
            with pe.Fori(0, NB // 2) as m:
                n = m * 2 + 1
                aggregate(n, n)
                products(n - 1, (n - 1) * BT, nt_sb[0], n)
                aggregate(n + 1, n + 1)
                products(n, n * BT, nt_sb[1], n + 1)
            pe.wait_ge(agg_copied, NB)
            products(NB - 1, (NB - 1) * BT, nt_sb[0], NB)

            def products2(n):
                products(n, BT * phase_of["B", n], nt_sb[(n + 1) % 2], NB + n + 1)

            def sparse_products(n):
                Q0 = BT * phase_of["C", n]
                pe.wait_ge(y_ready, n * BT + 1)
                transpose_tile(Q0, xy[n % 2][:, 0, :])
                for i in range(BT):
                    if i + 1 < BT:
                        pe.wait_ge(y_ready, n * BT + i + 2)
                        transpose_tile(Q0 + i + 1, xy[n % 2][:, i + 1, :])
                    pe.wait_ge(tp_copied, Q0 + i + 1)
                    pe.wait_ge(bank_read, free_at(Q0 + i, i))
                    for c in range(2):
                        last = mm(dense[i % 2][0:P, :], tr_sb[i % 2][:, c, :], wsn_sb[:, c, :], start=c == 0, stop=c == 1)
                    last.then_inc(mm_done, 1)

            aggregate(NB, 0, xs_loaded[0])
            aggregate(NB + 1, 1)
            pe.wait_ge(wts_loaded[1], 32)
            products2(0)
            pe.wait_ge(wsn_loaded, 32)
            for k in range(2, NB):
                aggregate(NB + k, k)
                sparse_products(k - 2)
                products2(k - 1)
            sparse_products(NB - 2)
            pe.wait_ge(agg_copied, 2 * NB)
            products2(NB - 1)
            sparse_products(NB - 1)

            pe.wait_ge(bank_read, BT * (NB + len(phases2)))
            for c in range(NB):
                pe.wait_ge(xs_loaded[1][c], 16)
            for g0, g1, s, cnt in ((0, 3, c_loaded[0], 48), (3, NB, c_loaded[1], 32)):
                pe.wait_ge(s, cnt)
                with pe.Fori(g0, g1) as g:
                    for i in range(BT):
                        T = g * BT + i
                        pe.wait_ge(n3_read, T + 1)
                        for b in range(NT):
                            last = mm(bank[i][0:P, :], ct[:, ds(T, 1), b * P:(b + 1) * P].rearrange("p o d -> p (o d)"),
                                      xs[:, b, :], start=b == 0, stop=b == NT - 1)
                        last.then_inc(n3_done, 1)


_INS = ["x", "src", "dst", "L0_gnn_W0", "L0_gnn_b0", "L0_gnn_W1", "L0_gnn_b1", "L1_gnn_W_self", "L1_gnn_W_neigh"]


def kernel(**inputs):
    import numpy as _np
    import concourse.bacc as _bacc
    from concourse import mybir as _mybir
    from concourse.bass_utils import run_bass_kernel_spmd as _run

    nc = _bacc.Bacc("TRN2", target_bir_lowering=False, num_devices=1, dynamic_dma_scratch_size=1024)
    arrays, args = {}, []
    for name in _INS:
        a = _np.ascontiguousarray(inputs[name])
        arrays[f"in_{name}_dram"] = a
        args.append(nc.dram_tensor(f"in_{name}_dram", a.shape, _mybir.dt.from_np(a.dtype), kind="ExternalInput").ap())
    out = nc.dram_tensor("out_dram", (N, F), _mybir.dt.float32, kind="ExternalOutput").ap()
    gnn(nc, *args, out)
    r = _run(nc, [arrays], core_ids=[0])
    return r.results[0]["out_dram"]
```

```python
from contextlib import ExitStack

import concourse.bass as bass
from concourse import mybir

N, E, F = 3125, 50000, 256
P = 125
NT = N // P
CH = E // P
SLAB = N + 3
G = 4
W = 25
WT = P // W
NW = N // W
S = 4
J = S + 1
XC = [0, 9, 17, 25]
SHIFTS = [64, 32, 16]
PACK = 128
KEY = NT * W
B0W = 13
EQ, EG = 4, CH // 4
YS = 2.0 ** 10
NSC = 7
NST = 10
BT = 5
NB = NT // BT
H0, H1 = 313, 312
MAXK = 32
EPS = 1e-5
NEG = -3.0e38
ROUND = 12582912.0
TG = [8, 4, 8, 5]
TG0 = [0, 8, 12, 20]

F32, F16, I32 = mybir.dt.float32, mybir.dt.float16, mybir.dt.int32
ALU = mybir.AluOpType
ACT = mybir.ActivationFunctionType
X = mybir.AxisListType.X
ds = bass.ds


def gnn(nc, x, src, dst, w0, b0, w1, b1, wself, wneigh, out):
    ctx = ExitStack()
    with ctx:
        sem_names = set()

        def sem(name):
            assert name not in sem_names
            sem_names.add(name)
            return ctx.enter_context(nc.semaphore(name))

        class Arena:

            def __init__(self, at, end):
                self.at, self.end = at, end

            def __call__(self, name, shape, dt):
                size = 2 if dt == F16 else 4
                for n in shape[1:]:
                    size *= n
                t = nc.alloc_sbuf_tensor_at(name, shape, dt, offset=self.at)
                self.at += (size + 31) // 32 * 32
                assert self.at <= self.end, (name, self.at, self.end)
                return t

        keep = Arena((nc.sbuf_base + 31) // 32 * 32, nc.sbuf_usable_end)
        ct_at = keep.at
        ct = keep("ct", [P, NT, N], F16)
        xs = keep("xs", [P, NT, 2 * F], F16)
        identf = keep("identf", [128, 128], F32)
        ident16 = keep("ident16", [P, P], F16)
        ones_col = keep("ones_col", [P, 1], F32)
        scales = keep("scales", [128, 2 * NSC], F32)
        unscale = keep("unscale", [128, 4], F32)
        rdeg_src = keep("rdeg_src", [P, NT], F32)
        rdeg_dst = keep("rdeg_dst", [P, NT], F32)
        deg_part = keep("deg_part", [P, NT, 4], F32)
        epsb = keep("epsb", [P, 1], F32)
        epsy = keep("epsy", [P, 1], F32)
        xs32 = xs[:, :, :].bitcast(F32)
        shared_at = keep.at

        bld = Arena(shared_at, nc.sbuf_usable_end)
        slab = [bld(f"slab{i}", [P, SLAB], F16) for i in range(2)]
        slab3 = [t[:, 0:N].rearrange("p (b d) -> p b d", d=P) for t in slab]
        src_hot2 = [bld(f"src_hot{i}", [128, 128, S], F16) for i in range(2)]
        key_hot2 = [bld(f"key_hot{i}", [128, S, KEY], F16) for i in range(2)]
        src_hot = [src_hot2[0][0:P, k * 128 // S:(k + 1) * 128 // S, :].rearrange("p a s -> p (a s)")
                   for k in range(G)]
        key_hot = [key_hot2[0][0:P, k, :] for k in range(G)]
        job_key = bld("job_key", [128, S, NW], F32)
        job_src = bld("job_src", [128, NW, S], F16)
        iota_src = bld("iota_src", [128, 128, S], F16)
        iota16 = bld("iota16", [128, KEY], F16)
        key_t = bld("key_t", [P, CH + G], F32)
        srcp_t = bld("srcp_t", [P, CH + G], F32)
        woff = bld("woff", [P, NW], F32)
        table = bld("table", [1, 2, 128], I32)
        matched = bld("matched", [1, 1], I32)
        w0_parts = bld("w0_parts", [128, 2, 2, F], F16)
        x_t16 = bld("x_t16", [128, 4, 128], F16)
        own = bld("own", [128, 2, F], F32)
        xscaled = bld("xscaled", [P, F], F32)
        xparts = bld("xparts", [P, 2 * F], F16)

        pre = Arena(ct_at, ct_at + NT * N * 2)
        edges_i = pre("edges_i", [EG, 2, EQ, P], I32)
        edges_f = pre("edges_f", [EG, 2, EQ, P], F32)
        hi_f = pre("hi_f", [EG, 2, EQ, P], F32)
        srcp = pre("srcp", [EG, EQ, P], F32)
        key = pre("key", [EG, EQ, P], F32)
        wlim = pre("wlim", [EG, 2, EQ], F32)
        onesq = pre("onesq", [P, P], F32)
        onesf = pre("onesf", [1, 128], F32)
        ones_h = pre("ones_h", [EG, EG], F16)
        before = pre("before", [EG, EQ, NW], F16)
        firsts = pre("firsts", [EG, NW], F32)
        win_row = pre("win_row", [EG, NW], F32)
        slot_no = pre("slot_no", [EG, J, NW], F32)
        chunk_no = pre("chunk_no", [EG, EQ], F32)
        want = pre("want", [EG, J, NW], F32)
        pick = pre("pick", [EG, EQ, J, NW], F32)
        packed = pre("packed", [EG, EQ, P], F32)
        row = [pre(f"row{i}", [P, J * P], F32) for i in range(2)]
        row_a = pre("row_a", [P, J * P], F32)
        row_key = pre("row_key", [P, S * 128], F32)
        row_col = pre("row_col", [P, S * 128], F32)
        row_src = pre("row_src", [P, S * 128], F32)
        wstart = pre("wstart", [P, 1], F32)
        wfirst = pre("wfirst", [P, 1], F32)
        bits = pre("bits", [P, 16], F32)
        wdiag = pre("wdiag", [EG, 2, EQ, EG], F32)
        inc_f = pre("inc_f", [P, CH], F32)
        rev_f = pre("rev_f", [P, CH], F32)
        wcol = pre("wcol", [P, 1], F32)
        xmax = pre("xmax", [P, 4], F32)
        cover = pre("cover", [P, CH], F32)
        cover2 = pre("cover2", [P, CH], F32)
        cover3 = pre("cover3", [P, CH], F32)
        cover4 = pre("cover4", [P, CH], F32)
        lim = pre("lim", [P, 8], F32)
        rows = pre("rows", [1, 4, 128], F32)
        w_nat = pre("w_nat", [128, 2, 2, 2 * F], F32)
        w_t = pre("w_t", [128, 2, 4, F], F32)
        wn_nat = pre("wn_nat", [128, 2, F], F32)
        ws_nat = pre("ws_nat", [128, 2, F], F32)
        bcol = pre("bcol", [128, 2], F32)
        junk = pre("junk", [128, 2 * F], F32)
        stat = pre("stat", [128, NST], F32)
        stat_r = pre("stat_r", [NST, 2], F32)
        sv = pre("sv", [1, 2, NST], F32)
        sw = pre("sw", [1, 8], F32)
        bound = pre("bound", [1, NSC], F32)
        bound2 = pre("bound2", [1, NSC], F32)
        svi = pre("svi", [1, 8], I32)
        sbits = pre("sbits", [1, 8], I32)
        srow = pre("srow", [1, 2 * NSC], F32)

        lay = Arena(shared_at, nc.sbuf_usable_end)
        w_own1 = lay("w_own1", [128, 2, 2, F], F16)
        w_agg = [lay(f"w_agg{l}", [128, 2, F], F32) for l in range(2)]
        wsn = lay("wsn", [128, 2, 2, 2 * F], F16)
        bias_sb = lay("bias_sb", [P, F], F32)
        nt_sb = lay("nt_sb", [128, 2, BT * P], F32)
        xy = [lay(f"xy{i}", [128, BT, F], F32) for i in range(2)]
        tr_sb = [lay(f"tr_sb{i}", [128, 4, 128], F16) for i in range(2)]
        t2 = [lay(f"t2_{i}", [P, F], F32) for i in range(2)]
        hb = [lay(f"hb{i}", [P, F], F32) for i in range(2)]
        part_all = lay("part", [128, 2, 2 * F], F16)
        part = [part_all[0:P, i, :] for i in range(2)]
        t1 = lay("t1", [P, F], F32)
        hn_all = lay("hn", [128, BT, F], F32)
        hn = [hn_all[0:P, i, :] for i in range(BT)]
        colsum = hn_all[0:P, 0:3, :].rearrange("p i f -> p (i f)")[:, 0:BT * P]
        w_scaled = hn_all[:, 3:5, :]
        w1_stage = part_all[:, :, :].bitcast(F32)
        wsn_stage = xy[1][:, 0:4, :].rearrange("p (c h) f -> p c h f", c=2)
        xy = [t[0:P] for t in xy]
        own_in = xy[0]
        m8 = [lay(f"m8_{i}", [P, 8], F32) for i in range(2)]
        st6 = [lay(f"st6_{i}", [P, 6], F32) for i in range(2)]
        mv = [lay(f"mv{i}", [P, 2], F32) for i in range(2)]
        sd = [lay(f"sd{i}", [P, 2], F32) for i in range(2)]
        work = hb
        sparse = t2

        c_dram = nc.dram_tensor("c_dram", (NT, P, N), F16).ap()
        wt_dram = nc.dram_tensor("wt_dram", (2, 128, 4 * F), F32).ap()
        own_dram = nc.dram_tensor("own_dram", (NT, P, F), F32).ap()
        parts_dram = [nc.dram_tensor(f"parts_dram{i}", (NT, P, 2 * F), F16).ap() for i in range(2)]
        z_dram = nc.dram_tensor("z_dram", (NT, P, F), F32).ap()
        x_t = x.rearrange("(t p) f -> t p f", p=P)
        out_t = out.rearrange("(t p) f -> t p f", p=P)

        bank = [ctx.enter_context(nc.psum_tensor(f"bank{i}", [128, 512], F32)) for i in range(8)]
        tr16 = [bank[4 + i][:, :].bitcast(F16).rearrange("p (k c) -> p k c", c=128) for i in range(2)]
        agg = [[bank[0], bank[1]], [bank[2], bank[3]]]
        tp = [bank[i][:, 0:4 * P].rearrange("p (c n) -> p c n", c=4) for i in (4, 7)]
        dense = [bank[5], bank[6]]

        const_ready = sem("const_ready")
        src_loaded, dst_loaded = sem("src_loaded"), sem("dst_loaded")
        x_loaded, w_loaded, wn_loaded, b_loaded = sem("x_loaded"), sem("w_loaded"), sem("wn_loaded"), sem("b_loaded")
        edge_keys, win_lims, lims_rows = sem("edge_keys"), sem("win_lims"), sem("lims_rows")
        keys_t, lims_b, rows_t = sem("keys_t"), sem("lims_b"), sem("rows_t")
        diag_ready = sem("diag_ready")
        wt_psum, wt_copied, wt_stored = sem("wt_psum"), sem("wt_copied"), sem("wt_stored")
        stat_ready, stat_psum, stat_red, stat_row = sem("stat_ready"), sem("stat_psum"), sem("stat_red"), sem("stat_row")
        scale_row, scale_psum, scale_ready = sem("scale_row"), sem("scale_psum"), sem("scale_ready")
        table_ready, act_sums = sem("table_ready"), sem("act_sums")
        before_ready, firsts_b, pick_ready, picked = sem("before_ready"), sem("firsts_b"), sem("pick_ready"), sem("picked")
        row_copied, cols_ready, cols_t, cols_copied = sem("row_copied"), sem("cols_ready"), sem("cols_t"), sem("cols_copied")
        count_ready, counted, matched_ready = sem("count_ready"), sem("counted"), sem("matched_ready")
        slow_step, win_rows, bound_step = sem("slow_step"), sem("win_rows"), sem("bound_step")
        unscale_ready = sem("unscale_ready")
        win_hot, win_done, colsum_ready, tr_zeroed = sem("win_hot"), sem("win_done"), sem("colsum_ready"), sem("tr_zeroed")
        hot_ready, jobs_done = sem("hot_ready"), sem("jobs_done")
        win_free, tr_done, tr_free = sem("win_free"), sem("tr_done"), sem("tr_free")
        slab_stored = [sem("slab_stored0"), sem("slab_stored1")]
        x_split, x_parts, stats3 = sem("x_split"), sem("x_parts"), sem("stats3")
        deg_done = sem("deg_done")
        agg_done, agg_copied = sem("agg_done"), sem("agg_copied")
        tp_done, tp_copied = sem("tp_done"), sem("tp_copied")
        mm_done, bank_read, c_read = sem("mm_done"), sem("bank_read"), sem("c_read")
        stage_loaded, w_split, deg_read = sem("stage_loaded"), [sem(f"w_split{i}") for i in range(3)], sem("deg_read")
        own_tp, own_tcopied, own_done, own_copied = sem("own_tp"), sem("own_tcopied"), sem("own_done"), sem("own_copied")
        own_stored, own_loaded, deg_summed = [sem("own_stored0"), sem("own_stored1")], sem("own_loaded"), sem("deg_summed")
        agg_w_loaded, bias_loaded, ws_loaded = sem("agg_w_loaded"), [sem("bias_loaded0"), sem("bias_loaded1")], sem("ws_loaded")
        relu_ready, lo_ready = sem("relu_ready"), sem("lo_ready")
        part_stored = [sem("part_stored0"), sem("part_stored1")]
        xy_loaded = [sem("xy_loaded0"), sem("xy_loaded1")]
        var_ready, sd_ready, normed = sem("var_ready"), sem("sd_ready"), sem("normed")
        y_high, y_ready = sem("y_high"), sem("y_ready")
        sparse_ready, sphi_ready, sp_lo = sem("sparse_ready"), sem("sphi_ready"), sem("sp_lo")
        sp_stored, z_stored = [sem("sp_stored0"), sem("sp_stored1")], sem("z_stored")
        xs_loaded = [[sem(f"xs_loaded{l}_{c}") for c in range(NB)] for l in (2, 3)]
        c_loaded = [sem(f"c_loaded{i}") for i in range(3)]
        n3_done, n3_read = sem("n3_done"), sem("n3_read")
        z_loaded, o_stored = [sem(f"z_loaded{i}") for i in range(BT)], [sem(f"o_stored{i}") for i in range(BT)]
        o_ready, var3, sd3 = sem("o_ready"), sem("var3"), sem("sd3")
        dve_step, act_step, pool_step = sem("dve_step"), sem("act_step"), sem("pool_step")

        STEPS = [(kind, i) for kind in "BC" for i in range(BT)]
        step_bank = [bank[k] for k in (5, 6, 0, 1, 2, 3, 5, 6, 5, 6)]

        def q0(n):
            return BT * NB + 2 * BT * n

        def c0(i):
            return i // 2

        def uses(i):
            return 3 if i % 2 == 0 else 2

        def free_at(Q, i):
            return Q if i == 0 else Q - 1

        block = ctx.enter_context(nc.Block())

        @block.sync
        def _(sp):
            sp.dma_start(edges_i[:, 1], dst.rearrange("(g q p) -> q g p", g=EQ, p=P)).then_inc(dst_loaded, 16)
            sp.dma_start(edges_i[:, 0], src.rearrange("(g q p) -> q g p", g=EQ, p=P)).then_inc(src_loaded, 16)
            sp.dma_start(xs32[:, :, :], x.rearrange("(t p) f -> p t f", p=P)).then_inc(x_loaded, 16)
            sp.dma_start(w_nat[:, 0], w0.rearrange("(h p) k -> p h k", p=128)).then_inc(w_loaded, 16)
            sp.dma_start(w_nat[:, 1], w1.rearrange("(h p) k -> p h k", p=128)).then_inc(w_loaded, 16)
            sp.dma_start(wn_nat[:, :, :], wneigh.rearrange("(h p) k -> p h k", p=128)).then_inc(wn_loaded, 16)
            sp.dma_start(ws_nat[:, :, :], wself.rearrange("(h p) k -> p h k", p=128)).then_inc(ws_loaded, 16)
            sp.dma_start(bcol[:, :], b0.rearrange("(h p) -> p h", p=128),
                         allow_slow_non_contiguous=True).then_inc(b_loaded, 16)
            sp.wait_ge(wt_copied, 4)
            sp.dma_start(wt_dram.rearrange("l p f -> p l f"), w_t[:, :, :, :].rearrange("p l c f -> p l (c f)")
                         ).then_inc(wt_stored, 16)

            def store_slab(t, par):
                sp.wait_ge(win_free, WT * t + WT + 2)
                sp.dma_start(c_dram[ds(t, 1), :, :].rearrange("o p n -> (o p) n"),
                             slab[par][:, 0:N]).then_inc(slab_stored[par], 16)

            def store_own(t, par):
                sp.wait_ge(own_copied, t + 2)
                sp.dma_start(own_dram[ds(t, 1), :, :].rearrange("o p n -> (o p) n"), own[0:P, par, :]
                             ).then_inc(own_stored[par], 16)

            store_slab(0, 0)
            with sp.Fori(0, NT // 2) as m:
                t = m * 2 + 1
                store_slab(t, 1)
                store_own(t - 1, 0)
                store_slab(t + 1, 0)
                store_own(t, 1)
            store_own(NT - 1, 0)

            sp.wait_ge(tr_done, 4 * NT)
            sp.wait_ge(x_split, NT)
            sp.wait_ge(slab_stored[0], 16 * 13)
            sp.wait_ge(slab_stored[1], 16 * 12)
            sp.wait_ge(own_stored[0], 16 * 14)
            sp.wait_ge(own_stored[1], 16 * 13)
            def load_own(n):
                sp.dma_start(own_in[:, :, :], own_dram[ds(n * BT, BT), :, :].rearrange("t p f -> p t f")
                             ).then_inc(own_loaded, 16)

            load_own(0)
            sp.dma_start(w1_stage.rearrange("p c f -> p (c f)"), wt_dram[1][:, 0:2 * F]).then_inc(stage_loaded, 16)
            sp.dma_start(wsn_stage[:, :, 0, :], wself.rearrange("(c p) f -> p c f", p=128)).then_inc(stage_loaded, 16)
            sp.dma_start(wsn_stage[:, :, 1, :], wneigh.rearrange("(c p) f -> p c f", p=128)).then_inc(stage_loaded, 16)
            for l in range(2):
                sp.dma_start(w_agg[l][:, :, :].rearrange("p c f -> p (c f)"), wt_dram[l][:, 2 * F:4 * F]
                             ).then_inc(agg_w_loaded, 16)
            sp.dma_start(bias_sb[:, :], b0.rearrange("(o f) -> o f", o=1).broadcast_to([P, F])).then_inc(bias_loaded[0], 16)

            def store_parts(n, i):
                sp.wait_ge(lo_ready, n * BT + i + 1)
                sp.dma_start(parts_dram[0][ds(n * BT + i, 1), :, :].rearrange("o p n -> (o p) n"), part[i % 2][:, :]
                             ).then_inc(part_stored[i % 2], 16)

            with sp.Fori(0, NB - 1) as n:
                for i in range(3):
                    store_parts(n, i)
                sp.wait_ge(bank_read, BT * n + BT)
                load_own(n + 1)
                for i in range(3, BT):
                    store_parts(n, i)

            def load_parts(l, c):
                sp.dma_start(xs[:, c * BT:(c + 1) * BT, :],
                             parts_dram[l][c * BT:(c + 1) * BT, :, :].rearrange("t p f -> p t f")
                             ).then_inc(xs_loaded[l][c], 16)

            def load_x(n):
                sp.dma_start(xy[n % 2][:, :, :], x_t[n * BT:(n + 1) * BT, :, :].rearrange("t p f -> p t f")
                             ).then_inc(xy_loaded[n % 2], 16)

            sp.wait_ge(agg_done, NB)
            sp.wait_ge(part_stored[0], 16 * 3 * (NB - 1))
            sp.wait_ge(part_stored[1], 16 * 2 * (NB - 1))
            for c in range(NB - 1):
                load_parts(0, c)
            sp.wait_ge(w_split[2], 1)
            load_x(1)
            sp.wait_ge(bank_read, BT * NB)
            load_x(0)
            sp.dma_start(bias_sb[:, :], b1.rearrange("(o f) -> o f", o=1).broadcast_to([P, F])).then_inc(bias_loaded[1], 16)

            def load_z(g, i):
                sp.dma_start(xy[1][:, i, :], z_dram[ds(g * BT + i, 1), :, :].rearrange("o p n -> (o p) n")
                             ).then_inc(z_loaded[i], 16)

            def load_c(c):
                sp.dma_start(ct[:, c * BT:(c + 1) * BT, :], c_dram[c * BT:(c + 1) * BT, :, :].rearrange("t p n -> p t n")
                             ).then_inc(c_loaded[(c + 1) // 2], 16)

            for n in range(NB):
                last = n == NB - 1
                if last:
                    sp.wait_ge(agg_done, 2 * NB)
                    sp.wait_ge(sp_stored[0], 16 * 3 * (NB - 1))
                    sp.wait_ge(sp_stored[1], 16 * 2 * (NB - 1))
                    for c in range(NB - 1):
                        load_parts(1, c)
                    load_c(0)
                    sp.wait_ge(z_stored, 16 * BT * (NB - 1))
                    for i in range(BT):
                        load_z(0, i)
                    load_c(1)
                for i in range(BT):
                    sp.wait_ge(c_read, n * BT + i + 1)
                    sp.dma_start(z_dram[n * BT + i], xy[n % 2][:, i, :]).then_inc(z_stored, 16)
                if n + 2 < NB:
                    sp.wait_ge(z_stored, 16 * BT * (n + 1))
                    load_x(n + 2)
                if not last:
                    for i in range(BT):
                        sp.wait_ge(sp_lo, n * BT + i + 1)
                        sp.dma_start(parts_dram[1][n * BT + i], part[i % 2][:, :]).then_inc(sp_stored[i % 2], 16)
            for c in range(2, NB):
                load_c(c)

            sp.wait_ge(z_stored, 16 * NT)

            def store_out(g, i):
                sp.wait_ge(o_ready, g * BT + i + 1)
                sp.dma_start(out_t[ds(g * BT + i, 1), :, :].rearrange("o p n -> (o p) n"), xy[0][:, i, :]
                             ).then_inc(o_stored[i], 16)

            with sp.Fori(0, NB - 1) as g:
                for i in range(BT):
                    store_out(g, i)
                    load_z(g + 1, i)
            for i in range(BT):
                store_out(NB - 1, i)
            for i in range(BT):
                sp.wait_ge(o_stored[i], 16 * NB)
            sp.wait_ge(wt_stored, 16)

        @block.gpsimd
        def _(pool):
            nc.gpsimd.iota(win_row[:, :], [[1, NW]], base=0, channel_multiplier=0,
                           allow_small_or_imprecise_dtypes=True).then_inc(win_rows, 1)
            nc.gpsimd.memset(ones_h[:, :], 1.0).then_inc(win_rows, 1)
            nc.gpsimd.iota(iota16[:, :], [[1, KEY]], base=0, channel_multiplier=0,
                           allow_small_or_imprecise_dtypes=True).then_inc(const_ready, 1)
            nc.gpsimd.iota(woff[:, :], [[KEY, NW]], base=0, channel_multiplier=0,
                           allow_small_or_imprecise_dtypes=True).then_inc(const_ready, 1)
            nc.gpsimd.iota(inc_f[:, :], [[1, CH]], base=1, channel_multiplier=0,
                           allow_small_or_imprecise_dtypes=True).then_inc(const_ready, 1)
            nc.gpsimd.iota(rev_f[:, :], [[-1, CH]], base=CH, channel_multiplier=0,
                           allow_small_or_imprecise_dtypes=True).then_inc(const_ready, 1)
            nc.gpsimd.iota(wcol[:, :], [[0, 1]], base=0, channel_multiplier=1,
                           allow_small_or_imprecise_dtypes=True).then_inc(const_ready, 1)
            nc.gpsimd.memset(identf[:, :], 0.0).then_inc(pool_step, 1)
            nc.gpsimd.memset(ident16[:, :], 0.0).then_inc(pool_step, 1)
            nc.gpsimd.memset(ones_col[:, :], 1.0).then_inc(const_ready, 1)
            nc.gpsimd.memset(epsy[:, :], EPS / YS ** 2).then_inc(const_ready, 1)
            for i in range(2):
                nc.gpsimd.memset(slab[i][:, N:SLAB], 0.0).then_inc(const_ready, 1)
            nc.gpsimd.iota(chunk_no[:, :], [[EG, EQ]], base=0, channel_multiplier=1,
                           allow_small_or_imprecise_dtypes=True).then_inc(const_ready, 1)
            nc.gpsimd.iota(iota_src[:, :, :], [[1, 128], [0, S]], base=0, channel_multiplier=0,
                           allow_small_or_imprecise_dtypes=True).then_inc(const_ready, 1)
            nc.gpsimd.iota(slot_no[:, :, :], [[1, J], [0, NW]], base=0, channel_multiplier=0,
                           allow_small_or_imprecise_dtypes=True).then_inc(const_ready, 1)
            nc.gpsimd.iota(wstart[:, :], [[0, 1]], base=PACK, channel_multiplier=KEY * PACK,
                           allow_small_or_imprecise_dtypes=True).then_inc(const_ready, 1)
            nc.gpsimd.iota(wfirst[:, :], [[0, 1]], base=-1, channel_multiplier=-KEY,
                           allow_small_or_imprecise_dtypes=True).then_inc(const_ready, 1)
            nc.gpsimd.memset(onesf[:, :], 1.0).then_inc(const_ready, 1)
            nc.gpsimd.memset(onesq[:, :], 1.0).then_inc(const_ready, 1)
            nc.gpsimd.memset(epsb[:, :], EPS).then_inc(const_ready, 1)
            nc.gpsimd.memset(key_t[:, CH:CH + G], -1.0).then_inc(const_ready, 1)
            nc.gpsimd.memset(srcp_t[:, CH:CH + G], 0.0).then_inc(const_ready, 1)
            nc.gpsimd.memset(stat[:, :], 0.0).then_inc(const_ready, 1)
            pool.wait_ge(pool_step, 2)
            for m, n in ((identf, 128), (ident16, P)):
                nc.gpsimd.affine_select(out=m[:, :], in_=m[:, :], compare_op=ALU.not_equal, fill=1.0, base=0,
                                        pattern=[[-1, n]], channel_multiplier=1).then_inc(const_ready, 1)
            pool.wait_ge(scale_ready, 1)
            pool.wait_ge(wt_copied, 4)
            by = scales[:, 3:4].rearrange("p (a o) -> p a o", o=1).broadcast_to([128, 2, F])
            nc.gpsimd.tensor_tensor(own[:, :, :], w_t[:, 0, 0:2, :], by, ALU.mult).then_inc(pool_step, 1)
            nc.gpsimd.tensor_tensor(w0_parts[:, :, 0, :], w_t[:, 0, 0:2, :], by, ALU.mult).then_inc(pool_step, 1)
            pool.wait_ge(pool_step, 4)
            nc.gpsimd.tensor_tensor(w0_parts[:, :, 1, :], own[:, :, :], w0_parts[:, :, 0, :], ALU.subtract
                                    ).then_inc(w_split[0], 1)
            with pool.Fori(0, NT) as t:
                step = 4 + 3 * t
                nc.gpsimd.tensor_tensor(xscaled[:, :], xs32[:, ds(t, 1), :].rearrange("p o f -> p (o f)"),
                                        scales[0:P, 0:1].broadcast_to([P, F]), ALU.mult).then_inc(pool_step, 1)
                nc.gpsimd.tensor_tensor(xparts[:, 0:F], xs32[:, ds(t, 1), :].rearrange("p o f -> p (o f)"),
                                        scales[0:P, 0:1].broadcast_to([P, F]), ALU.mult).then_inc(pool_step, 1)
                pool.wait_ge(pool_step, step + 2)
                nc.gpsimd.tensor_tensor(xparts[:, F:2 * F], xscaled[:, :], xparts[:, 0:F], ALU.subtract
                                        ).then_inc(pool_step, 1)
                pool.wait_ge(pool_step, step + 3)
                pool.sem_inc(x_parts, 1)
                nc.gpsimd.tensor_copy(xs[:, ds(t, 1), :].rearrange("p o f -> p (o f)"), xparts[:, :]
                                      ).then_inc(x_split, 1)
                pool.wait_ge(x_split, t + 1)
                pool.sem_inc(x_parts, 1)

            pool.wait_ge(stage_loaded, 48)
            step = 4 + 3 * NT
            for c in range(2):
                w_eye = wsn_stage[:, c, 0, c * 128:(c + 1) * 128]
                nc.gpsimd.tensor_tensor(w_eye, w_eye, identf[:, :], ALU.add).then_inc(pool_step, 1)
            step += 2
            for k, (w, out, p) in enumerate(((w1_stage, w_own1, 1), (wsn_stage[:, :, 0], wsn[:, :, :, 0:F], 2), (wsn_stage[:, :, 1], wsn[:, :, :, F:], 2))):
                by = scales[:, 4 + k:5 + k].rearrange("p (a o) -> p a o", o=1).broadcast_to([128, 2, F])
                pool.wait_ge(pool_step, step)
                nc.gpsimd.tensor_tensor(w_scaled, w, by, ALU.mult).then_inc(pool_step, 1)
                nc.gpsimd.tensor_tensor(out[:, :, 0, :], w, by, ALU.mult).then_inc(pool_step, 1)
                pool.wait_ge(pool_step, step + 2)
                nc.gpsimd.tensor_tensor(out[:, :, 1, :], w_scaled, out[:, :, 0, :], ALU.subtract).then_inc(pool_step, 1)
                step += 3
                if k != 1:
                    pool.wait_ge(pool_step, step)
                    pool.sem_inc(w_split[p], 1)
            for t in tr_sb:
                nc.gpsimd.memset(t[:, :, P:128], 0.0).then_inc(tr_zeroed, 1)

        NCONST = 22

        @block.vector
        def _(dve):
            done = [0]

            def step(ins):
                done[0] += 1
                ins.then_inc(dve_step, 1)
                dve.wait_ge(dve_step, done[0])

            v = nc.vector
            def whole_part(j, size):
                step(v.tensor_copy(edges_f[:, j], edges_i[:, j]))
                step(v.tensor_scalar(hi_f[:, j], edges_f[:, j], 1.0 / size, 0.5 / size - 0.5, ALU.mult, ALU.add))
                step(v.tensor_scalar(hi_f[:, j], hi_f[:, j], ROUND, -ROUND, ALU.add, ALU.add))

            dve.wait_ge(dst_loaded, 16)
            whole_part(1, W)
            step(v.tensor_reduce(wlim[:, 1, :], hi_f[:, 1], X, ALU.max))
            dve.wait_ge(win_rows, 2)
            for g in range(EQ):
                last = v.tensor_scalar(before[:, g, :], win_row[:, :], wlim[:, 1, g:g + 1], None, ALU.is_gt)
            last.then_inc(before_ready, 1)
            dve.wait_ge(src_loaded, 16)
            whole_part(0, P)
            step(v.scalar_tensor_tensor(key[:, :, :], hi_f[:, 1], float(KEY - W), edges_f[:, 1], ALU.mult, ALU.add))
            v.scalar_tensor_tensor(srcp[:, :, :], hi_f[:, 0], -float(P), edges_f[:, 0], ALU.mult, ALU.add
                                   ).then_inc(edge_keys, 1)
            v.scalar_tensor_tensor(key[:, :, :], hi_f[:, 0], float(W), key[:, :, :], ALU.mult, ALU.add
                                   ).then_inc(edge_keys, 1)
            dve.wait_ge(edge_keys, 2)
            step(v.tensor_scalar(packed[:, :, :], key[:, :, :], 1.0, float(PACK), ALU.add, ALU.mult))
            v.tensor_tensor(packed[:, :, :], packed[:, :, :], srcp[:, :, :], ALU.add).then_inc(pick_ready, 1)
            dve.wait_ge(const_ready, NCONST)
            dve.wait_ge(firsts_b, 1)
            step(v.tensor_copy(firsts[:, :], bank[0][0:EG, 0:NW]))
            step(v.tensor_tensor(want[:, :, :], slot_no[:, :, :],
                                 firsts[:, :].rearrange("p (o w) -> p o w", o=1).broadcast_to([EG, J, NW]), ALU.add))
            for g in range(EQ):
                v.tensor_scalar(pick[:, g, :, :], want[:, :, :], chunk_no[:, g:g + 1], None, ALU.is_equal
                                ).then_inc(pick_ready, 1)
            dve.wait_ge(x_loaded, 16)
            for c in range(2):
                v.tensor_reduce(xmax[:, c:c + 1], xs32[:, XC[c]:XC[c + 1], :].rearrange("p t f -> p (t f)"), X, ALU.max,
                                apply_absolute_value=True).then_inc(stat_ready, 1)
            dve.wait_ge(row_copied, 1)
            step(v.tensor_scalar(row_a[:, 0:P], row[0][:, 0:P], wstart[:, :], None, ALU.is_lt))
            step(v.tensor_reduce(bits[:, 0:1], row_a[:, 0:P], X, ALU.add))
            dve.wait_ge(row_copied, 2)
            for k, d in enumerate(SHIFTS):
                c = 4 * k
                v.tensor_scalar(bits[:, c + 1:c + 2], bits[:, c:c + 1], d - 0.5, None, ALU.is_gt).then_inc(dve_step, 1)
                v.tensor_scalar(bits[:, c + 2:c + 3], bits[:, c:c + 1], d - 0.5, None, ALU.is_lt).then_inc(dve_step, 1)
                done[0] += 2
                dve.wait_ge(dve_step, done[0])
                v.scalar_tensor_tensor(bits[:, c + 4:c + 5], bits[:, c + 1:c + 2], -float(d), bits[:, c:c + 1],
                                       ALU.mult, ALU.add).then_inc(dve_step, 1)
                n = S * 128 + sum(SHIFTS[k + 1:])
                a, b = row[k % 2], row[(k + 1) % 2]
                v.tensor_scalar(row_a[:, 0:n], a[:, 0:n], bits[:, c + 2:c + 3], None, ALU.mult).then_inc(dve_step, 1)
                done[0] += 2
                dve.wait_ge(dve_step, done[0])
                step(v.scalar_tensor_tensor(b[:, 0:n], a[:, d:d + n], bits[:, c + 1:c + 2], row_a[:, 0:n],
                                            ALU.mult, ALU.add))
            moved = row[len(SHIFTS) % 2][:, 0:S * 128]
            step(v.tensor_scalar(row_key[:, :], moved, 1.0 / PACK, -0.49, ALU.mult, ALU.add))
            step(v.tensor_scalar(row_key[:, :], row_key[:, :], ROUND, -ROUND, ALU.add, ALU.add))
            v.tensor_scalar(row_col[:, :], row_key[:, :], wfirst[:, :], None, ALU.add).then_inc(cols_ready, 1)
            v.scalar_tensor_tensor(row_src[:, :], row_key[:, :], -float(PACK), moved, ALU.mult, ALU.add
                                   ).then_inc(cols_ready, 1)
            dve.wait_ge(cols_ready, 2)
            step(v.tensor_scalar(row_a[:, 0:S * 128], row_col[:, :], KEY - 0.5, None, ALU.is_lt))
            step(v.scalar_tensor_tensor(row_key[:, :], row_col[:, :], -0.5, row_a[:, 0:S * 128], ALU.is_gt, ALU.mult))
            v.tensor_reduce(bits[:, 15:16], row_key[:, :], X, ALU.add).then_inc(count_ready, 1)
            dve.wait_ge(cols_t, 1)
            v.tensor_copy(job_key[:, :, :].rearrange("p s w -> p (s w)"), bank[3][:, 0:S * NW]).then_inc(cols_copied, 1)
            dve.wait_ge(counted, 1)
            v.tensor_copy(matched[:, :], bank[2][0:1, 256:257]).then_inc(matched_ready, 1)

            def general_table():
                count = [0]

                def step(ins):
                    count[0] += 1
                    ins.then_inc(slow_step, 1)
                    dve.wait_ge(slow_step, count[0])

                step(v.tensor_reduce(wlim[:, 0, :], hi_f[:, 1], X, ALU.min))
                for j in range(2):
                    for g in range(EQ):
                        last = v.tensor_scalar(wdiag[:, j, g, :], identf[0:EG, 0:EG], wlim[:, j, g:g + 1], None, ALU.mult)
                last.then_inc(diag_ready, 1)
                dve.wait_ge(keys_t, 1)
                step(v.tensor_copy(srcp_t[:, 0:CH], bank[0][0:P, 0:CH]))
                step(v.tensor_copy(key_t[:, 0:CH], bank[1][0:P, 0:CH]))
                dve.wait_ge(lims_b, 1)
                step(v.tensor_scalar(cover[:, :], bank[2][0:P, 0:CH], wcol[:, :], None, ALU.is_le))
                step(v.scalar_tensor_tensor(cover2[:, :], bank[3][0:P, 0:CH], wcol[:, :], cover[:, :], ALU.is_ge, ALU.mult))
                step(v.tensor_tensor(cover3[:, :], cover2[:, :], rev_f[:, :], ALU.mult))
                step(v.tensor_tensor(cover4[:, :], cover2[:, :], inc_f[:, :], ALU.mult))
                step(v.tensor_reduce(lim[:, 0:1], cover3[:, :], X, ALU.max))
                step(v.tensor_reduce(lim[:, 1:2], cover4[:, :], X, ALU.max))
                step(v.tensor_scalar(lim[:, 2:3], lim[:, 0:1], -1.0, float(CH), ALU.mult, ALU.add))
                step(v.tensor_tensor(lim[:, 3:4], lim[:, 1:2], lim[:, 2:3], ALU.subtract))
                step(v.tensor_scalar(lim[:, 4:5], lim[:, 3:4], 1.0 / G, (G - 1.0) / G + 0.5 / G - 0.5, ALU.mult, ALU.add))
                step(v.tensor_scalar(lim[:, 5:6], lim[:, 4:5], ROUND, -ROUND, ALU.add, ALU.add))
                v.tensor_scalar(lim[:, 6:7], lim[:, 5:6], 1.0, None, ALU.max).then_inc(win_lims, 1)
                dve.wait_ge(rows_t, 1)
                step(v.memset(rows[:, :, :], 0.0))
                step(v.memset(rows[:, 3, :], 1.0))
                step(v.tensor_copy(rows[:, 0, 0:NW], bank[4][0:1, 0:NW]))
                step(v.tensor_copy(rows[:, 2, 0:NW], bank[4][0:1, 128:128 + NW]))
                step(v.tensor_tensor_scan(rows[:, 1, 1:NW + 1], rows[:, 3, 0:NW], rows[:, 2, 0:NW], 0.0, ALU.mult, ALU.add))
                v.tensor_copy(table[:, :, :], rows[:, 0:2, :]).then_inc(table_ready, 1)

            def bound_parts():
                v.tensor_reduce(xmax[:, 2:3], xs32[:, XC[2]:XC[3], :].rearrange("p t f -> p (t f)"), X, ALU.max,
                                apply_absolute_value=True).then_inc(stat_ready, 1)
                dve.wait_ge(stat_ready, 3)
                v.tensor_reduce(stat[0:P, 0:1], xmax[:, 0:3], X, ALU.max).then_inc(stat_ready, 1)
                dve.wait_ge(b_loaded, 16)
                v.tensor_reduce(stat[:, 3:5], bcol[:, :].rearrange("p (h o) -> p h o", o=1), X, ALU.max,
                                apply_absolute_value=True).then_inc(stat_ready, 1)
                dve.wait_ge(wn_loaded, 16)
                v.tensor_reduce(stat[:, 5:7], wn_nat[:, :, :], X, ALU.max, apply_absolute_value=True
                                ).then_inc(stat_ready, 1)
                dve.wait_ge(ws_loaded, 16)
                v.tensor_reduce(stat[:, 7:9], ws_nat[:, :, :], X, ALU.max, apply_absolute_value=True
                                ).then_inc(stat_ready, 1)
                dve.wait_ge(w_loaded, 32)
                v.tensor_reduce(stat[:, 9:10], w_nat[:, 1].rearrange("p h k -> p (h k)"), X, ALU.max,
                                apply_absolute_value=True).then_inc(stat_ready, 1)

            def bound_rows():
                dve.wait_ge(stat_psum, 1)
                v.tensor_reduce(stat_r[:, 0:1], bank[6][0:NST, 0:128], X, ALU.max).then_inc(stat_red, 1)
                v.tensor_reduce(stat_r[:, 1:2], bank[6][0:NST, 0:128], X, ALU.add).then_inc(stat_red, 1)

            def bounds():
                count = [0]

                def step(ins):
                    count[0] += 1
                    ins.then_inc(bound_step, 1)
                    dve.wait_ge(bound_step, count[0])

                dve.wait_ge(stat_row, 1)
                step(v.tensor_copy(sv[:, :, :], bank[6][0:1, 0:2 * NST].rearrange("p (a b) -> p a b", a=2)))
                for at, a, b in ((0, 0, 0), (3, 1, 2), (4, 9, 9), (5, 7, 8), (6, 5, 6)):
                    v.tensor_tensor(bound[:, at:at + 1], sv[:, 0, a:a + 1], sv[:, 0, b:b + 1], ALU.max).then_inc(bound_step, 1)
                    count[0] += 1
                step(v.tensor_tensor(sw[:, 1:2], sv[:, 0, 3:4], sv[:, 0, 4:5], ALU.max))
                step(v.tensor_tensor(sw[:, 2:3], bound[:, 0:1], bound[:, 3:4], ALU.mult))
                step(v.tensor_tensor(bound[:, 1:2], sw[:, 2:3], sw[:, 1:2], ALU.add))
                step(v.tensor_tensor(sw[:, 3:4], sv[:, 1, 5:6], sv[:, 1, 6:7], ALU.add))
                step(v.tensor_scalar(bound[:, 2:3], sw[:, 3:4], 1.01 * F ** 0.5, None, ALU.mult))
                step(v.tensor_scalar(bound[:, 5:6], bound[:, 5:6], 1.0, None, ALU.add))
                step(v.tensor_scalar(bound2[:, :], bound[:, :], 1e-20, None, ALU.max))
                step(v.tensor_scalar(svi[:, 0:NSC], bound2[:, :].bitcast(I32), 0x7F800000, None, ALU.bitwise_and))
                step(v.tensor_scalar(sbits[:, 0:NSC], svi[:, 0:NSC], -1.0, float(268 << 23), ALU.mult, ALU.add))
                step(v.tensor_copy(srow[:, 0:NSC], sbits[:, 0:NSC].bitcast(F32)))
                v.tensor_scalar(srow[:, NSC:2 * NSC], svi[:, 0:NSC].bitcast(F32), 2.0 ** -14, None, ALU.mult).then_inc(scale_row, 1)

            def scales_out():
                dve.wait_ge(scale_psum, 1)
                v.tensor_copy(scales[:, :], bank[6][:, 32:32 + 2 * NSC]).then_inc(scale_ready, 1)
                dve.wait_ge(scale_ready, 1)
                v.tensor_tensor(unscale[:, 0:2], scales[:, NSC:NSC + 2], scales[:, NSC + 3:NSC + 5], ALU.mult
                                ).then_inc(unscale_ready, 1)
                v.tensor_scalar(unscale[:, 2:4], scales[:, NSC + 5:NSC + 7], 1.0 / YS, None, ALU.mult
                                ).then_inc(unscale_ready, 1)

            def quick_hots(w, b):
                dve.wait_ge(win_done, w + 1)
                v.tensor_tensor(src_hot2[b][:, :, :], iota_src[:, :, :],
                                job_src[:, ds(w, 1), :].broadcast_to([128, 128, S]), ALU.is_equal)
                for s in range(S):
                    last = v.tensor_scalar(key_hot2[b][:, s, :], iota16[:, :],
                                           job_key[:, s, ds(w, 1)], None, ALU.is_equal)
                last.then_inc(win_hot, 1)

            def general_hots(w):
                first = dve.value_load(table[0:1, 0, ds(w, 1)], min_val=0, max_val=CH)
                g0 = dve.value_load(table[0:1, 1, ds(w, 1)], min_val=0, max_val=NW * CH)
                g1 = dve.value_load(table[0:1, 1, ds(w + 1, 1)], min_val=0, max_val=NW * CH)
                off = woff[:, ds(w, 1)]
                with dve.Fori(g0, g1) as j:
                    chunk = nc.s_assert_within((j - g0) * G + first, 0, CH,
                                               skip_runtime_bounds_check_because="groups cover whole chunks up to the padding")
                    for k in range(G):
                        dve.wait_ge(jobs_done, j * G + k + 1)
                        v.tensor_scalar(src_hot[k][:, 0:P], iota16[0:P, 0:P], srcp_t[:, ds(chunk + k, 1)], None,
                                        ALU.is_equal)
                        v.tensor_scalar(key_hot[k][:, :], iota16[0:P, :], off, key_t[:, ds(chunk + k, 1)], ALU.add,
                                        ALU.is_equal).then_inc(hot_ready, 1)

            dve.wait_ge(matched_ready, 1)
            dve.wait_ge(cols_copied, 2)
            total = dve.value_load(matched[0:1, 0:1], min_val=0, max_val=E)
            with dve.If(total > E - 1):
                quick_hots(0, 0)
                bound_parts()
                quick_hots(1, 1)
                bound_rows()
                quick_hots(2, 0)
                bounds()
                quick_hots(3, 1)
                scales_out()
                quick_hots(4, 0)
                with dve.Fori(0, (NW - WT) // 4) as m:
                    for j in range(4):
                        quick_hots(m * 4 + (WT + j), (WT + j) % 2)
            with dve.If(total < E):
                general_table()
                bound_parts()
                bound_rows()
                bounds()
                scales_out()
                with dve.Fori(0, NW) as w:
                    general_hots(w)
            dve.wait_ge(tr_free, 4 * NT + 2)
            step(v.tensor_reduce(rdeg_dst[:, :], deg_part[:, :, :], X, ALU.add))
            step(v.tensor_scalar(rdeg_dst[:, :], rdeg_dst[:, :], 1.0, None, ALU.max))
            step(v.reciprocal(rdeg_dst[:, :], rdeg_dst[:, :]))
            step(v.tensor_scalar(rdeg_dst[:, :], rdeg_dst[:, :], scales[0:P, NSC + 2:NSC + 3], None, ALU.mult))
            dve.wait_ge(slab_stored[0], 16 * 13)
            dve.wait_ge(slab_stored[1], 16 * 12)
            dve.wait_ge(own_stored[0], 16 * 14)
            dve.wait_ge(own_stored[1], 16 * 13)
            dve.wait_ge(x_split, NT)

            def affine(T, i, ps, base):
                v.tensor_tensor(t1[:, :], own_in[:, i, :], bias_sb[:, :], ALU.add).then_inc(dve_step, 1)
                dve.wait_ge(mm_done, T + 1)
                dve.sem_inc(deg_done, 1)
                dve.wait_ge(dve_step, base + 1)
                v.scalar_tensor_tensor(t2[i % 2][:, :], ps[0:P, F:2 * F], rdeg_src[:, ds(T, 1)], t1[:, :],
                                       ALU.mult, ALU.add).then_inc(bank_read, 1)
                dve.wait_ge(bank_read, T + 1)

            def low_part1(T, i, out):
                dve.wait_ge(relu_ready, T + 1)
                v.scalar_tensor_tensor(out[:, F:2 * F], hb[i % 2][:, :], scales[0:P, 1:2],
                                       out[:, 0:F], ALU.mult, ALU.subtract).then_inc(lo_ready, 1)

            dve.wait_ge(bias_loaded[0], 16)
            base0 = done[0]

            def block1(n, out):
                v.tensor_reduce(colsum, ct[:, :, ds(n * (BT * P), BT * P)].rearrange("p t s -> p s t"), X, ALU.add
                                ).then_inc(colsum_ready, 1)
                dve.wait_ge(deg_summed, n + 1)
                v.tensor_scalar(rdeg_src[:, ds(n * BT, BT)], bank[7][0:P, 4 * P:4 * P + BT], 1.0, None, ALU.max
                                ).then_inc(deg_read, 1)
                dve.wait_ge(deg_read, 2 * n + 1)
                dve.sem_inc(deg_done, 1)
                v.reciprocal(rdeg_src[:, ds(n * BT, BT)], rdeg_src[:, ds(n * BT, BT)]).then_inc(deg_read, 1)
                dve.wait_ge(deg_read, 2 * n + 2)
                dve.sem_inc(deg_done, 1)
                dve.wait_ge(own_loaded, 16 * n + 16)
                for i in range(BT):
                    T = n * BT + i
                    affine(T, i, dense[i % 2], base0 + T)
                    if i:
                        low_part1(T - 1, i - 1, out(T - 1, i - 1))
                low_part1(n * BT + BT - 1, BT - 1, out(n * BT + BT - 1, BT - 1))

            with dve.Fori(0, NB - 1) as n:
                block1(n, lambda T, i: part[i % 2])
            block1(NB - 1, lambda T, i: xs[:, T, :])
            done[0] = base0 + NT

            dve.wait_ge(bias_loaded[1], 16)

            def counted_step(ins):
                done[0] += 1
                ins.then_inc(dve_step, 1)
                return done[0]

            def phase_b(n):
                dve.wait_ge(xy_loaded[n % 2], 16 * (n // 2 + 1))
                for i in range(BT + 1):
                    T, b = n * BT + i, i % 2
                    last, pb = i - 1, (i - 1) % 2
                    yp = xy[n % 2][:, max(last, 0), :].bitcast(F16)
                    if i < BT:
                        at = STEPS.index(("B", i))
                        ps = step_bank[at]
                        dve.wait_ge(mm_done, q0(n) + at + 1)
                        own = counted_step(v.scalar_tensor_tensor(t1[:, :], ps[0:P, 0:F], unscale[0:P, 1:2], bias_sb[:, :],
                                                                  ALU.mult, ALU.add))
                    if i:
                        dve.wait_ge(sd_ready, T)
                        root = counted_step(v.reciprocal(sd[pb][:, 1:2], sd[pb][:, 0:1]))
                    if i < BT:
                        dve.wait_ge(dve_step, own)
                        v.scalar_tensor_tensor(t2[b][:, :], ps[0:P, F:2 * F], rdeg_src[:, T:T + 1], t1[:, :],
                                               ALU.mult, ALU.add).then_inc(bank_read, 1)
                    if i:
                        dve.wait_ge(dve_step, root)
                        if last == BT - 1:
                            v.tensor_scalar(yp[:, 0:F], hb[pb][:, :], mv[pb][:, 0:1], sd[pb][:, 1:2],
                                            ALU.subtract, ALU.mult).then_inc(y_high, 1)
                        v.tensor_scalar(hb[pb][:, :], hb[pb][:, :], mv[pb][:, 0:1], sd[pb][:, 1:2],
                                        ALU.subtract, ALU.mult).then_inc(normed, 1)
                    if i < BT:
                        dve.wait_ge(bank_read, BT * NB + T + 1)
                        summed = counted_step(v.scalar_tensor_tensor(hb[b][:, :], t2[b][:, :], 0.0, xy[n % 2][:, i, :],
                                                                     ALU.max, ALU.add))
                        dve.wait_ge(dve_step, summed)
                        stats = counted_step(v.bn_stats(st6[b][:, :], hb[b][:, :]))
                    if i:
                        dve.wait_ge(normed, T)
                        dve.wait_ge(y_high, T)
                        v.tensor_tensor(yp[:, F:2 * F], hb[pb][:, :], yp[:, 0:F], ALU.subtract).then_inc(y_ready, 1)
                    if i < BT:
                        dve.wait_ge(dve_step, stats)
                        v.bn_aggr(mv[b][:, :], st6[b][:, :]).then_inc(var_ready, 1)

            def low_part2(n, i):
                T, b = n * BT + i, i % 2
                out = part[b] if n < NB - 1 else xs[:, T, :]
                dve.wait_ge(sphi_ready, T + 1)
                v.scalar_tensor_tensor(out[:, F:2 * F], sparse[b][:, :], scales[0:P, 2:3], out[:, 0:F],
                                       ALU.mult, ALU.subtract).then_inc(sp_lo, 1)

            def phase_k(n):
                waiting = []
                dve.wait_ge(y_ready, n * BT + BT)
                for pair in ((0, 1), (2, 3), (4,)):
                    dve.wait_ge(c_read, n * BT + pair[-1] + 1)
                    for r in range(MAXK // 8):
                        for i in pair:
                            cur = work[i % 2] if r else hn[i]
                            if r:
                                dve.wait_ge(dve_step, replaced[i])
                            v.max(m8[i % 2][:, :], cur[:, :]).then_inc(dve_step, 1)
                            done[0] += 1
                            found = done[0]
                            if len(pair) > 1:
                                tops[i] = found
                            else:
                                dve.wait_ge(dve_step, found)
                                step(v.match_replace(work[0][:, :], m8[0][:, :], cur[:, :], NEG))
                                replaced[i] = done[0]
                        if len(pair) > 1:
                            for i in pair:
                                cur = work[i % 2] if r else hn[i]
                                dve.wait_ge(dve_step, tops[i])
                                v.match_replace(work[i % 2][:, :], m8[i % 2][:, :], cur[:, :], NEG
                                                ).then_inc(dve_step, 1)
                                done[0] += 1
                                replaced[i] = done[0]
                    for i in waiting:
                        low_part2(n, i)
                    if waiting:
                        dve.wait_ge(sp_lo, n * BT + waiting[-1] + 1)
                    for i in pair:
                        dve.wait_ge(dve_step, replaced[i])
                        v.scalar_tensor_tensor(sparse[i % 2][:, :], work[i % 2][:, :], NEG, hn[i][:, :], ALU.is_equal,
                                               ALU.mult).then_inc(sparse_ready, 1)
                    waiting = list(pair)
                for i in waiting:
                    low_part2(n, i)

            tops, replaced = {}, {}
            for n in range(NB):
                phase_b(n)
                phase_k(n)

            base3 = done[0]
            dve.wait_ge(z_stored, 16 * NT)
            with dve.Fori(0, NB) as g:
                for i in range(BT):
                    T = g * BT + i
                    base = base3 + T * 4
                    dve.wait_ge(n3_done, T + 1)
                    dve.wait_ge(z_loaded[i], g * 16 + 16)
                    ps, zt = bank[i], xy[1][:, i, :]
                    v.scalar_tensor_tensor(zt, ps[0:P, 0:F], rdeg_dst[:, ds(T, 1)], zt, ALU.mult, ALU.add
                                           ).then_inc(dve_step, 1)
                    dve.wait_ge(dve_step, base + 1)
                    v.scalar_tensor_tensor(zt, ps[0:P, F:2 * F], rdeg_dst[:, ds(T, 1)], zt, ALU.mult, ALU.add
                                           ).then_inc(dve_step, 1)
                    dve.wait_ge(dve_step, base + 2)
                    v.bn_stats(st6[i % 2][:, :], zt).then_inc(dve_step, 1)
                    dve.wait_ge(dve_step, base + 3)
                    dve.sem_inc(stats3, 1)
                    v.bn_aggr(mv[i % 2][:, :], st6[i % 2][:, :]).then_inc(var3, 1)
                    dve.wait_ge(sd3, T + 1)
                    v.reciprocal(sd[i % 2][:, 1:2], sd[i % 2][:, 0:1]).then_inc(dve_step, 1)
                    dve.wait_ge(dve_step, base + 4)
                    dve.wait_ge(o_stored[i], g * 16)
                    v.tensor_scalar(xy[0][:, i, :], zt, mv[i % 2][:, 0:1], sd[i % 2][:, 1:2],
                                    ALU.subtract, ALU.mult).then_inc(o_ready, 1)
                    dve.wait_ge(o_ready, T + 1)
                    dve.sem_inc(n3_read, 1)

        @block.scalar
        def _(act):
            a = nc.scalar
            act.sem_inc(win_free, 2)
            act.sem_inc(tr_free, 2)
            act.wait_ge(picked, 1)
            a.activation(row[0][:, 0:S * P], bank[1][0:P, 0:S * P], ACT.Copy).then_inc(row_copied, 1)
            a.activation(row[0][:, S * P:J * P], bank[2][0:P, 0:P], ACT.Copy).then_inc(row_copied, 1)
            act.wait_ge(cols_t, 2)
            a.activation(job_src[:, :, :].rearrange("p w s -> p s w"), bank[4][:, 0:S * NW].rearrange("p (s w) -> p s w", s=S), ACT.Copy
                         ).then_inc(cols_copied, 1)
            act.wait_ge(w_loaded, 32)
            act.wait_ge(const_ready, NCONST)
            for h in range(2):
                a.activation(junk[:, :], w_nat[:, 0, h, :], ACT.Abs, accum_out=stat[:, 1 + h:2 + h]
                             ).then_inc(act_step, 1)
                act.wait_ge(act_step, h + 1)
            act.sem_inc(act_sums, 1)
            for l in range(2):
                for h in range(2):
                    act.wait_ge(wt_psum, 2 * l + h + 1)
                    b = bank[6 + h]
                    a.activation(w_t[:, l, :, h * 128:(h + 1) * 128],
                                 b[:, :].rearrange("p (c o) -> p c o", c=4), ACT.Copy).then_inc(wt_copied, 1)

            def win_copy(t, par, u, quick):
                w = t * WT + u
                if quick:
                    act.wait_ge(win_done, w + 3)
                else:
                    g1 = act.value_load(table[0:1, 1, ds(w + 1, 1)], min_val=0, max_val=NW * CH)
                    act.wait_ge(jobs_done, g1 * G + G)
                if u == 0:
                    act.wait_ge(slab_stored[par], t * 8 if par == 0 else (t - 1) * 8)
                q = (par + u) % 2
                out0 = slab3[par][:, 0:B0W, u * W:(u + 1) * W]
                out1 = slab3[par][:, B0W:NT, u * W:(u + 1) * W]
                a.activation(out0, bank[2 * q][0:P, 0:B0W * W].rearrange("p (b d) -> p b d", d=W), ACT.Copy)
                a.activation(out1, bank[2 * q + 1][0:P, 0:(NT - B0W) * W].rearrange("p (b d) -> p b d", d=W),
                             ACT.Copy).then_inc(win_free, 1)

            def tr_copy(t, g):
                act.wait_ge(tr_done, 4 * t + g + 1)
                a.activation(ct[:, ds(t, 1), TG0[g] * P:(TG0[g] + TG[g]) * P].rearrange("p o (b s) -> p (o b) s", s=P),
                             tr16[g % 2][0:P, 0:TG[g], 0:P], ACT.Copy,
                             accum_out=deg_part[:, ds(t, 1), g:g + 1].rearrange("p o g -> p (o g)")
                             ).then_inc(tr_free, 1)

            def own_t(t):
                act.wait_ge(own_tp, t + 1)
                a.activation(x_t16[:, :, 0:P], tp[1], ACT.Copy).then_inc(own_tcopied, 1)

            def own_copy(t, par, m):
                act.wait_ge(own_done, t + 1)
                act.wait_ge(own_stored[par], 16 * m + 16)
                a.activation(own[0:P, par, :], bank[6][0:P, 0:F], ACT.Copy, scale=unscale[0:P, 0:1]).then_inc(own_copied, 1)

            def copies(quick):
                for u in range(WT):
                    win_copy(0, 0, u, quick)
                act.wait_ge(wt_stored, 16)
                act.wait_ge(unscale_ready, 2)
                act.wait_ge(w_split[0], 1)
                act.sem_inc(own_copied, 1)
                for i in range(2):
                    act.sem_inc(own_stored[i], 16)
                with act.Fori(0, NT // 2) as m:
                    t = m * 2 + 1
                    for par, tt in ((1, t), (0, t + 1)):
                        for u in range(WT):
                            win_copy(tt, par, u, quick)
                            if u < 4:
                                tr_copy(tt - 1, u)
                            if u == 1:
                                own_t(tt - 1)
                            if u == 4:
                                own_copy(tt - 1, 1 - par, m)

            act.wait_ge(matched_ready, 1)
            total = act.value_load(matched[0:1, 0:1], min_val=0, max_val=E)
            with act.If(total > E - 1):
                copies(True)
            with act.If(total < E):
                act.wait_ge(table_ready, 1)
                copies(False)
            for g in range(4):
                tr_copy(NT - 1, g)
                if g == 1:
                    own_t(NT - 1)
            own_copy(NT - 1, 0, NT // 2)

            act.wait_ge(tr_done, 4 * NT)
            act.wait_ge(slab_stored[0], 16 * 13)
            act.wait_ge(slab_stored[1], 16 * 12)
            act.wait_ge(x_split, NT)

            def tr_out(Q, i):
                act.wait_ge(tp_done, Q - BT * NB + 1)
                act.wait_ge(mm_done, free_at(Q, i))
                a.activation(tr_sb[i % 2][:, :, 0:P], tp[i % 2], ACT.Copy).then_inc(tp_copied, 1)

            def agg_copy(k, l, Q0):
                act.wait_ge(agg_done, k + 1)
                for h, (lo, wd) in enumerate(((0, H0), (H0, H1))):
                    for f in range(2):
                        last = a.activation(nt_sb[:, f, lo:lo + wd], agg[f][h][:, 0:wd], ACT.Copy,
                                            scale=scales[:, NSC + l:NSC + l + 1])
                        if f or h:
                            last.then_inc(agg_copied, 1)
                        if h == 0 and l == 1:
                            tr_out(Q0 + f, f)

            def block1(n, out, parts_out):
                agg_copy(n, 0, None)
                for i in range(BT):
                    b, T = i % 2, n * BT + i
                    act.wait_ge(bank_read, T + 1)
                    if parts_out:
                        act.wait_ge(part_stored[b], (n * uses(i) + c0(i)) * 16)
                    a.activation(hb[b][:, :], t2[b][:, :], ACT.Relu)
                    a.activation(out(T, i)[:, 0:F], t2[b][:, :], ACT.Relu, scale=scales[0:P, 1:2]
                                 ).then_inc(relu_ready, 1)

            act.wait_ge(w_split[1], 1)
            with act.Fori(0, NB - 1) as n:
                block1(n, lambda T, i: part[i % 2], True)
            block1(NB - 1, lambda T, i: xs[:, T, :], False)

            def root(n, i):
                b, T = i % 2, n * BT + i
                act.wait_ge(var_ready, T + 1)
                a.activation(sd[b][:, 0:1], mv[b][:, 1:2], ACT.Sqrt, bias=epsy[:, :], scale=1.0 / YS ** 2
                             ).then_inc(sd_ready, 1)

            def y_high_part(n, i):
                act.wait_ge(normed, n * BT + i + 1)
                a.activation(xy[n % 2][:, i, :].bitcast(F16)[:, 0:F], hb[i % 2][:, :], ACT.Copy).then_inc(y_high, 1)

            def high(n, i):
                b, T = i % 2, n * BT + i
                act.wait_ge(sparse_ready, T + 1)
                if n < NB - 1:
                    act.wait_ge(sp_stored[b], 16 * (uses(i) * n + c0(i)))
                out = part[b] if n < NB - 1 else xs[:, T, :]
                a.activation(out[:, 0:F], sparse[b][:, :], ACT.Copy, scale=scales[0:P, 2:3]).then_inc(sphi_ready, 1)

            act.wait_ge(part_stored[0], 16 * 3 * (NB - 1))
            act.wait_ge(part_stored[1], 16 * 2 * (NB - 1))
            for n in range(NB):
                Q0 = q0(n)
                agg_copy(NB + n, 1, Q0)
                for s, (kind, i) in enumerate(STEPS):
                    if kind == "C":
                        act.wait_ge(mm_done, Q0 + s + 1)
                        ps = step_bank[s]
                        if n:
                            act.wait_ge(sparse_ready, (n - 1) * BT + i + 1)
                        a.activation(hn[i][:, :], ps[0:P, F:2 * F], ACT.Copy, scale=unscale[0:P, 3:4])
                        a.activation(xy[n % 2][:, i, :], ps[0:P, 0:F], ACT.Copy, scale=unscale[0:P, 2:3]).then_inc(c_read, 1)
                    if s + 2 < len(STEPS):
                        tr_out(Q0 + s + 2, s + 2)
                    if s and STEPS[s - 1][0] == "B":
                        root(n, STEPS[s - 1][1])
                        if STEPS[s - 1][1] < BT - 1:
                            y_high_part(n, STEPS[s - 1][1])
                for i in range(BT):
                    high(n, i)

            with act.Fori(0, NB) as g:
                for i in range(BT):
                    act.wait_ge(var3, g * BT + i + 1)
                    a.activation(sd[i % 2][:, 0:1], mv[i % 2][:, 1:2], ACT.Sqrt, bias=epsb[:, :]).then_inc(sd3, 1)

        @block.tensor
        def _(pe):
            mm = nc.tensor.matmul
            pe.wait_ge(before_ready, 1)
            for g in range(EQ):
                last = mm(bank[0][0:EG, 0:NW], ones_h[:, :], before[:, g, :], start=g == 0, stop=g == EQ - 1)
            last.then_inc(firsts_b, 1)
            pe.wait_ge(pick_ready, 1 + EQ)
            for j in range(J):
                for g in range(EQ):
                    out = bank[1 + j // S][0:P, (j % S) * P:(j % S + 1) * P]
                    last = mm(out, pick[:, g, j, :], packed[:, g, :], start=g == 0, stop=g == EQ - 1)
            last.then_inc(picked, 1)
            pe.wait_ge(w_loaded, 32)

            def weights_t(l, h):
                for c in range(4):
                    last = nc.tensor.transpose(bank[6 + h][:, c * 128:(c + 1) * 128],
                                               w_nat[:, l, h, c * 128:(c + 1) * 128], identf[:, :])
                last.then_inc(wt_psum, 1)

            weights_t(0, 0)
            weights_t(0, 1)
            for j, (m, b) in enumerate(((row_col, bank[3]), (row_src, bank[4]))):
                pe.wait_ge(cols_ready, j + 1)
                for k in range(S):
                    last = nc.tensor.transpose(b[:, k * NW:(k + 1) * NW], m[:, k * 128:(k + 1) * 128], identf[0:P, 0:P])
                last.then_inc(cols_t, 1)
            pe.wait_ge(count_ready, 1)
            mm(bank[2][0:1, 256:257], bits[:, 15:16], onesq[:, 0:1], start=True, stop=True).then_inc(counted, 1)

            def more_weights_t():
                for h in range(2):
                    pe.wait_ge(wt_copied, h + 1)
                    weights_t(1, h)

            def general_table():
                for j, (m, b) in enumerate(((srcp, bank[0]), (key, bank[1]))):
                    for g in range(EQ):
                        last = nc.tensor.transpose(b[0:P, g * EG:(g + 1) * EG], m[:, g, :], identf[0:EG, 0:EG])
                last.then_inc(keys_t, 1)
                pe.wait_ge(diag_ready, 1)
                for j in range(2):
                    for g in range(EQ):
                        last = mm(bank[2 + j][0:P, g * EG:(g + 1) * EG], onesq[0:EG, :], wdiag[:, j, g, :],
                                  start=True, stop=True)
                last.then_inc(lims_b, 1)
                pe.wait_ge(win_lims, 1)
                mm(bank[4][0:1, 0:P], lim[:, 2:3], identf[0:P, 0:P], start=True, stop=True)
                mm(bank[4][0:1, 128:128 + P], lim[:, 6:7], identf[0:P, 0:P], start=True, stop=True).then_inc(rows_t, 1)
                pe.wait_ge(table_ready, 1)

            def bounds_t():
                pe.wait_ge(stat_ready, 8)
                pe.wait_ge(act_sums, 1)
                pe.wait_ge(wt_copied, 4)
                nc.tensor.transpose(bank[6][0:NST, 0:128], stat[:, :], identf[:, :]).then_inc(stat_psum, 1)

            def bounds_row():
                pe.wait_ge(stat_red, 2)
                mm(bank[6][0:1, 0:NST], stat_r[:, 0:1], identf[0:NST, 0:NST], start=True, stop=True)
                mm(bank[6][0:1, NST:2 * NST], stat_r[:, 1:2], identf[0:NST, 0:NST], start=True, stop=True).then_inc(stat_row, 1)

            def scales_b():
                pe.wait_ge(scale_row, 1)
                mm(bank[6][:, 32:32 + 2 * NSC], onesf[:, :], srow[:, :], start=True, stop=True).then_inc(scale_psum, 1)

            pe.wait_ge(matched_ready, 1)
            pe.wait_ge(cols_copied, 2)
            pe.sem_inc(jobs_done, G)
            pe.sem_inc(win_done, 2)

            def job(q, k, start, stop):
                pe_kw = dict(start=start, stop=stop, skip_group_check=True)
                mm(bank[2 * q][0:P, 0:B0W * W], src_hot[k][:, 0:P], key_hot[k][:, 0:B0W * W], **pe_kw)
                mm(bank[2 * q + 1][0:P, 0:(NT - B0W) * W], src_hot[k][:, 0:P], key_hot[k][:, B0W * W:KEY], **pe_kw
                   ).then_inc(jobs_done, 1)

            def quick_window(t, par, u):
                w = t * WT + u
                q = b = (par + u) % 2
                pe.wait_ge(win_hot, w + 1)
                pe.wait_ge(win_free, w + 1)
                for s in range(S):
                    kw = dict(start=s == 0, stop=s == S - 1, skip_group_check=True)
                    mm(bank[2 * q][:, 0:B0W * W], src_hot2[b][:, :, s], key_hot2[b][:, s, 0:B0W * W], **kw)
                    last = mm(bank[2 * q + 1][:, 0:(NT - B0W) * W], src_hot2[b][:, :, s],
                              key_hot2[b][:, s, B0W * W:KEY], **kw)
                last.then_inc(win_done, 1)

            def window(t, par, u):
                w = t * WT + u
                q = (par + u) % 2
                g0 = pe.value_load(table[0:1, 1, ds(w, 1)], min_val=0, max_val=NW * CH)
                g1 = pe.value_load(table[0:1, 1, ds(w + 1, 1)], min_val=0, max_val=NW * CH)
                pe.wait_ge(win_free, w + 1)
                for k in range(G):
                    pe.wait_ge(hot_ready, g0 * G + k + 1)
                    job(q, k, k == 0, False)
                with pe.If(g0 + 1 < g1):
                    with pe.Fori(g0 + 1, g1) as j:
                        for k in range(G):
                            pe.wait_ge(hot_ready, j * G + k + 1)
                            job(q, k, False, False)

            def transposes(t, par, g):
                pe.wait_ge(win_free, WT * t + WT + 2)
                pe.wait_ge(tr_free, 4 * t + g + 1)
                for i in range(TG[g]):
                    last = nc.tensor.transpose(tr16[g % 2][:, i, 0:P],
                                               slab[par][:, (TG0[g] + i) * P:(TG0[g] + i) * P + 128], ident16[:, :])
                last.then_inc(tr_done, 1)

            def xs_part(T):
                if isinstance(T, int):
                    return lambda c: xs[:, T, c * 128:(c + 1) * 128]
                return lambda c: xs[:, ds(T, 1), c * 128:(c + 1) * 128].rearrange("p o f -> p (o f)")

            def in_parts(out, lhs, w, halves=(0, 1)):
                for h in halves:
                    for k, (pt, q) in enumerate(((0, 0), (0, 1), (1, 0))):
                        last = mm(out, lhs(2 * pt + h), w[:, h, q, :], start=h == 0 and k == 0, stop=h == 1 and k == 2,
                                  skip_group_check=True)
                return last

            def own_transposes(t):
                pe.wait_ge(x_split, t + 1)
                for c in range(4):
                    last = mm(tp[1][:, c, :], xs_part(t)(c), ident16[:, :], start=True, stop=True)
                last.then_inc(own_tp, 1)

            def own_product(t, h):
                if h == 0:
                    pe.wait_ge(own_tcopied, t + 1)
                    pe.wait_ge(own_copied, t + 1)
                last = in_parts(bank[6][0:P, 0:F], lambda k: x_t16[:, k, 0:P], w0_parts, (h,))
                if h == 1:
                    last.then_inc(own_done, 1)

            def windows(one_window, between=()):
                for u in range(WT):
                    one_window(0, 0, u)
                    for action in between[u:u + 1]:
                        action()
                pe.wait_ge(w_split[0], 1)
                with pe.Fori(0, NT // 2) as m:
                    t = m * 2 + 1
                    for par, tt in ((1, t), (0, t + 1)):
                        for u in range(WT):
                            one_window(tt, par, u)
                            if u < 4:
                                transposes(tt - 1, 1 - par, u)
                            if u == 1:
                                own_transposes(tt - 1)
                            if u >= 3:
                                own_product(tt - 1, u - 3)

            total = pe.value_load(matched[0:1, 0:1], min_val=0, max_val=E)
            with pe.If(total > E - 1):
                def weights_and_bounds():
                    more_weights_t()
                    bounds_t()

                windows(quick_window, (weights_and_bounds, bounds_row, scales_b))
            with pe.If(total < E):
                general_table()
                more_weights_t()
                bounds_t()
                bounds_row()
                scales_b()
                windows(window)
            for g in range(4):
                transposes(NT - 1, 0, g)
                if g == 1:
                    own_transposes(NT - 1)
            own_product(NT - 1, 0)
            own_product(NT - 1, 1)

            pe.wait_ge(tr_free, 4 * NT + 2)
            pe.wait_ge(x_split, NT)

            def aggregate(k, n, parts=None):
                pe.wait_ge(agg_copied, 3 * k)

                def one(t, start, stop):
                    for h, (lo, wd) in enumerate(((0, H0), (H0, H1))):
                        for f in range(2):
                            for p in range(2):
                                if isinstance(t, int):
                                    lhs = xs[:, t, p * F + f * 128:p * F + f * 128 + 128]
                                    rhs = ct[:, t, ds(n * BT * P + lo, wd)]
                                else:
                                    lhs = xs[:, ds(t, 1), p * F + f * 128:p * F + f * 128 + 128].rearrange("p o f -> p (o f)")
                                    rhs = ct[:, ds(t, 1), ds(n * BT * P + lo, wd)].rearrange("p o f -> p (o f)")
                                last = mm(agg[f][h][:, 0:wd], lhs, rhs, start=start and p == 0, stop=stop and p == 1,
                                          skip_group_check=True)
                    return last

                if parts is None:
                    one(0, True, False)
                    with pe.Fori(0, (NT - 1) // 4 - 1) as m:
                        for j in range(4):
                            one(m * 4 + (j + 1), False, False)
                    for t in range(NT - 4, NT - 1):
                        one(t, False, False)
                else:
                    for c in range(NB):
                        if c < NB - 1:
                            pe.wait_ge(parts[c], 16)
                        else:
                            pe.wait_ge(lo_ready, NT)
                        if c == 0:
                            one(0, True, False)
                        with pe.Fori(max(1, c * BT), min(NT - 1, (c + 1) * BT)) as t:
                            one(t, False, False)
                one(NT - 1, False, True).then_inc(agg_done, 1)

            def transpose_tile(Q, i, tile):
                if Q > BT * NB:
                    pe.wait_ge(tp_copied, free_at(Q - BT * NB, i))
                for c in range(4):
                    last = mm(tp[i % 2][:, c, :], tile(c), ident16[:, :], start=True, stop=True)
                last.then_inc(tp_done, 1)

            def agg_product(ps, i, k, l):
                pe.wait_ge(agg_copied, 3 * k + (1 if i < 2 else 3))
                for c in range(2):
                    last = mm(ps[0:P, F:2 * F], nt_sb[:, c, i * P:(i + 1) * P], w_agg[l][:, c, :],
                              start=c == 0, stop=c == 1, skip_group_check=True)
                last.then_inc(mm_done, 1)

            with pe.Fori(0, NB) as n:
                aggregate(n, n)
                pe.wait_ge(agg_w_loaded, 32)
                pe.wait_ge(colsum_ready, n + 1)
                for i in range(BT):
                    last = mm(bank[7][0:P, 4 * P + i:4 * P + i + 1], colsum[:, i * P:(i + 1) * P], ones_col[:, :],
                              start=True, stop=True)
                last.then_inc(deg_summed, 1)
                for i in range(BT):
                    pe.wait_ge(bank_read, free_at(n * BT + i, i))
                    agg_product(dense[i % 2], i, n, 0)

            for n in range(NB):
                if n:
                    pe.wait_ge(bank_read, BT * (NB + n))
                    pe.wait_ge(c_read, BT * (n - 1) + 1)
                aggregate(NB + n, n, None if n else xs_loaded[0])
                Q0 = q0(n)
                if n == 0:
                    pe.wait_ge(tr_zeroed, 2)
                    pe.wait_ge(deg_read, 2 * NB)
                    pe.wait_ge(w_split[1], 1)
                    pe.wait_ge(w_split[2], 1)

                def turn(s):
                    kind, i = STEPS[s]
                    if kind == "C":
                        pe.wait_ge(y_ready, n * BT + i + 1)
                        yp = xy[n % 2][:, i, :].bitcast(F16)
                        transpose_tile(Q0 + s, s, lambda c: yp[:, c * 128:(c + 1) * 128])
                    else:
                        transpose_tile(Q0 + s, s, xs_part(n * BT + i))

                turn(0)
                turn(1)
                for s, (kind, i) in enumerate(STEPS):
                    if s < 2 and n == 0:
                        pe.wait_ge(bank_read, BT * NB)
                    elif s < 2:
                        pe.wait_ge(c_read, n * BT)
                    elif s < 6:
                        pe.wait_ge(agg_copied, 3 * (NB + n + 1))
                    elif s < 8:
                        pe.wait_ge(bank_read, BT * (NB + n) + s - 5)
                    else:
                        pe.wait_ge(c_read, n * BT + s - 6)
                    pe.wait_ge(tp_copied, Q0 + s + 1 - BT * NB)
                    ps, lhs = step_bank[s], lambda k: tr_sb[s % 2][:, k, :]
                    if kind == "B":
                        in_parts(ps[:, 0:F], lhs, w_own1)
                        agg_product(ps, i, NB + n, 1)
                    else:
                        in_parts(ps[:, :], lhs, wsn).then_inc(mm_done, 1)
                    if s + 2 < len(STEPS):
                        turn(s + 2)

            def tile3(T, i, b0_, b1_):
                for b in range(b0_, b1_):
                    if b < NT - 1:
                        out, lhs = bank[i][:, :], ct[:, ds(T, 1), b * P:b * P + 128]
                    else:
                        out, lhs = bank[i][0:P, :], ct[:, ds(T, 1), b * P:(b + 1) * P]
                    last = mm(out, lhs.rearrange("p o d -> p (o d)"), xs[:, b, :], start=b == 0, stop=b == NT - 1,
                              skip_group_check=True)
                return last

            pe.wait_ge(bank_read, 2 * NT)
            pe.wait_ge(c_read, BT * (NB - 1) + 1)
            for c in range(NB - 1):
                pe.wait_ge(xs_loaded[1][c], 16)
            pe.wait_ge(c_loaded[0], 16)
            for i in range(BT):
                tile3(i, i, 0, NT - BT)
            pe.wait_ge(sp_lo, NT)
            for i in range(BT):
                tile3(i, i, NT - BT, NT).then_inc(n3_done, 1)
            for g0, g1, s in ((1, 3, c_loaded[1]), (3, NB, c_loaded[2])):
                pe.wait_ge(s, 32)
                with pe.Fori(g0, g1) as g:
                    for i in range(BT):
                        T = g * BT + i
                        pe.wait_ge(n3_read, T + 1 - BT)
                        tile3(T, i, 0, NT).then_inc(n3_done, 1)


_INS = ["x", "src", "dst", "L0_gnn_W0", "L0_gnn_b0", "L0_gnn_W1", "L0_gnn_b1", "L1_gnn_W_self", "L1_gnn_W_neigh"]


def kernel(**inputs):
    import numpy as _np
    import concourse.bacc as _bacc
    from concourse import mybir as _mybir
    from concourse.bass_utils import run_bass_kernel_spmd as _run

    nc = _bacc.Bacc("TRN2", target_bir_lowering=False, num_devices=1, dynamic_dma_scratch_size=1024)
    arrays, args = {}, []
    for name in _INS:
        a = _np.ascontiguousarray(inputs[name])
        arrays[f"in_{name}_dram"] = a
        args.append(nc.dram_tensor(f"in_{name}_dram", a.shape, _mybir.dt.from_np(a.dtype), kind="ExternalInput").ap())
    out = nc.dram_tensor("out_dram", (N, F), _mybir.dt.float32, kind="ExternalOutput").ap()
    gnn(nc, *args, out)
    r = _run(nc, [arrays], core_ids=[0])
    return r.results[0]["out_dram"]
```
